# Optimizing a Trainium2 kernel written in Bass

```python
import numpy as np
import jax
import jax.numpy as jnp

def _softmax(x, axis=-1):
    return jax.nn.softmax(x, axis=axis)

def _gelu(x):
    return jax.nn.gelu(x, approximate=True)

def _silu(x):
    return jax.nn.silu(x)

def _sigmoid(x):
    return jax.nn.sigmoid(x)

def _layernorm(x, axis=-1, eps=1e-05):
    m = jnp.mean(x, axis=axis, keepdims=True)
    v = jnp.var(x, axis=axis, keepdims=True)
    return (x - m) / jnp.sqrt(v + eps)

def _scatter_add(tgt, idx, src, axis=0):
    return tgt.at[idx].add(src)

def _segment_sum(src, seg, n):
    return jax.ops.segment_sum(src, seg, n)
kernel_name = 'mk_xattn_ffn_d2_seqx_r8_27bf2f'

def setup_inputs(seed: int=0):
    np.random.seed(seed)
    _w = jnp.asarray

    def _rec_inputs():
        import jax
        import jax.numpy as jnp
        _rk = jax.random.key(seed)
        x = -0.0002928 + 1 * jax.random.normal(jax.random.fold_in(_rk, 1), (4, 256, 128), jnp.float32)
        _lenS = 256 - jax.random.randint(jax.random.fold_in(_rk, 7), (4,), 0, max(1, 256 // 4) + 1, jnp.int32)
        _lenS2 = 256 - jax.random.randint(jax.random.fold_in(_rk, 8), (4,), 0, max(1, 256 // 4) + 1, jnp.int32)
        _ctx_1024P = jax.random.normal(jax.random.fold_in(_rk, 11), (4, 16, 128), jnp.float32)
        _ctx_1024c = jax.random.dirichlet(jax.random.fold_in(_rk, 511), 0.3 * jnp.ones((16,), jnp.float32), (4, 256))
        _ctx_1024t = jnp.einsum('bsk,bkd->bsd', _ctx_1024c, _ctx_1024P)
        _ctx_1024t = _ctx_1024t * jax.lax.rsqrt(jnp.mean(jnp.square(_ctx_1024t)) + 1e-12) * 0.953939
        ctx_1024 = -1.39393e-06 + 0.999914 * (_ctx_1024t + 0.3 * jax.random.normal(jax.random.fold_in(_rk, 611), (4, 256, 128), jnp.float32))
        return (x, ctx_1024)
    x, ctx_1024 = _rec_inputs()

    def _L0_xattn_setup():
        import jax, jax.numpy as jnp
        import numpy as np
        H = 16
        D_MODEL = 128
        D_K = D_MODEL // H

        def _mha(query, key, value, Wq, bq, Wk, bk, Wv, bv, Wo, bo):
            B, S, _ = query.shape
            q = query @ Wq.T + bq
            k = key @ Wk.T + bk
            v = value @ Wv.T + bv
            q = q.reshape(B, S, H, D_K).transpose(0, 2, 1, 3)
            k = k.reshape(B, S, H, D_K).transpose(0, 2, 1, 3)
            v = v.reshape(B, S, H, D_K).transpose(0, 2, 1, 3)
            scores = jnp.einsum('bhqd,bhkd->bhqk', q, k) / jnp.sqrt(jnp.float32(D_K))
            stable = scores - jnp.max(scores, axis=-1, keepdims=True)
            e = jnp.exp(stable)
            attn = e / jnp.sum(e, axis=-1, keepdims=True)
            ctx = jnp.einsum('bhqk,bhkd->bhqd', attn, v)
            ctx = ctx.transpose(0, 2, 1, 3).reshape(B, S, H * D_K)
            return ctx @ Wo.T + bo
        key = jax.random.key(seed)
        ks = jax.random.split(key, 11)
        B, S = (2, 256)
        scale = 1.0 / np.sqrt(D_MODEL)
        inp = {'query': jax.random.normal(ks[0], (B, S, D_MODEL), dtype=jnp.float32), 'key': jax.random.normal(ks[1], (B, S, D_MODEL), dtype=jnp.float32), 'value': jax.random.normal(ks[2], (B, S, D_MODEL), dtype=jnp.float32), 'Wq': jax.random.normal(ks[3], (D_MODEL, D_MODEL), dtype=jnp.float32) * scale, 'bq': jnp.zeros((D_MODEL,), dtype=jnp.float32), 'Wk': jax.random.normal(ks[4], (D_MODEL, D_MODEL), dtype=jnp.float32) * scale, 'bk': jnp.zeros((D_MODEL,), dtype=jnp.float32), 'Wv': jax.random.normal(ks[5], (D_MODEL, D_MODEL), dtype=jnp.float32) * scale, 'bv': jnp.zeros((D_MODEL,), dtype=jnp.float32), 'Wo': jax.random.normal(ks[6], (D_MODEL, D_MODEL), dtype=jnp.float32) * scale, 'bo': jnp.zeros((D_MODEL,), dtype=jnp.float32)}
        return inp
    _L0_xattn_all = _L0_xattn_setup()
    _L0_xattn_in = {k: v for k, v in _L0_xattn_all.items() if k in ('Wq', 'bq', 'Wk', 'bk', 'Wv', 'bv', 'Wo', 'bo')}
    del _L0_xattn_all

    def _L0_ffn_setup():
        import jax, jax.numpy as jnp
        import numpy as np
        B, S, H, F, E = (8, 256, 128, 512, 8)
        INIT_LAMBDA = 0.2
        key = jax.random.key(seed)
        ks = jax.random.split(key, 12)
        std = 0.02
        return {'hidden_states': jax.random.normal(ks[0], (B, S, H), jnp.float32), 'gate_w1': jax.random.normal(ks[1], (H, H), jnp.float32) * 0.01, 'gate_b1': jnp.zeros((H,), jnp.float32), 'gate_w2': jax.random.normal(ks[2], (E, H), jnp.float32) * 0.01, 'gate_b2': jnp.full((E,), INIT_LAMBDA, jnp.float32), 'W1': jax.random.normal(ks[3], (F, H), jnp.float32) * std, 'b1': jax.random.normal(ks[4], (F,), jnp.float32) * std, 'W2': jax.random.normal(ks[5], (H, F), jnp.float32) * std, 'b2': jax.random.normal(ks[6], (H,), jnp.float32) * std, 'TW1': jax.random.normal(ks[7], (E, F, H), jnp.float32) * std, 'Tb1': jax.random.normal(ks[8], (E, F), jnp.float32) * std, 'TW2': jax.random.normal(ks[9], (E, H, F), jnp.float32) * std, 'Tb2': jax.random.normal(ks[10], (E, H), jnp.float32) * std}
    _L0_ffn_all = _L0_ffn_setup()
    _L0_ffn_in = {k: v for k, v in _L0_ffn_all.items() if k in ('gate_w1', 'gate_b1', 'gate_w2', 'gate_b2', 'W1', 'b1', 'W2', 'b2', 'TW1', 'Tb1', 'TW2', 'Tb2')}
    del _L0_ffn_all

    def _L1_xattn_setup():
        import jax, jax.numpy as jnp
        import numpy as np
        H, DK, DV = (16, 64, 64)
        MEM = 128
        D_MODEL = 128
        OUT_DIM = 128
        key = jax.random.key(seed)
        ks = jax.random.split(key, 12)
        B, S = (2, 256)
        scale = 1.0 / np.sqrt(D_MODEL)
        inp = {'queries': jax.random.normal(ks[0], (B, S, D_MODEL), jnp.float32), 'keys': jax.random.normal(ks[1], (B, S, D_MODEL), jnp.float32), 'values': jax.random.normal(ks[2], (B, S, D_MODEL), jnp.float32), 'wq_w': jax.random.normal(ks[3], (D_MODEL, H * DK), jnp.float32) * scale, 'wq_b': jnp.zeros((H * DK,), jnp.float32), 'wk_w': jax.random.normal(ks[4], (D_MODEL, H * DK), jnp.float32) * scale, 'wk_b': jnp.zeros((H * DK,), jnp.float32), 'wv_w': jax.random.normal(ks[5], (D_MODEL, H * DV), jnp.float32) * scale, 'wv_b': jnp.zeros((H * DV,), jnp.float32), 'mk': jax.random.normal(ks[6], (1, MEM, H * DK), jnp.float32) * (0.1 / DK), 'mv': jax.random.normal(ks[7], (1, MEM, H * DV), jnp.float32) * (0.1 / MEM), 'wo_w': jax.random.normal(ks[8], (H * DV, OUT_DIM), jnp.float32) * (1.0 / np.sqrt(H * DV)), 'wo_b': jnp.zeros((OUT_DIM,), jnp.float32)}
        return inp
    _L1_xattn_all = _L1_xattn_setup()
    _L1_xattn_in = {k: v for k, v in _L1_xattn_all.items() if k in ('wq_w', 'wq_b', 'wk_w', 'wk_b', 'wv_w', 'wv_b', 'mk', 'mv', 'wo_w', 'wo_b')}
    del _L1_xattn_all

    def _L1_ffn_setup():
        import jax, jax.numpy as jnp
        import numpy as np
        from jax import lax
        H = 128
        E = 8
        E_MLP = E - 4
        TOP_K = 2
        I = 64
        KC = 4
        SHARED_SCALE = 1.0
        key = jax.random.key(seed)
        ks = jax.random.split(key, 8)
        B, S = (4, 512)
        s_h = 1.0 / np.sqrt(H)
        s_i = 1.0 / np.sqrt(I)
        return {'hidden_states': jax.random.normal(ks[0], (B, S, H), dtype=jnp.float32), 'Wr': jax.random.normal(ks[1], (H, E), dtype=jnp.float32) * s_h, 'router_bias': jnp.zeros((E,), dtype=jnp.float32), 'Wg': jax.random.normal(ks[2], (E_MLP, H, I), dtype=jnp.float32) * s_h, 'Wu': jax.random.normal(ks[3], (E_MLP, H, I), dtype=jnp.float32) * s_h, 'Wd': jax.random.normal(ks[4], (E_MLP, I, H), dtype=jnp.float32) * s_i, 'conv_w': jax.random.normal(ks[5], (KC, 1, H), dtype=jnp.float32) * (1.0 / np.sqrt(KC)), 'conv_b': jnp.zeros((H,), dtype=jnp.float32)}
    _L1_ffn_all = _L1_ffn_setup()
    _L1_ffn_in = {k: v for k, v in _L1_ffn_all.items() if k in ('Wr', 'router_bias', 'Wg', 'Wu', 'Wd', 'conv_w', 'conv_b')}
    del _L1_ffn_all
    return {'x': x, 'ctx_1024': ctx_1024, 'L0_xattn_Wq': _L0_xattn_in['Wq'], 'L0_xattn_bq': _L0_xattn_in['bq'], 'L0_xattn_Wk': _L0_xattn_in['Wk'], 'L0_xattn_bk': _L0_xattn_in['bk'], 'L0_xattn_Wv': _L0_xattn_in['Wv'], 'L0_xattn_bv': _L0_xattn_in['bv'], 'L0_xattn_Wo': _L0_xattn_in['Wo'], 'L0_xattn_bo': _L0_xattn_in['bo'], 'L0_ffn_gate_w1': _L0_ffn_in['gate_w1'], 'L0_ffn_gate_b1': _L0_ffn_in['gate_b1'], 'L0_ffn_gate_w2': _L0_ffn_in['gate_w2'], 'L0_ffn_gate_b2': _L0_ffn_in['gate_b2'], 'L0_ffn_W1': _L0_ffn_in['W1'], 'L0_ffn_b1': _L0_ffn_in['b1'], 'L0_ffn_W2': _L0_ffn_in['W2'], 'L0_ffn_b2': _L0_ffn_in['b2'], 'L0_ffn_TW1': _L0_ffn_in['TW1'], 'L0_ffn_Tb1': _L0_ffn_in['Tb1'], 'L0_ffn_TW2': _L0_ffn_in['TW2'], 'L0_ffn_Tb2': _L0_ffn_in['Tb2'], 'L1_xattn_wq_w': _L1_xattn_in['wq_w'], 'L1_xattn_wq_b': _L1_xattn_in['wq_b'], 'L1_xattn_wk_w': _L1_xattn_in['wk_w'], 'L1_xattn_wk_b': _L1_xattn_in['wk_b'], 'L1_xattn_wv_w': _L1_xattn_in['wv_w'], 'L1_xattn_wv_b': _L1_xattn_in['wv_b'], 'L1_xattn_mk': _L1_xattn_in['mk'], 'L1_xattn_mv': _L1_xattn_in['mv'], 'L1_xattn_wo_w': _L1_xattn_in['wo_w'], 'L1_xattn_wo_b': _L1_xattn_in['wo_b'], 'L1_ffn_Wr': _L1_ffn_in['Wr'], 'L1_ffn_router_bias': _L1_ffn_in['router_bias'], 'L1_ffn_Wg': _L1_ffn_in['Wg'], 'L1_ffn_Wu': _L1_ffn_in['Wu'], 'L1_ffn_Wd': _L1_ffn_in['Wd'], 'L1_ffn_conv_w': _L1_ffn_in['conv_w'], 'L1_ffn_conv_b': _L1_ffn_in['conv_b']}

def reference(x, ctx_1024, L0_xattn_Wq, L0_xattn_bq, L0_xattn_Wk, L0_xattn_bk, L0_xattn_Wv, L0_xattn_bv, L0_xattn_Wo, L0_xattn_bo, L0_ffn_gate_w1, L0_ffn_gate_b1, L0_ffn_gate_w2, L0_ffn_gate_b2, L0_ffn_W1, L0_ffn_b1, L0_ffn_W2, L0_ffn_b2, L0_ffn_TW1, L0_ffn_Tb1, L0_ffn_TW2, L0_ffn_Tb2, L1_xattn_wq_w, L1_xattn_wq_b, L1_xattn_wk_w, L1_xattn_wk_b, L1_xattn_wv_w, L1_xattn_wv_b, L1_xattn_mk, L1_xattn_mv, L1_xattn_wo_w, L1_xattn_wo_b, L1_ffn_Wr, L1_ffn_router_bias, L1_ffn_Wg, L1_ffn_Wu, L1_ffn_Wd, L1_ffn_conv_w, L1_ffn_conv_b):
    import jax
    import jax.numpy as jnp

    def _L0_xattn_ref(query, key, value, Wq, bq, Wk, bk, Wv, bv, Wo, bo):
        import jax, jax.numpy as jnp
        import numpy as np
        H = 16
        D_MODEL = 128
        D_K = D_MODEL // H

        def _mha(query, key, value, Wq, bq, Wk, bk, Wv, bv, Wo, bo):
            B, S, _ = query.shape
            q = query @ Wq.T + bq
            k = key @ Wk.T + bk
            v = value @ Wv.T + bv
            q = q.reshape(B, S, H, D_K).transpose(0, 2, 1, 3)
            k = k.reshape(B, S, H, D_K).transpose(0, 2, 1, 3)
            v = v.reshape(B, S, H, D_K).transpose(0, 2, 1, 3)
            scores = jnp.einsum('bhqd,bhkd->bhqk', q, k) / jnp.sqrt(jnp.float32(D_K))
            stable = scores - jnp.max(scores, axis=-1, keepdims=True)
            e = jnp.exp(stable)
            attn = e / jnp.sum(e, axis=-1, keepdims=True)
            ctx = jnp.einsum('bhqk,bhkd->bhqd', attn, v)
            ctx = ctx.transpose(0, 2, 1, 3).reshape(B, S, H * D_K)
            return ctx @ Wo.T + bo
        return _mha(query, key, value, Wq, bq, Wk, bk, Wv, bv, Wo, bo)

    def _L0_ffn_ref(hidden_states, gate_w1, gate_b1, gate_w2, gate_b2, W1, b1, W2, b2, TW1, Tb1, TW2, Tb2):
        import jax, jax.numpy as jnp
        import numpy as np
        B, S, H, F, E = (8, 256, 128, 512, 8)
        INIT_LAMBDA = 0.2
        x = hidden_states
        h = jax.nn.relu(jnp.einsum('bsh,oh->bso', x, gate_w1) + gate_b1)
        g = jnp.einsum('bso,eo->bse', h, gate_w2) + gate_b2
        g = g.mean(axis=1)
        mW1 = W1 + jnp.einsum('be,efh->bfh', g, TW1)
        mb1 = b1 + g @ Tb1
        mW2 = W2 + jnp.einsum('be,ehf->bhf', g, TW2)
        mb2 = b2 + g @ Tb2
        u = jax.nn.gelu(jnp.einsum('bsh,bfh->bsf', x, mW1) + mb1[:, None, :])
        out = jnp.einsum('bsf,bhf->bsh', u, mW2) + mb2[:, None, :]
        return out

    def _L1_xattn_ref(queries, keys, values, wq_w, wq_b, wk_w, wk_b, wv_w, wv_b, mk, mv, wo_w, wo_b):
        import jax, jax.numpy as jnp
        import numpy as np
        H, DK, DV = (16, 64, 64)
        MEM = 128
        D_MODEL = 128
        OUT_DIM = 128
        B, S, _ = queries.shape
        q = (queries @ wq_w + wq_b).reshape(B, S, H, DK).transpose(0, 2, 1, 3)
        k_proj = keys @ wk_w + wk_b
        v_proj = values @ wv_w + wv_b
        k_ext = jnp.concatenate([k_proj, jnp.broadcast_to(mk, (B, MEM, H * DK))], axis=1)
        v_ext = jnp.concatenate([v_proj, jnp.broadcast_to(mv, (B, MEM, H * DV))], axis=1)
        T = S + MEM
        k = k_ext.reshape(B, T, H, DK).transpose(0, 2, 1, 3)
        v = v_ext.reshape(B, T, H, DV).transpose(0, 2, 1, 3)
        scores = jnp.einsum('bhsd,bhtd->bhst', q, k) / jnp.sqrt(jnp.float32(DK))
        attn = jax.nn.softmax(scores, axis=-1)
        out = jnp.einsum('bhst,bhtd->bhsd', attn, v)
        out = out.transpose(0, 2, 1, 3).reshape(B, S, H * DV)
        return out @ wo_w + wo_b

    def _L1_ffn_ref(hidden_states, Wr, router_bias, Wg, Wu, Wd, conv_w, conv_b):
        import jax, jax.numpy as jnp
        import numpy as np
        from jax import lax
        H = 128
        E = 8
        E_MLP = E - 4
        TOP_K = 2
        I = 64
        KC = 4
        SHARED_SCALE = 1.0
        B, S, Hd = hidden_states.shape
        T = B * S
        x = hidden_states.reshape(T, Hd)
        scores = jax.nn.sigmoid(x @ Wr)
        _, idx = lax.top_k(scores + router_bias, TOP_K)
        w = jnp.take_along_axis(scores, idx, axis=-1)
        w = w / (jnp.sum(w, axis=-1, keepdims=True) + 1e-09)
        cw = jnp.zeros((T, E), dtype=x.dtype).at[jnp.arange(T)[:, None], idx].add(w)
        g = jnp.einsum('th,ehi->tei', x, Wg)
        u = jnp.einsum('th,ehi->tei', x, Wu)
        hid = jax.nn.silu(g) * u
        mlp_out = jnp.einsum('tei,eih->teh', hid, Wd)
        routed = jnp.einsum('te,teh->th', cw[:, :E_MLP], mlp_out)
        routed = routed + cw[:, E_MLP:E_MLP + 1] * x
        routed = routed + cw[:, E_MLP + 2:E_MLP + 3] * x
        routed = routed + cw[:, E_MLP + 3:E_MLP + 4] * jax.nn.relu(x)
        routed = routed.reshape(B, S, Hd)
        shared = lax.conv_general_dilated(hidden_states, conv_w, window_strides=(1,), padding=[(KC - 1, 0)], dimension_numbers=('NHC', 'HIO', 'NHC'), feature_group_count=Hd) + conv_b
        return routed + SHARED_SCALE * shared
    x = x + _L0_xattn_ref(_layernorm(x, axis=-1), ctx_1024, ctx_1024, L0_xattn_Wq, L0_xattn_bq, L0_xattn_Wk, L0_xattn_bk, L0_xattn_Wv, L0_xattn_bv, L0_xattn_Wo, L0_xattn_bo)
    x = x + _L0_ffn_ref(_layernorm(x, axis=-1), L0_ffn_gate_w1, L0_ffn_gate_b1, L0_ffn_gate_w2, L0_ffn_gate_b2, L0_ffn_W1, L0_ffn_b1, L0_ffn_W2, L0_ffn_b2, L0_ffn_TW1, L0_ffn_Tb1, L0_ffn_TW2, L0_ffn_Tb2)
    x = x + _L1_xattn_ref(_layernorm(x, axis=-1), ctx_1024, ctx_1024, L1_xattn_wq_w, L1_xattn_wq_b, L1_xattn_wk_w, L1_xattn_wk_b, L1_xattn_wv_w, L1_xattn_wv_b, L1_xattn_mk, L1_xattn_mv, L1_xattn_wo_w, L1_xattn_wo_b)
    x = x + _L1_ffn_ref(_layernorm(x, axis=-1), L1_ffn_Wr, L1_ffn_router_bias, L1_ffn_Wg, L1_ffn_Wu, L1_ffn_Wd, L1_ffn_conv_w, L1_ffn_conv_b)
    return x

_drawn_inputs = setup_inputs


def setup_inputs(seed=0):
    import zlib

    import numpy as np

    out = dict(_drawn_inputs(seed))
    spreads = {'L0_xattn_bq': (0.0, 0.1),
     'L0_xattn_bk': (0.0, 0.8),
     'L0_xattn_bv': (0.0, 0.1),
     'L0_xattn_bo': (0.0, 0.1),
     'L0_ffn_gate_b1': (0.0, 0.559),
     'L0_ffn_gate_b2': (0.20000000298023224, 0.6),
     'L1_xattn_wq_b': (0.0, 0.319),
     'L1_xattn_wk_b': (0.0, 0.338),
     'L1_xattn_wv_b': (0.0, 0.1),
     'L1_xattn_wo_b': (0.0, 0.1),
     'L1_ffn_router_bias': (0.0, 0.1),
     'L1_ffn_conv_b': (0.0, 0.1)}
    factors = {'L0_ffn_gate_w1': 8.0,
     'L0_ffn_gate_w2': 4.907,
     'L0_ffn_b1': 4.455,
     'L0_ffn_Tb1': 7.857,
     'L0_ffn_Tb2': 3.033,
     'L1_xattn_mk': 8.0,
     'L1_xattn_mv': 8.0}
    for name, (base, spread) in spreads.items():
        noise = np.random.default_rng([zlib.crc32(name.encode()), seed]).standard_normal(out[name].shape)
        drawn = base * np.exp(spread * noise) if base else spread * noise
        out[name] = jnp.asarray(drawn.astype(out[name].dtype))
    for name, factor in factors.items():
        out[name] = (out[name] * factor).astype(out[name].dtype)
    return out
```

```python
from contextlib import ExitStack

import numpy as np

import concourse.bass as bass
from concourse import mybir

F32 = mybir.dt.float32
BF16 = mybir.dt.bfloat16
ALU = mybir.AluOpType
ACT = mybir.ActivationFunctionType
AX = mybir.AxisListType

P = 128
B, S, D = 4, 256, 128
T = B * S
NT = T // P
TB = S // P
H = 16
DK0 = D // H
DK1 = 64
MEM = 128
KT1 = (S + MEM) // P
E, F = 8, 512
J = P // E
FC = F // P
EM, EI = 4, 64
KC = 4
EPS = 1e-5

QPART = (0, 1, 0, 1, 0, 2)
KPART = (0, 0, 1, 1, 2, 0)
ST0 = len(QPART) * DK0
ST0X = ST0 + 2

PACK = {}


def _pack(name, *widths):
    at = 0
    for key, w in widths:
        PACK[key] = (name, at, w)
        at += w
    return at


N_EARLY = _pack("early", ("wk0", D), ("wv0", D), ("wq0", D), ("ident", P), ("bk0", 1), ("bq0", 1),
                ("gb1", 1), ("gb2", 1), ("b1", FC), ("bq1", H // 2), ("bk1", H // 2), ("convw", KC))
N_LATE = _pack("late", ("wo0", 4 * D), ("den_pick", 4 * H), ("den_spread", 4 * P), ("gw1", D), ("gw2", P),
               ("delta", J), ("w1", F), ("w2", FC * D), ("tb1", F), ("tb2", D), ("wgu", 2 * EM * EI),
               ("wd", 2 * D), ("wr", E), ("before", E * E))
ROWS = {}
_at = 0
for _k, _w in (("bv0", D), ("bo0", D), ("b2", D), ("bo1", D), ("convb", D), ("rb", E), ("bv1", H * DK1)):
    ROWS[_k] = (_at, _w)
    _at += _w
N_ROWS = _at


def schedule():
    units = []
    ring = [0]

    def small(kind, key, readers, banks=(0, 1)):
        units.append((kind, key, (banks[ring[0] % len(banks)],), readers))
        ring[0] += 1

    for half in range(2):
        units.append(("k0", (half,), (4 + half,), "a"))
    for half in range(2):
        units.append(("v0", (half,), (6 + half,), "v"))
    for half in range(2):
        units.append(("xt0", (half,), (half,), "a"))
    for half in range(2):
        units.append(("q0", (half,), (2 + half,), "a"))
    for u in range(H):
        small("a0", (0, u), "v")
    small("t0", (0,), "v")
    for b in range(B):
        for hp in range(H // 2):
            units.append(("s0", (b, hp), (2 + 2 * (hp % 2), 3 + 2 * (hp % 2)), "a"))
            if b + 1 < B:
                small("a0", (b + 1, 2 * hp), "v")
                small("a0", (b + 1, 2 * hp + 1), "v")
            if hp == 2 and b:
                small("d0", (b - 1,), "v")
            if hp == 4 and b:
                small("e0", (b - 1, 0), "v")
                small("e0", (b - 1, 1), "v")
            if hp == 6 and b:
                small("w0", (b - 1,), "v")
            if hp % 2 == 1 and hp > 1:
                units.append(("o0", (b, hp // 2 - 1), (6 + (hp // 2 - 1) % 2,), "a"))
        if b + 1 < B:
            small("t0", (b + 1,), "v")
        units.append(("o0", (b, H // 4 - 1), (7,), "a"))
    wide = (0, 1, 2, 3, 4, 5)
    small("d0", (B - 1,), "v", wide)
    for t in range(2):
        for half in range(2):
            small("v1", (t, half), "v", wide)
    for g in range(2):
        small("e0", (B - 1, g), "v", wide)
    for t in range(2, 5):
        for half in range(2):
            small("v1", (t, half), "v", wide)
    small("w0", (B - 1,), "v", wide)
    small("xt1", (0,), "a", wide)
    small("g1", (0,), "a", wide)
    for t in range(5, NT):
        for half in range(2):
            small("v1", (t, half), "v", wide)
    small("xt1", (1,), "a", wide)
    small("g1", (1,), "a", wide)
    for c in range(4):
        small("k1", (0, c), "av", wide)
    small("gc", (), "v", wide)
    for c in range(4, H // 2):
        small("k1", (0, c), "av", wide)
    small("mb", (), "v", wide)
    for k in range(4):
        small("m1", (k,), "v", wide)
    for k in range(4):
        small("m2", (k,), "v", wide)
    for b in range(B):
        for c in range(2):
            small("u1", (b, c), "a", wide)
        if b:
            small("y1", (b - 1,), "v", wide)
    small("y1", (B - 1,), "v", wide)
    for half in range(2):
        small("xt2", (half,), "a", wide)
    for c in range(H // 2):
        small("q1", (0, c), "av", wide)
    for h in range(H):
        for qt in range(TB):
            small("a1", (0, h, qt), "v", wide)
    small("t1", (0,), "v", wide)
    small("q1", (1, 0), "av", wide)
    small("k1", (1, 0), "av", wide)
    for b in range(B):
        for hp in range(H // 2):
            for h in (2 * hp, 2 * hp + 1):
                units.append(("s1", (b, h), (2 + 2 * (h % 2), 3 + 2 * (h % 2)), "a"))
                if b + 1 < B:
                    small("a1", (b + 1, h, 0), "v")
                    small("a1", (b + 1, h, 1), "v")
                if h % 2 == 0 and b + 1 < B and hp + 1 < H // 2:
                    small("q1", (b + 1, hp + 1), "av")
                    small("k1", (b + 1, hp + 1), "av")
            if hp:
                units.append(("o1", (b, hp - 1), (6 + (hp - 1) % 2,), "v"))
            if hp == 1 and b:
                small("w1", (b - 1,), "v")
        if b + 1 < B:
            small("t1", (b + 1,), "v")
        units.append(("o1", (b, H // 2 - 1), (6 + (H // 2 - 1) % 2,), "v"))
        if b + 2 < B:
            small("q1", (b + 2, 0), "av")
            small("k1", (b + 2, 0), "av")
    small("w1", (B - 1,), "v", wide)
    for half in range(2):
        small("xt3", (half,), "a", wide)
    small("rt", (), "a", wide)
    for t in range(NT):
        small("gu", (t,), "av", wide)
        if t >= 2:
            small("ht", (t - 2,), "a", wide)
        if t >= 3:
            small("f3", (t - 3,), "v", wide)
    for t in range(NT, NT + 3):
        if t - 2 < NT:
            small("ht", (t - 2,), "a", wide)
        small("f3", (t - 3,), "v", wide)
    return units


def xattn_ffn_kernel(nc, x, ctx_t, early, late, rows, tw1, tw2, wq1, wk1, wv1, wo1, mem_k, mem_v, out):
    units = schedule()
    index, count, reads = {}, {}, {}
    last_of_bank, before = {}, []
    for n, (kind, key, banks, readers) in enumerate(units):
        count[kind] = count.get(kind, 0) + 1
        index[kind, key] = (count[kind], banks)
        before.append([last_of_bank.get(k) for k in banks])
        for k in banks:
            last_of_bank[k] = (kind, count[kind], readers)

    with ExitStack() as ctx:
        def sb(name, shape, dt=F32):
            return ctx.enter_context(nc.sbuf_tensor(name, shape, dt))

        sems = {}

        def sem(name):
            if name not in sems:
                sems[name] = ctx.enter_context(nc.semaphore(name))
            return sems[name]

        psum = ctx.enter_context(nc.psum_tensor("psum", [P, 8, 512], F32))

        r_q = sb("r_q", [P, 2 * H * S])
        r_k = sb("r_k", [P, 2 * H * S])
        r_p = sb("r_p", [P, 4096])
        r_w = sb("r_w", [P, 6144])
        r_o = sb("r_o", [P, 4096])
        r_v = sb("r_v", [P, NT * H * DK1])

        tw_sb = [r_q[:, i * 4096:(i + 1) * 4096] for i in range(2)]
        qa = [r_q[:, i * H * S:(i + 1) * H * S].rearrange("p (h s) -> p h s", h=H) for i in range(2)]
        kb = [r_k[:, i * H * S:(i + 1) * H * S].rearrange("p (h s) -> p h s", h=H) for i in range(2)]
        half_k = H * S // 2
        stack = [r_k[:, i * half_k:(i + 1) * half_k].bitcast(BF16).rearrange("p (h s) -> p h s", h=H)
                 for i in range(4)]
        q_stack, k_stack = stack[:2], stack[2:]
        p0 = r_p[:, :].rearrange("p (n j k s) -> p n j k s", n=4, j=2, k=2)
        p1 = r_p[:, 0:4 * KT1 * S].rearrange("p (n k s) -> p n k s", n=4, k=KT1)
        mw1 = r_p[:, 0:B * F].rearrange("p (b f) -> p b f", b=B)
        mw2 = r_p[:, B * F:2 * B * F].rearrange("p (c b h) -> p c b h", c=FC, b=B)
        qk_f = [r_w[:, i * T:(i + 1) * T] for i in range(2)]
        rest = r_w[:, 2 * T:3 * T]
        part = [[r_w[:, 3 * T + (3 * i + n) * T // 2:3 * T + (3 * i + n + 1) * T // 2].bitcast(BF16)
                 for n in range(3)] for i in range(2)]
        wq1_sb, wk1_sb, wv1_sb, wo1_sb = (r_w[:, i * 1024:(i + 1) * 1024] for i in range(4))
        mem_k_sb = r_w[:, 4096:4096 + H * MEM].rearrange("p (h m) -> p h m", h=H)
        u0 = [r_o[:, i * 1024:(i + 1) * 1024] for i in range(2)]
        un0 = r_o[:, 2048:3072]
        ct1 = [r_o[:, i * 2048:(i + 1) * 2048].rearrange("p (c s) -> p c s", c=H // 2) for i in range(2)]
        ff_u = [r_o[:, i * 1024:(i + 1) * 1024] for i in range(2)]
        ff_y = [r_o[:, (2 + i) * 1024:(3 + i) * 1024] for i in range(2)]
        mem_v_sb = r_p[:, 4 * KT1 * S:4 * KT1 * S + H * DK1]
        v0 = r_v[:, 0:NT * H * 32].rearrange("p (t h e) -> p t h e", t=NT, h=H)
        v1 = r_v[:, :].rearrange("p (t n) -> p t n", t=NT)

        hid = [r_p[:, i * 256:(i + 1) * 256] for i in range(2)]
        hidt = [r_p[:, 512 + i * 256:512 + (i + 1) * 256] for i in range(2)]
        gu_t = [r_p[:, 1024 + i * 256:1024 + (i + 1) * 256] for i in range(2)]
        gu_w = [r_p[:, 1536 + i * 256:1536 + (i + 1) * 256] for i in range(2)]
        conv = r_p[:, 2560:2560 + T]

        ctx_sb = sb("ctx_sb", [P, T])
        early_sb = sb("early_sb", [P, N_EARLY])
        late_sb = sb("late_sb", [P, N_LATE])
        rows_sb = sb("rows_sb", [P, N_ROWS])
        xs = [sb("x0_sb", [P, NT, D]), sb("x1_sb", [P, NT, D]), sb("x2_sb", [P, NT, D])]
        xs.append(xs[0])
        xb = xs
        xn = sb("xn", [P, NT, D])
        xt = sb("xt", [P, T])
        stats = sb("stats", [P, NT, 6])
        mv = sb("mv", [P, NT, 2])
        veps = sb("veps", [P, NT])
        rstd = sb("rstd", [P, NT])
        minus_half = sb("minus_half", [P, NT])
        neg_max = sb("neg_max", [P, 2, TB, H])
        nm_rest = sb("nm_rest", [P, TB, H])
        nm_part = sb("nm_part", [P, TB, 2 * H], BF16)
        ident_bf = sb("ident_bf", [P, P], BF16)
        nmt0 = sb("nmt0", [2 * H, S], BF16)
        nmt1 = sb("nmt1", [H, S])
        rden1 = sb("rden1", [P, 2, S])
        rden0 = rden1[0:H, 0, :]
        ones64 = sb("ones64", [P, DK1])
        hsum = sb("hsum", [P, B])
        gate_relu = [r_p[:, b * S:(b + 1) * S] for b in range(B)]
        gcol = sb("gcol", [P, B])
        gdiag = sb("gdiag", [P, B, J])
        gwide = sb("gwide", [P, B, P])
        mb1 = sb("mb1", [P, FC, B])
        router = r_o[:, 2 * NT * E * E:2 * NT * E * E + 4 * NT * E].rearrange("p (n t e) -> p n t e", n=4, t=NT)
        cmp_gt, cmp_eq = (r_o[:, i * NT * E * E:(i + 1) * NT * E * E].rearrange("p (t i j) -> p t i j", t=NT, i=E)
                          for i in range(2))
        rank = sb("rank", [P, NT, E])
        cw_sum = sb("cw_sum", [P, 2, NT])
        stay = sb("stay", [P, NT])

        def pk(key, p=P):
            name, at, w = PACK[key]
            return (early_sb if name == "early" else late_sb)[0:p, at:at + w]

        def row(key):
            at, w = ROWS[key]
            return rows_sb[:, at:at + w]

        ident = pk("ident")
        scratch = nc.dram_tensor("parts_dram", [2, 3, P, T], BF16).ap()

        def ready(eng, kind, *key):
            n, banks = index[kind, key]
            eng.wait_ge(sem(kind + "_filled"), n)
            return banks[0]

        def bank(n, cols=slice(0, 512), parts_=slice(0, P)):
            return psum[parts_, n, cols]

        x_tiles = x.rearrange("(t p) d -> p t d", p=P)
        out_tiles = out.rearrange("(t p) d -> p t d", p=P)

        block = ctx.enter_context(nc.Block())

        @block.sync
        def _(sp):
            sp.dma_start(xs[0][:, :, :], x_tiles).then_inc(sem("x_loaded"), 16)
            sp.dma_start(ctx_sb[:, :], ctx_t).then_inc(sem("ctx_loaded"), 16)
            sp.dma_start(early_sb[:, :], early).then_inc(sem("early_loaded"), 16)
            sp.dma_start(rows_sb[:, :], rows.broadcast_to([P, N_ROWS])).then_inc(sem("rows_loaded"), 16)
            sp.dma_start(late_sb[:, :], late).then_inc(sem("late_loaded"), 16)
            for i in (1, 0):
                for n in range(3):
                    sp.wait_ge(sem(f"part{n}_ready"), 2 - i)
                    sp.dma_start(scratch[i, n], part[i][n]).then_inc(sem("parts_stored"), 16)
            sp.wait_ge(sem("parts_stored"), 6 * 16)
            sp.wait_ge(sem("stack_ones"), 2)

            def load_stacks(b):
                if b >= 2:
                    sp.wait_ge(sem("s0_filled"), index["s0", (b - 2, H // 2 - 1)][0])
                for i, to, of in ((1, k_stack[b % 2], KPART), (0, q_stack[b % 2], QPART)):
                    for g, n in enumerate(of):
                        src = scratch[i, n].rearrange("(h d) t -> d h t", d=DK0)[:, :, b * S:(b + 1) * S]
                        sp.dma_start(to[g * DK0:(g + 1) * DK0], src).then_inc(sem(f"stack_loaded{b % 2}"), 16)

            load_stacks(0)
            load_stacks(1)
            sp.dma_start(tw_sb[0], tw1).then_inc(sem("tw_loaded"), 16)
            sp.dma_start(tw_sb[1], tw2).then_inc(sem("tw_loaded"), 16)
            for w, to in ((wq1, wq1_sb), (wk1, wk1_sb), (wv1, wv1_sb), (wo1, wo1_sb)):
                sp.dma_start(to, w).then_inc(sem("w1_loaded"), 16)
            sp.dma_start(mem_k_sb[0:DK1], mem_k).then_inc(sem("w1_loaded"), 16)
            for b in range(B):
                sp.wait_ge(sem("t0_read_v"), b + 1)
                for n in range(2):
                    sp.dma_start(q_stack[b % 2][ST0 + n:ST0 + n + 1],
                                 nmt0[n * H:(n + 1) * H, :]).then_inc(sem("max0_stored"), 16)
                if b + 2 < B:
                    load_stacks(b + 2)
            sp.wait_ge(sem("y1_filled"), B)
            sp.dma_start(mem_v_sb, mem_v).then_inc(sem("memv_loaded"), 16)
            for b in range(B):
                sp.wait_ge(sem("t1_read_v"), b + 1)
                sp.dma_start(qa[b % 2][DK1:DK1 + 1], nmt1[:, :]).then_inc(sem("max1_stored"), 16)
            for t in range(NT):
                sp.wait_ge(sem("f3_read_v"), t + 1)
                sp.dma_start(out_tiles[:, t, :], xs[1][:, t, :]).then_inc(sem("out_stored"), 16)
            sp.wait_ge(sem("out_stored"), 16 * NT)

        @block.tensor
        def _(pe):
            def matmul(o, w, m, start=True, stop=True):
                return nc.tensor.matmul(o, w, m, start=start, stop=stop, skip_group_check=True)

            def k0(o, half):
                if half == 0:
                    pe.wait_ge(sem("ctx_loaded"), 16)
                    pe.wait_ge(sem("early_loaded"), 16)
                return matmul(bank(o), pk("wk0"), ctx_sb[:, half * 512:(half + 1) * 512])

            def v0_(o, half):
                for t in range(4):
                    at = half * 512 + t * P
                    mm = matmul(bank(o, slice(t * P, (t + 1) * P)), ctx_sb[:, at:at + P], pk("wv0"))
                return mm

            def transposes(layer, o, half):
                for b in range(2):
                    pe.wait_ge(sem("xn_ready"), layer * B + half * 2 + b + 1)
                    for t in range(TB):
                        n = b * TB + t
                        mm = nc.tensor.transpose(bank(o, slice(n * P, (n + 1) * P)), xn[:, half * 4 + n, :], ident)
                return mm

            def q0(o, half):
                pe.wait_ge(sem("xt0_read_a"), half + 1)
                return matmul(bank(o), pk("wq0"), xt[:, half * 512:(half + 1) * 512])

            def a0(o, b, u):
                if u == 0:
                    pe.wait_ge(sem(f"stack_loaded{b % 2}"), 12 * 16 * (b // 2 + 1))
                hp, qt = u // 2, u % 2
                for j in range(2):
                    h = 2 * hp + j
                    mm = matmul(bank(o, slice(j * S, (j + 1) * S)),
                                q_stack[b % 2][0:ST0, h, qt * P:(qt + 1) * P], k_stack[b % 2][0:ST0, h, :])
                return mm

            def t0(o, b):
                pe.wait_ge(sem("nm_part_ready"), b + 1)
                pe.wait_ge(sem("ident_ready"), 1)
                for qt in range(TB):
                    mm = nc.tensor.transpose(bank(o, slice(0, P), slice(0, 2 * H)).bitcast(BF16)[:, qt * P:(qt + 1) * P],
                                             nm_part[:, qt, :], ident_bf[:, :])
                return mm

            def s0(o, b, hp):
                if hp == 0:
                    pe.wait_ge(sem("max0_stored"), 2 * 16 * (b + 1))
                for j in range(2):
                    h = 2 * hp + j
                    for kt in range(TB):
                        mm = matmul(bank(o + j, slice(kt * S, (kt + 1) * S)),
                                    k_stack[b % 2][:, h, kt * P:(kt + 1) * P], q_stack[b % 2][:, h, :])
                return mm

            def o0(o, b, g):
                if b == 0 and g == 0:
                    pe.wait_ge(sem("v0_read_v"), 2)
                pe.wait_ge(sem("s0_read_a"), 8 * b + 2 * g + 2)
                for kt in range(TB):
                    for j in range(4):
                        pair = 8 * b + 2 * g + j // 2
                        mm = matmul(bank(o, slice(0, S), slice(32 * j, 32 * j + 32)),
                                    v0[:, b * TB + kt, 4 * g + j, :], p0[:, pair % 4, j % 2, kt, :],
                                    start=(kt == 0), stop=(kt == TB - 1))
                return mm

            def d0(o, b):
                if b == 0:
                    pe.wait_ge(sem("late_loaded"), 16)
                pe.wait_ge(sem("o0_read_a"), 4 * b + 4)
                for g in range(4):
                    mm = matmul(bank(o, slice(0, S), slice(0, H)), pk("den_pick")[:, g * H:(g + 1) * H],
                                u0[b % 2][:, g * S:(g + 1) * S], start=(g == 0), stop=(g == 3))
                return mm

            def e0(o, b, half):
                pe.wait_ge(sem("d0_read_v"), b + 1)
                for j in range(2):
                    g = 2 * half + j
                    mm = matmul(bank(o, slice(j * S, (j + 1) * S)), pk("den_spread", H)[:, g * P:(g + 1) * P],
                                rden0)
                return mm

            def w0(o, b):
                pe.wait_ge(sem("e0_read_v"), 2 * b + 2)
                for t in range(TB):
                    for g in range(4):
                        mm = matmul(bank(o, slice(t * P, (t + 1) * P)),
                                    un0[:, g * S + t * P:g * S + (t + 1) * P], pk("wo0")[:, g * D:(g + 1) * D],
                                    start=(g == 0), stop=(g == 3))
                return mm

            def v1_(o, t, half):
                if t == 0 and half == 0:
                    pe.wait_ge(sem("w1_loaded"), 5 * 16)
                return matmul(bank(o), ctx_sb[:, t * P:(t + 1) * P], wv1_sb[:, half * 512:(half + 1) * 512])

            def k1(o, b, c):
                return matmul(bank(o, slice(0, S)), wk1_sb[:, c * P:(c + 1) * P], ctx_sb[:, b * S:(b + 1) * S])

            def g1(o, half):
                pe.wait_ge(sem("xt1_read_a"), half + 1)
                return matmul(bank(o), pk("gw1"), xt[:, half * 512:(half + 1) * 512])

            def gc(o):
                pe.wait_ge(sem("g1_read_a"), 2)
                return matmul(bank(o, slice(0, B)), pk("gw2"), hsum[:, :])

            def mb(o):
                pe.wait_ge(sem("gc_read_v"), 1)
                for c in range(FC):
                    mm = matmul(bank(o, slice(c * B, (c + 1) * B)), pk("tb1")[:, c * P:(c + 1) * P], gcol[:, :])
                return mm

            def merge(i, o, k):
                if i == 0 and k == 0:
                    pe.wait_ge(sem("tw_loaded"), 2 * 16)
                    pe.wait_ge(sem("gdiag_ready"), 1)
                for n in range(8):
                    at = (k * 8 + n) * P if i == 0 else (n * FC + k) * P
                    mm = matmul(bank(o, slice(n * B * J, (n + 1) * B * J)), tw_sb[i][:, at:at + P],
                                gdiag[:, :, :].rearrange("p b j -> p (b j)"))
                return mm

            def u1(o, b, c2):
                if b == 0 and c2 == 0:
                    pe.wait_ge(sem("m1_read_v"), 4)
                for j in range(2):
                    c = 2 * c2 + j
                    mm = matmul(bank(o, slice(j * S, (j + 1) * S)), mw1[:, b, c * P:(c + 1) * P],
                                xt[:, b * S:(b + 1) * S])
                return mm

            def y1(o, b):
                if b == 0:
                    pe.wait_ge(sem("m2_read_v"), 4)
                pe.wait_ge(sem("ffy_ready"), b + 1)
                for t in range(TB):
                    for c in range(FC):
                        matmul(bank(o, slice(t * P, (t + 1) * P)), ff_y[b % 2][:, c * S + t * P:c * S + (t + 1) * P],
                               mw2[:, c, b, :], start=(c == 0), stop=False)
                    mm = matmul(bank(o, slice(t * P, (t + 1) * P)), gwide[:, b, :], pk("tb2"), start=False)
                return mm

            def q1(o, b, c):
                if b == 0 and c == 0:
                    pe.wait_ge(sem("xt2_read_a"), 2)
                return matmul(bank(o, slice(0, S)), wq1_sb[:, c * P:(c + 1) * P], xt[:, b * S:(b + 1) * S])

            def tops(ap):
                return ap.bitcast(BF16)[:, 1::2]

            def a1(o, b, h, qt):
                qn, kn = index["q1", (b, h // 2)][0], index["k1", (b, h // 2)][0]
                for who in ("a" if h % 2 == 0 else "v"):
                    pe.wait_ge(sem("q1_read_" + who), qn)
                    pe.wait_ge(sem("k1_read_" + who), kn)
                w = tops(qa[b % 2][0:DK1, h, qt * P:(qt + 1) * P])
                matmul(bank(o, slice(0, S)), w, tops(kb[b % 2][0:DK1, h, :]))
                return matmul(bank(o, slice(S, S + MEM)), w, tops(mem_k_sb[0:DK1, h, :]))

            def t1(o, b):
                pe.wait_ge(sem("a1_read_v"), H * TB * (b + 1))
                for qt in range(TB):
                    mm = nc.tensor.transpose(bank(o, slice(qt * P, (qt + 1) * P), slice(0, H)),
                                             neg_max[:, b % 2, qt, :], ident)
                return mm

            def s1(o, b, h):
                if h == 0:
                    pe.wait_ge(sem("max1_stored"), 16 * (b + 1))
                    pe.wait_ge(sem("kb_ones"), 2)
                for kt in range(KT1):
                    w = kb[b % 2][:, h, kt * P:(kt + 1) * P] if kt < TB else mem_k_sb[:, h, :]
                    mm = matmul(bank(o + kt // 2, slice((kt % 2) * S, (kt % 2 + 1) * S)), w,
                                qa[b % 2][:, h, :])
                return mm

            def o1(o, b, hp):
                pe.wait_ge(sem("s1_read_a"), H * b + 2 * hp + 2)
                if b == 0 and hp == 0:
                    pe.wait_ge(sem("memv_loaded"), 16)
                    pe.wait_ge(sem("ones64_ready"), 1)
                for den in range(2):
                    for kt in range(KT1):
                        for j in range(2):
                            h = 2 * hp + j
                            if den:
                                w = ones64[:, :]
                            elif kt < TB:
                                w = v1[:, b * TB + kt, h * DK1:(h + 1) * DK1]
                            else:
                                w = mem_v_sb[:, h * DK1:(h + 1) * DK1]
                            mm = matmul(bank(o, slice(den * S, (den + 1) * S), slice(j * DK1, (j + 1) * DK1)), w,
                                        p1[:, (H * b + h) % 4, kt, :], start=(kt == 0), stop=(kt == KT1 - 1))
                return mm

            def w1(o, b):
                pe.wait_ge(sem("o1_read_v"), (H // 2) * (b + 1))
                for t in range(TB):
                    for c in range(H // 2):
                        mm = matmul(bank(o, slice(t * P, (t + 1) * P)), ct1[b % 2][:, c, t * P:(t + 1) * P],
                                    wo1_sb[:, c * D:(c + 1) * D], start=(c == 0), stop=(c == H // 2 - 1))
                return mm

            def rt(o):
                pe.wait_ge(sem("xt3_read_a"), 2)
                for t in range(NT):
                    mm = matmul(bank(o, slice(t * E, (t + 1) * E)), xt[:, t * P:(t + 1) * P], pk("wr"))
                return mm

            def gu(o, t):
                return matmul(bank(o), xt[:, t * P:(t + 1) * P], pk("wgu"))

            def ht(o, t):
                pe.wait_ge(sem("hid_ready"), t + 1)
                for c in range(2):
                    mm = nc.tensor.transpose(bank(o, slice(c * P, (c + 1) * P)), hid[t % 2][:, c * P:(c + 1) * P],
                                             ident)
                return mm

            def f3(o, t):
                pe.wait_ge(sem("ht_read_a"), t + 1)
                if t == 0:
                    pe.wait_ge(sem("conv_ready"), 1)
                for c in range(2):
                    matmul(bank(o, slice(0, D)), hidt[t % 2][:, c * P:(c + 1) * P], pk("wd")[:, c * D:(c + 1) * D],
                           start=(c == 0), stop=False)
                return matmul(bank(o, slice(0, D)), conv[:, t * P:(t + 1) * P], ident, start=False)

            emit = {
                "k0": k0, "v0": v0_, "q0": q0, "a0": a0, "t0": t0, "s0": s0, "o0": o0, "d0": d0, "e0": e0, "w0": w0,
                "v1": v1_, "k1": k1, "g1": g1, "gc": gc, "mb": mb, "u1": u1, "y1": y1, "q1": q1, "a1": a1, "t1": t1,
                "s1": s1, "o1": o1, "w1": w1, "rt": rt, "gu": gu, "ht": ht, "f3": f3,
                "m1": lambda o, k: merge(0, o, k), "m2": lambda o, k: merge(1, o, k),
                "xt0": lambda o, h: transposes(0, o, h), "xt1": lambda o, h: transposes(1, o, h),
                "xt2": lambda o, h: transposes(2, o, h), "xt3": lambda o, h: transposes(3, o, h),
            }
            for (kind, key, banks, _), earlier in zip(units, before):
                for was in earlier:
                    if was:
                        for who in was[2]:
                            pe.wait_ge(sem(f"{was[0]}_read_{who}"), was[1])
                emit[kind](banks[0], *key).then_inc(sem(kind + "_filled"), 1)

        @block.scalar
        def _(act):
            def done(ins, kind):
                return ins.then_inc(sem(kind + "_read_a"), 1)

            hsum_n = 0
            for kind, key, banks, readers in units:
                if "a" not in readers:
                    continue
                o = ready(act, kind, *key)
                if kind in ("k0", "q0"):
                    i, half = (1 if kind == "k0" else 0), key[0]
                    done(nc.scalar.activation(qk_f[i][:, half * 512:(half + 1) * 512], bank(o), ACT.Identity,
                                              bias=pk("bk0" if i else "bq0")), kind)
                elif kind in ("xt0", "xt1", "xt2", "xt3"):
                    layer, half = int(kind[2]), key[0]
                    if layer == 2:
                        act.wait_ge(sem("u1_filled"), 2 * B)
                    if layer == 1:
                        act.wait_ge(sem("q0_filled"), 2)
                    if layer == 3:
                        act.wait_ge(sem("q1_filled"), B * H // 2)
                    ins = nc.scalar.activation(xt[:, half * 512:(half + 1) * 512], bank(o), ACT.Copy)
                    done(ins, kind)
                elif kind == "s0":
                    b, hp = key
                    pair = 8 * b + hp
                    if pair >= 4:
                        act.wait_ge(sem("o0_filled"), (pair - 4) // 2 + 1)
                    ins = nc.scalar.activation(p0[:, pair % 4].rearrange("p j k s -> p (j k s)"),
                                               psum[:, o:o + 2, :].rearrange("p a n -> p (a n)"), ACT.Exp,
                                               scale=float(DK0) ** -0.5)
                    ins.then_inc(sem("s0_read_a"), 1)
                elif kind == "o0":
                    b, g = key
                    if b >= 2 and g == 0:
                        act.wait_ge(sem("e0_read_v"), 2 * (b - 2) + 2)
                        act.wait_ge(sem("d0_filled"), b - 1)
                    nc.scalar.activation(u0[b % 2][:, g * S:(g + 1) * S], bank(o, slice(0, S)),
                                         ACT.Copy).then_inc(sem("o0_read_a"), 1)
                elif kind == "g1":
                    act.wait_ge(sem("o0_filled"), 4 * B)
                    for j in range(2):
                        b = 2 * key[0] + j
                        ins = nc.scalar.activation(gate_relu[b], bank(o, slice(j * S, (j + 1) * S)), ACT.Relu,
                                                   bias=pk("gb1"), accum_out=hsum[:, b:b + 1])
                    done(ins, kind)
                elif kind in ("k1", "q1"):
                    b, c = key
                    if kind == "k1" and b == 0 and c == 0:
                        act.wait_ge(sem("s0_filled"), 8 * B)
                    if kind == "q1" and b == 0 and c == 0:
                        act.wait_ge(sem("m2_filled"), 4)
                    if b >= 2:
                        act.wait_ge(sem("s1_filled"), index["s1", (b - 2, 2 * c)][0])
                    to = (kb if kind == "k1" else qa)[b % 2]
                    done(nc.scalar.activation(to[0:DK1, 2 * c, :], bank(o, slice(0, S), slice(0, DK1)), ACT.Identity,
                                              bias=pk("bk1" if kind == "k1" else "bq1")[0:DK1, c:c + 1]), kind)
                elif kind == "u1":
                    b, c2 = key
                    if b == 0 and c2 == 0:
                        act.wait_ge(sem("mb_read_v"), 1)
                        act.wait_ge(sem("w0_filled"), B)
                    if b >= 2 and c2 == 0:
                        act.wait_ge(sem("ffy_ready"), b - 1)
                    for j in range(2):
                        c = 2 * c2 + j
                        ins = nc.scalar.activation(ff_u[b % 2][:, c * S:(c + 1) * S], bank(o, slice(j * S, (j + 1) * S)),
                                                   ACT.Identity, bias=mb1[:, c, b:b + 1])
                    ins.then_inc(sem("u1_read_a"), 1)
                    if c2 == 1:
                        act.wait_ge(sem("cubic_ready"), b + 1)
                        nc.scalar.activation(ff_y[b % 2], ff_y[b % 2], ACT.Tanh,
                                             scale=0.7978845608028654).then_inc(sem("tanh_ready"), 1)
                elif kind == "s1":
                    b, h = key
                    n = H * b + h
                    if n >= 4:
                        act.wait_ge(sem("o1_filled"), (n - 4) // 2 + 1)
                    elif n == 0:
                        act.wait_ge(sem("y1_filled"), B)
                    nc.scalar.activation(p1[:, n % 4].rearrange("p k s -> p (k s)"),
                                         psum[:, o:o + 2, :].rearrange("p a n -> p (a n)")[:, 0:KT1 * S], ACT.Exp,
                                         scale=float(DK1) ** -0.5).then_inc(sem("s1_read_a"), 1)
                elif kind == "rt":
                    nc.scalar.activation(router[:, 0].rearrange("p t e -> p (t e)"), bank(o, slice(0, NT * E)),
                                         ACT.Tanh, scale=0.5).then_inc(sem("rt_read_a"), 1)
                elif kind == "gu":
                    t = key[0]
                    if t == 0:
                        act.wait_ge(sem("o1_filled"), B * H // 2)
                    if t >= 2:
                        act.wait_ge(sem("gu_read_v"), t - 1)
                    nc.scalar.activation(gu_t[t % 2], bank(o, slice(0, 256)), ACT.Tanh,
                                         scale=0.5).then_inc(sem("gu_read_a"), 1)
                elif kind == "ht":
                    t = key[0]
                    if t >= 2:
                        act.wait_ge(sem("f3_filled"), t - 1)
                    nc.scalar.activation(hidt[t % 2], bank(o, slice(0, 256)), ACT.Copy).then_inc(sem("ht_read_a"), 1)

        @block.gpsimd
        def _(pool):
            steps = [0]

            def then(ins):
                steps[0] += 1
                ins.then_inc(sem("pool_step"), 1)
                pool.wait_ge(sem("pool_step"), steps[0])

            then(nc.gpsimd.memset(minus_half[:, :], -0.5))

            def inverse_root(layer, b):
                if layer * B + b:
                    pool.wait_ge(sem("rstd_ready"), layer * B + b)
                t = slice(b * TB, (b + 1) * TB)
                pool.wait_ge(sem("mv_ready"), layer * B + b + 1)
                then(nc.gpsimd.tensor_scalar(veps[:, t], mv[:, t, 1], EPS, None, ALU.add))
                nc.gpsimd.tensor_tensor(rstd[:, t], veps[:, t], minus_half[:, t], ALU.pow).then_inc(sem("rstd_ready"), 1)

            for b in range(B):
                inverse_root(0, b)
            pool.wait_ge(sem("rstd_ready"), B)
            then(nc.gpsimd.memset(r_k[DK1:P, :], 0.0))
            for i in range(2):
                then(nc.gpsimd.memset(q_stack[i][0:DK1], 0.0))
                nc.gpsimd.memset(k_stack[i][0:DK1], 1.0).then_inc(sem("stack_ones"), 1)
                pool.wait_ge(sem("stack_ones"), i + 1)
            for i in (1, 0):
                n = 1 - i
                pool.wait_ge(sem("k0_read_a" if i else "q0_read_a"), 2)
                pool.wait_ge(sem("part0_ready"), n + 1)
                if n:
                    pool.wait_ge(sem("part2_ready"), n)
                nc.gpsimd.tensor_tensor(rest, qk_f[i], part[i][0], ALU.subtract).then_inc(sem("rest_ready"), 1)
                pool.wait_ge(sem("part1_ready"), n + 1)
                nc.gpsimd.tensor_tensor(part[i][2], rest, part[i][1], ALU.subtract).then_inc(sem("part2_ready"), 1)
            pool.wait_ge(sem("parts_stored"), 6 * 16)
            pool.wait_ge(sem("part2_ready"), 2)
            then(nc.gpsimd.memset(mem_k_sb[DK1:P], 0.0))
            then(nc.gpsimd.memset(mem_k_sb[DK1:DK1 + 1], 1.0))
            pool.wait_ge(sem("rows_loaded"), 16)

            def add_bias(layer, b, key, value=None):
                for t in range(b * TB, (b + 1) * TB):
                    ins = nc.gpsimd.tensor_tensor(xb[layer][:, t, :], xs[layer][:, t, :], row(key), ALU.add)
                ins.then_inc(sem("bias_added"), 1)

            for b in range(B):
                pool.wait_ge(sem("xn_ready"), b + 1)
                add_bias(0, b, "bo0")
            for b in range(B):
                inverse_root(1, b)
                pool.wait_ge(sem("xn_ready"), B + b + 1)
                add_bias(1, b, "b2")
            pool.wait_ge(sem("s0_filled"), B * H // 2)
            pool.wait_ge(sem("bias_added"), 2 * B)
            for i in range(2):
                nc.gpsimd.memset(kb[i][DK1:DK1 + 1], 1.0).then_inc(sem("kb_ones"), 1)
                pool.wait_ge(sem("kb_ones"), i + 1)

            def square(b):
                pool.wait_ge(sem("u1_read_a"), 2 * b + 2)
                if b >= 2:
                    pool.wait_ge(sem("y1_filled"), b - 1)
                nc.gpsimd.tensor_tensor(ff_y[b % 2], ff_u[b % 2], ff_u[b % 2], ALU.mult).then_inc(sem("square_ready"), 1)

            square(0)
            for b in range(B):
                if b + 1 < B:
                    square(b + 1)
                inverse_root(2, b)
                pool.wait_ge(sem("xn_ready"), 2 * B + b + 1)
                add_bias(2, b, "bo1")
            for b in range(B):
                inverse_root(3, b)
                pool.wait_ge(sem("xn_ready"), 3 * B + b + 1)
                add_bias(3, b, "convb")

        @block.vector
        def _(dve):
            steps = [0]

            def then(ins):
                steps[0] += 1
                ins.then_inc(sem("vector_step"), 1)
                dve.wait_ge(sem("vector_step"), steps[0])

            def signal(ins, kind):
                return ins.then_inc(sem(kind + "_read_v"), 1)

            def moments(layer, b):
                src = xs[layer]
                for t in range(b * TB, (b + 1) * TB):
                    ins = nc.vector.bn_stats(stats[:, t, :], src[:, t, :])
                then(ins)
                for t in range(b * TB, (b + 1) * TB):
                    ins = nc.vector.bn_aggr(mv[:, t, :], stats[:, t, :])
                ins.then_inc(sem("mv_ready"), 1)

            def normalise(layer, b):
                dve.wait_ge(sem("rstd_ready"), layer * B + b + 1)
                if layer:
                    dve.wait_ge(sem(f"xt{layer - 1}_filled"), 2)
                for t in range(b * TB, (b + 1) * TB):
                    ins = nc.vector.tensor_scalar(xn[:, t, :], xs[layer][:, t, :], mv[:, t, 0:1], rstd[:, t:t + 1],
                                                  ALU.subtract, ALU.mult)
                ins.then_inc(sem("xn_ready"), 1)

            def two_parts(i):
                n = 1 - i
                dve.wait_ge(sem("k0_read_a" if i else "q0_read_a"), 2)
                nc.vector.tensor_copy(part[i][0], qk_f[i]).then_inc(sem("part0_ready"), 1)
                dve.wait_ge(sem("rest_ready"), n + 1)
                nc.vector.tensor_copy(part[i][1], rest).then_inc(sem("part1_ready"), 1)

            nc.vector.memset(ones64[:, :], 1.0).then_inc(sem("ones64_ready"), 1)
            then(nc.vector.memset(v0[:, :, :, :].rearrange("p t h e -> p (t h e)"), 1.0))
            dve.wait_ge(sem("x_loaded"), 16)
            for b in range(B):
                moments(0, b)
            for b in range(B):
                normalise(0, b)
            dve.wait_ge(sem("early_loaded"), 16)
            nc.vector.tensor_copy(ident_bf[:, :], ident).then_inc(sem("ident_ready"), 1)
            two_parts(1)
            dve.wait_ge(sem("rows_loaded"), 16)

            def cubic(b):
                u, y = ff_u[b % 2], ff_y[b % 2]
                dve.wait_ge(sem("square_ready"), b + 1)
                then(nc.vector.tensor_scalar(y, y, 0.044715, 1.0, ALU.mult, ALU.add))
                nc.vector.tensor_tensor(y, y, u, ALU.mult).then_inc(sem("cubic_ready"), 1)
                dve.wait_ge(sem("tanh_ready"), b + 1)
                nc.vector.scalar_tensor_tensor(y, y, 1.0, u, ALU.add, ALU.mult).then_inc(sem("ffy_ready"), 1)

            def routing():
                s, biased, chosen, cw = (router[:, i] for i in range(4))
                dve.wait_ge(sem("rt_read_a"), 1)
                then(nc.vector.tensor_scalar(s, s, 0.5, 0.5, ALU.mult, ALU.add))
                then(nc.vector.tensor_tensor(biased, s, row("rb").unsqueeze(1).to_broadcast([P, NT, E]), ALU.add))
                other = biased.unsqueeze(2).to_broadcast([P, NT, E, E])
                mine = biased.unsqueeze(3).to_broadcast([P, NT, E, E])
                then(nc.vector.tensor_tensor(cmp_gt[:, :, :, :], other, mine, ALU.is_gt))
                then(nc.vector.tensor_tensor(cmp_eq[:, :, :, :], other, mine, ALU.is_equal))
                then(nc.vector.tensor_tensor(cmp_eq[:, :, :, :].rearrange("p t i j -> p t (i j)"),
                                             cmp_eq[:, :, :, :].rearrange("p t i j -> p t (i j)"),
                                             pk("before").unsqueeze(1).to_broadcast([P, NT, E * E]), ALU.mult))
                then(nc.vector.tensor_tensor(cmp_gt[:, :, :, :].rearrange("p t i j -> p (t i j)"),
                                             cmp_gt[:, :, :, :].rearrange("p t i j -> p (t i j)"),
                                             cmp_eq[:, :, :, :].rearrange("p t i j -> p (t i j)"), ALU.add))
                then(nc.vector.tensor_reduce(rank[:, :, :], cmp_gt[:, :, :, :], AX.X, ALU.add))
                then(nc.vector.tensor_scalar(chosen, rank[:, :, :], 1.5, None, ALU.is_lt))
                then(nc.vector.tensor_tensor(cw, s, chosen, ALU.mult))
                then(nc.vector.tensor_reduce(cw_sum[:, 0, :], cw, AX.X, ALU.add))
                then(nc.vector.tensor_scalar(cw_sum[:, 0, :], cw_sum[:, 0, :], 1e-9, None, ALU.add))
                then(nc.vector.reciprocal(cw_sum[:, 1, :], cw_sum[:, 0, :]))
                then(nc.vector.tensor_tensor(cw, cw, cw_sum[:, 1, :].unsqueeze(2).to_broadcast([P, NT, E]),
                                             ALU.mult))
                then(nc.vector.tensor_tensor(stay[:, :], cw[:, :, EM], cw[:, :, EM + 2], ALU.add))
                dve.wait_ge(sem("bias_added"), 4 * B)
                for t in range(NT):
                    ins = nc.vector.scalar_tensor_tensor(xs[2][:, t, :], xn[:, t, :], stay[:, t:t + 1],
                                                         xs[3][:, t, :], ALU.mult, ALU.add)
                then(ins)
                for t in range(NT):
                    ins = nc.vector.tensor_scalar(xs[0][:, t, :], xn[:, t, :], 0.0, cw[:, t, EM + 3:EM + 4],
                                                  ALU.max, ALU.mult)
                then(ins)
                then(nc.vector.tensor_tensor(xs[2][:, :, :].rearrange("p t d -> p (t d)"),
                                             xs[2][:, :, :].rearrange("p t d -> p (t d)"),
                                             xs[0][:, :, :].rearrange("p t d -> p (t d)"), ALU.add))
                then(nc.vector.tensor_scalar(cw[:, :, 0:EM], cw[:, :, 0:EM], 0.5, None, ALU.mult))
                dve.wait_ge(sem("xt3_read_a"), 2)
                dve.wait_ge(sem("o1_filled"), B * H // 2)
                then(nc.vector.tensor_scalar(conv, xt[:, :], pk("convw")[:, KC - 1:KC], None, ALU.mult))
                for k in range(KC - 1):
                    back = KC - 1 - k
                    to = conv.rearrange("p (b s) -> p b s", b=B)[:, :, back:]
                    of = xt[:, :].rearrange("p (b s) -> p b s", b=B)[:, :, 0:S - back]
                    ins = nc.vector.scalar_tensor_tensor(to, of, pk("convw")[:, k:k + 1], to, ALU.mult, ALU.add)
                    if k < KC - 2:
                        then(ins)
                ins.then_inc(sem("conv_ready"), 1)

            for kind, key, banks, readers in units:
                if "v" not in readers:
                    continue
                o = ready(dve, kind, *key)
                if kind == "v0":
                    half = key[0]
                    for t in range(4):
                        ins = nc.vector.tensor_tensor(
                            v0[:, half * 4 + t, :, 0:DK0],
                            bank(o, slice(t * P, (t + 1) * P)).rearrange("p (h d) -> p h d", h=H),
                            row("bv0").rearrange("p (h d) -> p h d", h=H), ALU.add)
                    ins.then_inc(sem("v0_read_v"), 1)
                    if half == 1:
                        two_parts(0)
                elif kind == "a0":
                    b, u = key
                    hp, qt = u // 2, u % 2
                    signal(nc.vector.tensor_reduce(neg_max[:, b % 2, qt, 2 * hp:2 * hp + 2],
                                                   bank(o).rearrange("p (j s) -> p j s", j=2), AX.X, ALU.max,
                                                   negate=True), kind)
                    if u == H - 1:
                        nm = neg_max[:, b % 2]
                        dve.wait_ge(sem("a0_read_v"), H * (b + 1))
                        if b:
                            dve.wait_ge(sem("t0_filled"), b)
                        then(nc.vector.tensor_copy(nm_part[:, :, 0:H], nm))
                        then(nc.vector.tensor_tensor(nm_rest[:, :, :], nm, nm_part[:, :, 0:H], ALU.subtract))
                        nc.vector.tensor_copy(nm_part[:, :, H:2 * H], nm_rest[:, :, :]).then_inc(
                            sem("nm_part_ready"), 1)
                elif kind == "t0":
                    b = key[0]
                    if b:
                        dve.wait_ge(sem("max0_stored"), 2 * 16 * b)
                    signal(nc.vector.tensor_copy(nmt0[:, :], bank(o, slice(0, P), slice(0, 2 * H)).bitcast(BF16)),
                           kind)
                elif kind == "d0":
                    b = key[0]
                    if b:
                        dve.wait_ge(sem("e0_filled"), 2 * b)
                    signal(nc.vector.reciprocal(rden0, bank(o, slice(0, S), slice(0, H))), kind)
                elif kind == "e0":
                    b, half = key
                    if b and half == 0:
                        dve.wait_ge(sem("w0_filled"), b)
                    cols = slice(half * 512, (half + 1) * 512)
                    dve.wait_ge(sem("o0_read_a"), 4 * b + 4)
                    signal(nc.vector.tensor_tensor(un0[:, cols], u0[b % 2][:, cols], bank(o), ALU.mult), kind)
                elif kind in ("w0", "w1"):
                    b, layer = key[0], 0 if kind == "w0" else 2
                    dve.wait_ge(sem("bias_added"), layer * B + b + 1)
                    signal(nc.vector.tensor_tensor(
                        xs[layer + 1][:, b * TB:(b + 1) * TB, :].rearrange("p t d -> p (t d)"), bank(o, slice(0, S)),
                        xb[layer][:, b * TB:(b + 1) * TB, :].rearrange("p t d -> p (t d)"), ALU.add), kind)
                    dve.wait_ge(sem(kind + "_read_v"), b + 1)
                    moments(layer + 1, b)
                    normalise(layer + 1, b)
                elif kind == "v1":
                    t, half = key
                    cols = slice(half * 512, (half + 1) * 512)
                    if t == 0 and half == 0:
                        dve.wait_ge(sem("o0_filled"), 4 * B)
                    signal(nc.vector.tensor_tensor(v1[:, t, cols], bank(o), row("bv1")[:, cols], ALU.add), kind)
                elif kind in ("k1", "q1"):
                    b, c = key
                    if kind == "k1" and b == 0 and c == 0:
                        dve.wait_ge(sem("s0_filled"), 8 * B)
                    if kind == "q1" and b == 0 and c == 0:
                        dve.wait_ge(sem("m2_filled"), 4)
                    if b >= 2:
                        dve.wait_ge(sem("s1_filled"), index["s1", (b - 2, 2 * c + 1)][0])
                    to = (kb if kind == "k1" else qa)[b % 2]
                    signal(nc.vector.tensor_scalar(to[0:DK1, 2 * c + 1, :], bank(o, slice(0, S), slice(DK1, P)),
                                                   pk("bk1" if kind == "k1" else "bq1")[DK1:P, c:c + 1], None,
                                                   ALU.add), kind)
                elif kind == "gc":
                    signal(nc.vector.tensor_scalar(gcol[:, :], bank(o, slice(0, B)), 1.0 / S, pk("gb2"), ALU.mult,
                                                   ALU.add), kind)
                    dve.wait_ge(sem("gc_read_v"), 1)
                    for b in range(B):
                        ins = nc.vector.tensor_scalar(gdiag[:, b, :], pk("delta"), gcol[:, b:b + 1], None, ALU.mult)
                    ins.then_inc(sem("gdiag_ready"), 1)
                    for b in range(B):
                        ins = nc.vector.tensor_scalar(gwide[:, b, :], ident, 0.0, gcol[:, b:b + 1], ALU.mult, ALU.add)
                    then(ins)
                    ins = nc.vector.tensor_scalar(gwide[:, :, :].rearrange("p b n -> p (b n)"),
                                                  gwide[:, :, :].rearrange("p b n -> p (b n)"), 2.0, None, ALU.mult)
                    then(ins)
                elif kind == "mb":
                    signal(nc.vector.tensor_tensor(mb1[:, :, :], bank(o, slice(0, FC * B)).rearrange(
                        "p (c b) -> p c b", c=FC), pk("b1").unsqueeze(2).to_broadcast([P, FC, B]), ALU.add), kind)
                elif kind == "m1":
                    k = key[0]
                    if k == 0:
                        dve.wait_ge(sem("o0_filled"), 4 * B)
                    signal(nc.vector.tensor_tensor(
                        mw1[:, :, k * P:(k + 1) * P].rearrange("p b (c j) -> p c b j", j=J),
                        bank(o).rearrange("p (c b j) -> p c b j", b=B, j=J),
                        pk("w1")[:, k * P:(k + 1) * P].rearrange("p (c j) -> p c j", j=J).unsqueeze(2).to_broadcast(
                            [P, 8, B, J]), ALU.add), kind)
                elif kind == "m2":
                    k = key[0]
                    signal(nc.vector.tensor_tensor(
                        mw2[:, k, :, :].rearrange("p b (j n) -> p n b j", n=8),
                        bank(o).rearrange("p (n b j) -> p n b j", b=B, j=J),
                        pk("w2")[:, k * D:(k + 1) * D].rearrange("p (j n) -> p n j", n=8).unsqueeze(2).to_broadcast(
                            [P, 8, B, J]), ALU.add), kind)
                    if k == 3:
                        cubic(0)
                elif kind == "y1":
                    b = key[0]
                    dve.wait_ge(sem("bias_added"), B + b + 1)
                    signal(nc.vector.scalar_tensor_tensor(
                        xs[2][:, b * TB:(b + 1) * TB, :].rearrange("p t d -> p (t d)"), bank(o, slice(0, S)), 0.5,
                        xb[1][:, b * TB:(b + 1) * TB, :].rearrange("p t d -> p (t d)"), ALU.mult, ALU.add), kind)
                    dve.wait_ge(sem("y1_read_v"), b + 1)
                    moments(2, b)
                    normalise(2, b)
                elif kind == "a1":
                    b, h, qt = key
                    if b >= 2 and h == 0 and qt == 0:
                        dve.wait_ge(sem("t1_filled"), b - 1)
                    signal(nc.vector.tensor_reduce(neg_max[:, b % 2, qt, h:h + 1], bank(o, slice(0, S + MEM)), AX.X,
                                                   ALU.max, negate=True), kind)
                elif kind == "t1":
                    b = key[0]
                    if b:
                        dve.wait_ge(sem("max1_stored"), 16 * b)
                    signal(nc.vector.tensor_copy(nmt1[:, :], bank(o, slice(0, S), slice(0, H))), kind)
                elif kind == "o1":
                    b, hp = key
                    if b == 0 and hp == 0:
                        dve.wait_ge(sem("y1_filled"), B)
                    if b >= 2 and hp == 0:
                        dve.wait_ge(sem("w1_filled"), b - 1)
                    rd = rden1[:, hp % 2, :]
                    then(nc.vector.reciprocal(rd, bank(o, slice(S, 2 * S))))
                    signal(nc.vector.tensor_tensor(ct1[b % 2][:, hp, :], bank(o, slice(0, S)), rd, ALU.mult), kind)
                elif kind == "gu":
                    t = key[0]
                    if t == 0:
                        routing()
                    gt, w = gu_t[t % 2], gu_w[t % 2]
                    dve.wait_ge(sem("gu_read_a"), t + 1)
                    then(nc.vector.scalar_tensor_tensor(w, gt, 1.0, bank(o, slice(0, 256)), ALU.add, ALU.mult))
                    if t >= 2:
                        dve.wait_ge(sem("ht_filled"), t - 1)
                    signal(nc.vector.tensor_tensor(w, w, bank(o, slice(256, 512)), ALU.mult), kind)
                    dve.wait_ge(sem("gu_read_v"), t + 1)
                    nc.vector.tensor_tensor(
                        hid[t % 2].rearrange("p (e i) -> p e i", e=EM), w.rearrange("p (e i) -> p e i", e=EM),
                        router[:, 3, t, 0:EM].unsqueeze(2).to_broadcast([P, EM, EI]), ALU.mult).then_inc(
                            sem("hid_ready"), 1)
                elif kind == "f3":
                    t = key[0]
                    y = xs[1][:, t, :]
                    signal(nc.vector.tensor_tensor(y, bank(o, slice(0, D)), xs[2][:, t, :], ALU.add), kind)
                if kind == "y1" and key[0] + 2 < B:
                    cubic(key[0] + 2)
                if kind == "m2" and key[0] == 3:
                    cubic(1)


def _layout(inp):
    g = {k: np.ascontiguousarray(np.asarray(v)) for k, v in inp.items()}

    def cols(v, n=P):
        return np.ascontiguousarray(v.reshape(-1, n).T)

    f_order = np.arange(F).reshape(J, F // J).T.reshape(-1)
    pack = {}
    pack["wk0"], pack["wv0"], pack["wq0"] = (g[f"L0_xattn_W{c}"].T for c in "kvq")
    pack["ident"] = np.eye(P, dtype=np.float32)
    pack["bk0"], pack["bq0"] = cols(g["L0_xattn_bk"]), cols(g["L0_xattn_bq"])
    pack["gb1"] = cols(g["L0_ffn_gate_b1"])
    pack["gb2"] = np.repeat(g["L0_ffn_gate_b2"], J)[:, None]
    pack["b1"] = cols(g["L0_ffn_b1"][f_order])
    pack["bq1"], pack["bk1"] = cols(g["L1_xattn_wq_b"]), cols(g["L1_xattn_wk_b"])
    pack["convw"] = g["L1_ffn_conv_w"][:, 0, :].T
    wo = g["L0_xattn_Wo"].T.reshape(4, 4, DK0, D)
    spread = np.zeros((P, 4, D), np.float32)
    for j in range(4):
        spread[32 * j:32 * j + DK0] = wo[:, j].transpose(1, 0, 2)
    pack["wo0"] = spread.reshape(P, 4 * D)
    pick = np.zeros((P, 4, H), np.float32)
    put = np.zeros((P, 4, P), np.float32)
    for q in range(4):
        for j in range(4):
            pick[32 * j + DK0, q, 4 * q + j] = 1
            put[4 * q + j, q, 32 * j:32 * j + 32] = 1
    pack["den_pick"], pack["den_spread"] = pick.reshape(P, -1), put.reshape(P, -1)
    pack["gw1"] = g["L0_ffn_gate_w1"].T
    pack["gw2"] = np.repeat(g["L0_ffn_gate_w2"].T, J, axis=1)
    pack["delta"] = np.tile(np.eye(J, dtype=np.float32), (E, 1))
    pack["w1"] = g["L0_ffn_W1"].T[:, f_order]
    pack["w2"] = g["L0_ffn_W2"].T[f_order].reshape(FC, P, D).transpose(1, 0, 2).reshape(P, FC * D)
    tb1, tb2 = np.zeros((P, F), np.float32), np.zeros((P, D), np.float32)
    tb1[::J], tb2[::J] = g["L0_ffn_Tb1"][:, f_order], g["L0_ffn_Tb2"]
    pack["tb1"], pack["tb2"] = tb1, tb2
    wg, wu = (g[f"L1_ffn_W{c}"].transpose(1, 0, 2).reshape(D, EM * EI) for c in "gu")
    pack["wgu"] = np.concatenate([wg, wu], 1)
    pack["wd"] = g["L1_ffn_Wd"].reshape(2, P, D).transpose(1, 0, 2).reshape(P, 2 * D)
    pack["wr"] = g["L1_ffn_Wr"]
    pack["before"] = np.tile(np.tril(np.ones((E, E), np.float32), -1).reshape(1, -1), (P, 1))
    packed = {}
    for name in ("early", "late"):
        packed[name] = np.concatenate([pack[k] for k, v in PACK.items() if v[0] == name], 1)
    rows = {"bv0": g["L0_xattn_bv"], "bo0": g["L0_xattn_bo"], "b2": g["L0_ffn_b2"], "bo1": g["L1_xattn_wo_b"],
            "convb": g["L1_ffn_conv_b"], "rb": g["L1_ffn_router_bias"], "bv1": g["L1_xattn_wv_b"]}
    tw2 = g["L0_ffn_TW2"][:, :, f_order].reshape(P, 8 * F)
    return {
        "x": g["x"].reshape(T, D),
        "ctx_t": g["ctx_1024"].reshape(T, D).T,
        "early": packed["early"], "late": packed["late"],
        "rows": np.concatenate([rows[k] for k in ROWS])[None, :],
        "tw1": g["L0_ffn_TW1"].reshape(P, 32 * D),
        "tw2": tw2,
        "wq1": g["L1_xattn_wq_w"], "wk1": g["L1_xattn_wk_w"], "wv1": g["L1_xattn_wv_w"],
        "wo1": g["L1_xattn_wo_w"].reshape(H // 2, P, D).transpose(1, 0, 2).reshape(P, -1),
        "mem_k": g["L1_xattn_mk"][0].reshape(MEM, H, DK1).transpose(2, 1, 0),
        "mem_v": g["L1_xattn_mv"][0],
    }


def kernel(**inputs):
    import concourse.bacc as _bacc
    from concourse.bass_utils import run_bass_kernel_spmd as _run

    nc = _bacc.Bacc("TRN2", target_bir_lowering=False, num_devices=1)
    arrays, args = {}, []
    for name, a in _layout(inputs).items():
        a = np.ascontiguousarray(a)
        arrays[f"in_{name}"] = a
        args.append(nc.dram_tensor(f"in_{name}", a.shape, F32, kind="ExternalInput").ap())
    args.append(nc.dram_tensor("out_x", (T, D), F32, kind="ExternalOutput").ap())
    xattn_ffn_kernel(nc, *args)
    r = _run(nc, [arrays], core_ids=[0])
    return r.results[0]["out_x"].reshape(B, S, D)
```

```python
from contextlib import ExitStack

import numpy as np

import concourse.bass as bass
from concourse import mybir

F32 = mybir.dt.float32
BF16 = mybir.dt.bfloat16
ALU = mybir.AluOpType
ACT = mybir.ActivationFunctionType
AX = mybir.AxisListType

P = 128
B, S, D = 4, 256, 128
T = B * S
NT = T // P
TB = S // P
H = 16
DK0 = D // H
DK1 = 64
MEM = 128
KT1 = (S + MEM) // P
E, F = 8, 512
J = P // E
FC = F // P
EM, EI = 4, 64
KC = 4
EPS = 1e-5
BF16_ONES = float(np.array(0x3F803F80, np.uint32).view(np.float32))
CUBIC = 0.044715

QPART = ("h", "m", "h", "m", "h", "l")
KPART = ("m", "m", "h", "h", "l", "h")
Q_SLOT, K_SLOT = "hml", "lmh"
ST0 = len(QPART) * DK0
ST0X = ST0 + 2

PACK = {}


def _pack(name, *widths):
    at = 0
    for key, w in widths:
        PACK[key] = (name, at, w)
        at += w
    return at


N_EARLY = _pack("early", ("wk0", D), ("wv0", D), ("wq0", D), ("ident", P), ("bk0", 1), ("bq0", 1),
                ("gb1", 1), ("gb2", 1), ("b1", FC), ("bq1", H // 2), ("bk1", H // 2), ("convw", KC))
N_LATE = _pack("late", ("wo0", 4 * D), ("den_pick", 4 * H), ("den_spread", 4 * P), ("gw1", D), ("gw2", P),
               ("delta", J), ("w1", F), ("w2", FC * D), ("tb1", F), ("tb2", D), ("wgu", 2 * EM * EI),
               ("wd", 2 * D), ("wr", E), ("before", E * E))
ROWS = {}
_at = 0
for _k, _w in (("bv0", D), ("bo0", D), ("b2", D), ("bo1", D), ("convb", D), ("rb", E), ("bv1", H * DK1)):
    ROWS[_k] = (_at, _w)
    _at += _w
N_ROWS = _at


def schedule():
    units = []
    ring = [0]
    everything, wide, narrow0, narrow1 = tuple(range(8)), (0, 1, 2, 3, 4, 5), (0, 1, 7), (0, 1)

    def small(kind, key, readers, banks):
        units.append((kind, key, (banks[ring[0] % len(banks)],), readers))
        ring[0] += 1

    def step(kind, key, engines="v"):
        units.append((kind, key, (), engines))

    step("norm", (0, 0))
    small("k0", (0,), "a", everything)
    step("split", (1, 0))
    for b in range(1, B):
        step("norm", (0, b))
    small("xt0", (0,), "a", everything)
    small("q0", (0,), "a", everything)
    step("split", (0, 0))
    for b in range(1, B):
        small("k0", (b,), "a", everything)
    step("split", (1, 1))
    for b in range(1, B):
        small("xt0", (b,), "a", everything)
        small("q0", (b,), "a", everything)
    step("split", (0, 1))
    for half in range(2):
        small("v0", (half,), "v", everything)

    for u in range(H):
        small("a0", (0, u), "v", everything)
    step("parts0", (0,))
    small("t0", (0,), "v", everything)
    for b in range(B):
        at = 0
        for hp, n in enumerate((3, 3, 2, 2, 2, 2, 1, 1)):
            units.append(("s0", (b, hp), (2 + 2 * (hp % 2), 3 + 2 * (hp % 2)), "a"))
            if b + 1 < B:
                for u in range(at, at + n):
                    small("a0", (b + 1, u), "v", narrow0)
                at += n
            if hp == 0 and b:
                small("w0", (b - 1,), "v", narrow0)
            if hp == 1 and b:
                step("norm", (1, b - 1))
            if hp == 3 and b:
                small("xt1", (b - 1,), "a", narrow0)
            if hp == 5 and b:
                small("g1", (b - 1,), "a", narrow0)
            if hp % 2 == 0 and hp:
                units.append(("o0", (b, hp // 2 - 1), (6,), "a"))
        if b + 2 < B:
            step("stacks", (b + 2,), "a")
        if b + 1 < B:
            step("parts0", (b + 1,))
            small("t0", (b + 1,), "v", narrow0)
        units.append(("o0", (b, H // 4 - 1), (6,), "a"))
        if b + 1 < B:
            small("d0", (b,), "v", narrow0)
            for g in range(2):
                small("e0", (b, g), "v", narrow0)

    small("d0", (B - 1,), "v", wide)
    small("v1", (4, 0), "v", wide)
    small("v1", (4, 1), "v", wide)
    small("v1", (5, 0), "v", wide)
    for g in range(2):
        small("e0", (B - 1, g), "v", wide)
    small("v1", (5, 1), "v", wide)
    small("w0", (B - 1,), "v", wide)
    for t in (6, 7):
        for half in range(2):
            small("v1", (t, half), "v", wide)
        if t == 6:
            step("norm", (1, B - 1))
    small("xt1", (B - 1,), "a", wide)
    for c in range(2):
        small("k1", (0, c), "av", wide)
    small("g1", (B - 1,), "a", wide)
    for c in range(2, 5):
        small("k1", (0, c), "av", wide)
    small("gc", (), "v", wide)
    for c in range(5, H // 2):
        small("k1", (0, c), "av", wide)
    small("mb", (), "v", wide)

    for k in range(4):
        small("m1", (k,), "v", wide)

    def u1(b):
        for c in range(2):
            small("u1", (b, c), "a", wide)
        step("cubic", (b,))

    u1(0)
    small("m2", (0,), "v", wide)
    step("tanh", (0,), "a")
    u1(1)
    small("m2", (1,), "v", wide)
    step("tanh", (1,), "a")
    step("gate", (0,))
    small("m2", (2,), "v", wide)
    step("gate", (1,))
    small("m2", (3,), "v", wide)
    small("y1", (0,), "v", wide)
    u1(2)
    step("tanh", (2,), "a")
    small("v1", (0, 0), "v", wide)
    step("norm", (2, 0))
    small("y1", (1,), "v", wide)
    small("v1", (0, 1), "v", wide)
    small("xt2", (0,), "a", wide)
    step("norm", (2, 1))
    fillers = [
        [lambda: u1(3), lambda: step("tanh", (3,), "a")],
        [lambda: small("v1", (1, 0), "v", wide), lambda: step("gate", (2,))],
        [lambda: small("y1", (2,), "v", wide), lambda: step("gate", (3,))],
        [lambda: small("v1", (1, 1), "v", wide), lambda: step("norm", (2, 2))],
        [lambda: small("y1", (3,), "v", wide), lambda: small("xt2", (1,), "a", wide)],
        [lambda: small("v1", (2, 0), "v", wide), lambda: step("norm", (2, 3)),
         lambda: small("v1", (2, 1), "v", wide)],
        [lambda: small("v1", (3, 0), "v", wide), lambda: small("xt2", (2,), "a", wide)],
        [lambda: small("v1", (3, 1), "v", wide), lambda: small("xt2", (3,), "a", wide)],
    ]
    for c in range(H // 2):
        small("q1", (0, c), "av", wide)
        for f in fillers[c]:
            f()
        for h in (2 * c, 2 * c + 1):
            for qt in range(TB):
                small("a1", (0, h, qt), "v", wide)
    small("q1", (1, 0), "av", wide)
    small("k1", (1, 0), "av", wide)
    small("t1", (0,), "v", wide)

    def ahead(b):
        todo = []
        for c in range(H // 2):
            if c + 1 < H // 2:
                todo += [("q1", (b, c + 1), "av"), ("k1", (b, c + 1), "av")]
            todo += [("a1", (b, h, qt), "v") for h in (2 * c, 2 * c + 1) for qt in range(TB)]
        n = H - 2
        return [todo[len(todo) * i // n:len(todo) * (i + 1) // n] for i in range(n)] + [[], []]

    def last_layer(b):
        return [[("xt3", (b,), "a"), ("rt", (b,), "a"), ("route", (b,), "")], [("gu", (2 * b,), "av")],
                [("gu", (2 * b + 1,), "av")], [("ht", (2 * b,), "a"), ("conv", (b,), "")],
                [("ht", (2 * b + 1,), "a"), ("f3", (2 * b,), "v")], [("f3", (2 * b + 1,), "v")]]

    def place(todo, banks):
        for kind, key, readers in todo:
            if readers:
                small(kind, key, readers, banks)
            else:
                step(kind, key)

    for b in range(B):
        beside = ahead(b + 1) if b + 1 < B else [[] for _ in range(H)]
        if b == B - 1:
            for i in range(B - 1):
                for n, todo in enumerate(last_layer(i)):
                    beside[min(4 * i + n, H - 1)] += todo
        for hp in range(H // 2):
            for h in (2 * hp, 2 * hp + 1):
                units.append(("s1", (b, h), (2 + 2 * (h % 2), 3 + 2 * (h % 2)), "a"))
                place(beside[h], narrow1)
            if hp == H // 2 - 1 and b + 1 < B:
                small("t1", (b + 1,), "v", narrow1)
            if hp >= 2:
                step("head_out", (b, hp - 2))
            if hp:
                units.append(("o1", (b, hp - 1), (6 + (hp - 1) % 2,), ""))
            if hp == 1 and b:
                small("w1", (b - 1,), "v", narrow1)
            if hp == 2 and b:
                step("norm", (3, b - 1))
        step("head_out", (b, H // 2 - 2))
        units.append(("o1", (b, H // 2 - 1), (6 + (H // 2 - 1) % 2,), ""))
        if b + 2 < B:
            small("q1", (b + 2, 0), "av", narrow1)
            small("k1", (b + 2, 0), "av", narrow1)
        step("head_out", (b, H // 2 - 1))
    small("w1", (B - 1,), "v", wide)
    step("norm", (3, B - 1))
    for todo in last_layer(B - 1):
        place(todo, wide)
    return units


def xattn_ffn_kernel(nc, x, ctx_t, early, late, rows, tw1, tw2, wq1, wk1, wv1, wo1, mem_k, mem_v, out):
    units = schedule()
    index, count, reads = {}, {}, {}
    last_of_bank, before = {}, []
    for n, (kind, key, banks, readers) in enumerate(units):
        count[kind] = count.get(kind, 0) + 1
        index[kind, key] = (count[kind], banks)
        before.append([last_of_bank.get(k) for k in banks])
        for k in banks:
            last_of_bank[k] = (kind, count[kind], readers or "v")

    with ExitStack() as ctx:
        def sb(name, shape, dt=F32):
            return ctx.enter_context(nc.sbuf_tensor(name, shape, dt))

        sems = {}

        def sem(name):
            if name not in sems:
                sems[name] = ctx.enter_context(nc.semaphore(name))
            return sems[name]

        psum = ctx.enter_context(nc.psum_tensor("psum", [P, 8, 512], F32))

        r_q = sb("r_q", [P, 2 * H * S])
        r_k = sb("r_k", [P, 2 * H * S])
        r_p = sb("r_p", [P, 4096])
        r_w = sb("r_w", [P, 6144])
        r_o = sb("r_o", [P, 4096])
        r_v = sb("r_v", [P, NT * H * DK1])

        tw_sb = [r_q[:, i * 4096:(i + 1) * 4096] for i in (1, 0)]
        qa = [r_q[:, i * H * S:(i + 1) * H * S].rearrange("p (h s) -> p h s", h=H) for i in range(2)]
        kb = [r_k[:, i * H * S:(i + 1) * H * S].rearrange("p (h s) -> p h s", h=H) for i in range(2)]
        half_k = H * S // 2
        stack = [r_k[:, i * half_k:(i + 1) * half_k].bitcast(BF16).rearrange("p (h s) -> p h s", h=H)
                 for i in range(4)]
        q_stack, k_stack = stack[:2], stack[2:]
        p0 = r_p[:, :].rearrange("p (n j k s) -> p n j k s", n=4, j=2, k=2)
        p1 = r_p[:, 0:4 * KT1 * S].rearrange("p (n k s) -> p n k s", n=4, k=KT1)
        mw1 = r_p[:, 0:B * F].rearrange("p (b f) -> p b f", b=B)
        mw2 = r_p[:, B * F:2 * B * F].rearrange("p (c b h) -> p c b h", c=FC, b=B)
        qk_f = [r_w[:, i * T:(i + 1) * T] for i in range(2)]
        rest = r_w[:, 2 * T:3 * T]
        part = [[r_w[:, 3 * T + (3 * i + n) * T // 2:3 * T + (3 * i + n + 1) * T // 2].bitcast(BF16)
                 for n in range(3)] for i in range(2)]
        wq1_sb, wk1_sb, wv1_sb, wo1_sb = (r_w[:, i * 1024:(i + 1) * 1024] for i in range(4))
        mem_k_sb = r_w[:, 4096:4096 + H * MEM].rearrange("p (h m) -> p h m", h=H)
        u0 = [r_o[:, i * 1024:(i + 1) * 1024] for i in range(2)]
        un0 = r_o[:, 2048:3072]
        ct1 = [r_o[:, i * 2048:(i + 1) * 2048].rearrange("p (c s) -> p c s", c=H // 2) for i in range(2)]
        ff_u = [r_o[:, b * 1024:(b + 1) * 1024] for b in range(B)]
        ff_y = [r_q[:, 4096 + b * 1024:4096 + (b + 1) * 1024] for b in range(B)]
        mem_v_sb = r_p[:, 4 * KT1 * S:4 * KT1 * S + H * DK1]
        v0 = r_v[:, 0:NT * H * 32].rearrange("p (t h e) -> p t h e", t=NT, h=H)
        v1 = r_v[:, :].rearrange("p (t n) -> p t n", t=NT)

        hid = [r_q[:, i * 256:(i + 1) * 256] for i in range(2)]
        hidt = [r_q[:, 512 + i * 256:512 + (i + 1) * 256] for i in range(2)]
        gu_t = [r_q[:, 1024 + i * 256:1024 + (i + 1) * 256] for i in range(2)]
        gu_w = [r_q[:, 1536 + i * 256:1536 + (i + 1) * 256] for i in range(2)]
        conv = r_q[:, 2048:2048 + T]
        router = r_q[:, 3072:3072 + 4 * NT * E].rearrange("p (n t e) -> p n t e", n=4, t=NT)
        cmp_gt, cmp_eq = (r_q[:, 3328 + i * TB * E * E:3328 + (i + 1) * TB * E * E].rearrange(
            "p (t i j) -> p t i j", t=TB, i=E) for i in range(2))

        ctx_sb = sb("ctx_sb", [P, T])
        early_sb = sb("early_sb", [P, N_EARLY])
        late_sb = sb("late_sb", [P, N_LATE])
        rows_sb = sb("rows_sb", [P, N_ROWS])

        def pk(key, p=P):
            name, at, w = PACK[key]
            return (early_sb if name == "early" else late_sb)[0:p, at:at + w]

        xs = [sb("x0_sb", [P, NT, D]), sb("x1_sb", [P, NT, D]), sb("x2_sb", [P, NT, D])]
        xs.append(xs[0])
        xb = xs
        xn = sb("xn", [P, NT, D])
        xt = sb("xt", [P, T])
        stats = sb("stats", [P, NT, 6])
        mv = sb("mv", [P, NT, 2])
        veps = sb("veps", [P, NT])
        rstd = sb("rstd", [P, NT])
        minus_half = sb("minus_half", [P, NT])
        neg_max = sb("neg_max", [P, 2, TB, H])
        nm_rest = sb("nm_rest", [P, TB, H])
        nm_part = sb("nm_part", [P, TB, 2 * H], BF16)
        ident_bf = sb("ident_bf", [P, P], BF16)
        nmt0 = sb("nmt0", [2 * H, S], BF16)
        nmt1 = sb("nmt1", [H, S])
        rden1 = sb("rden1", [P, 2, S])
        rden0 = rden1[0:H, 0, :]
        ones64 = sb("ones64", [P, DK1])
        hsum = sb("hsum", [P, B])
        gate_relu = rden1[:, 1, :]
        gcol = sb("gcol", [P, B])
        gdiag = sb("gdiag", [P, B, J])
        gwide = sb("gwide", [P, B, P])
        mb1 = sb("mb1", [P, FC, B])
        mb1_root = sb("mb1_root", [P, FC, B])
        key_sum = late_sb[:, PACK["w1"][1]:PACK["w1"][1] + 4 * S].rearrange("p (n j s) -> p n j s", n=2, j=2)
        rank = sb("rank", [P, NT, E])
        cw_sum = sb("cw_sum", [P, 2, NT])
        stay = sb("stay", [P, NT])

        def row(key):
            at, w = ROWS[key]
            return rows_sb[:, at:at + w]

        ident = pk("ident")
        scratch = nc.dram_tensor("parts_dram", [2, B, 3, DK0, H, S], BF16).ap()

        def ready(eng, kind, *key):
            n, banks = index[kind, key]
            eng.wait_ge(sem(kind + "_filled"), n)
            return banks[0]

        def bank(n, cols=slice(0, 512), parts_=slice(0, P)):
            return psum[parts_, n, cols]

        x_tiles = x.rearrange("(t p) d -> p t d", p=P)
        out_tiles = out.rearrange("(t p) d -> p t d", p=P)

        def load_k_stack(queue, b):
            to, of = k_stack[b % 2], scratch[1, b].rearrange("n d h s -> n d (h s)")
            loaded = sem(f"stack_loaded{b % 2}")
            for at, n in ((0, 1), (2, 2)):
                queue.dma_start(to[at * DK0:(at + 2) * DK0].rearrange("p h s -> p (h s)"),
                                of[n].unsqueeze(0).to_broadcast([2, DK0, H * S])).then_inc(loaded, 16)
            queue.dma_start(to[4 * DK0:ST0].rearrange("p h s -> p (h s)"), of[0::2]).then_inc(loaded, 16)

        def load_q_stack(queue, b):
            to, of = q_stack[b % 2], scratch[0, b].rearrange("n d h s -> n d (h s)")
            loaded = sem(f"stack_loaded{b % 2}")
            queue.dma_start(to[0:4 * DK0].rearrange("p h s -> p (h s)"),
                            of[0:2].rearrange("n d c -> (n d) c").unsqueeze(0).to_broadcast(
                                [2, 2 * DK0, H * S])).then_inc(loaded, 16)
            queue.dma_start(to[4 * DK0:ST0].rearrange("p h s -> p (h s)"), of[0::2]).then_inc(loaded, 16)

        block = ctx.enter_context(nc.Block())

        @block.sync
        def _(sp):
            sp.dma_start(ctx_sb[:, :], ctx_t).then_inc(sem("ctx_loaded"), 16)
            sp.dma_start(early_sb[:, :], early).then_inc(sem("early_loaded"), 16)
            sp.dma_start(xs[0][:, :, :], x_tiles).then_inc(sem("x_loaded"), 16)
            sp.dma_start(rows_sb[:, :], rows.broadcast_to([P, N_ROWS])).then_inc(sem("rows_loaded"), 16)
            sp.dma_start(late_sb[:, :], late).then_inc(sem("late_loaded"), 16)

            def store_parts(chunk, b):
                for i, slots in ((1, K_SLOT), (0, Q_SLOT)):
                    for n, name in enumerate("hml"):
                        if b < 2:
                            sp.wait_ge(sem("part_ready"), 6 * chunk + 3 * (1 - i) + n + 1)
                        sp.dma_start(scratch[i, b, slots.index(name)].rearrange("d h s -> h d s"),
                                     part[i][n][:, b * S:(b + 1) * S]).then_inc(sem("qk"[i] + "_stored"), 16)

            store_parts(0, 0)
            sp.wait_ge(sem("k_stack_cleared"), 1)
            sp.wait_ge(sem("k_stored"), 3 * 16)
            load_k_stack(sp, 0)
            sp.wait_ge(sem("q_stack_cleared"), 1)
            sp.wait_ge(sem("q_stored"), 3 * 16)
            load_q_stack(sp, 0)
            for b in range(1, B):
                store_parts(1, b)
                if b == 1:
                    sp.wait_ge(sem("k_stack_cleared"), 2)
                    sp.wait_ge(sem("k_stored"), 2 * 3 * 16)
                    load_k_stack(sp, 1)
                    sp.wait_ge(sem("q_stored"), 2 * 3 * 16)
                    load_q_stack(sp, 1)
            sp.wait_ge(sem("k_stored"), B * 3 * 16)
            sp.wait_ge(sem("q_stored"), B * 3 * 16)
            weights = (((tw_sb[0], tw1, "tw_loaded"), (wv1_sb, wv1, "w1_loaded")),
                       ((tw_sb[1], tw2, "tw_loaded"), (wk1_sb, wk1, "w1_loaded")),
                       ((wq1_sb, wq1, "w1_loaded"), (wo1_sb, wo1, "w1_loaded"), (mem_k_sb[0:DK1], mem_k, "w1_loaded")))
            for b in range(B):
                sp.wait_ge(sem("t0_read_v"), b + 1)
                for n in range(2):
                    sp.dma_start(q_stack[b % 2][ST0 + n:ST0 + n + 1],
                                 nmt0[n * H:(n + 1) * H, :]).then_inc(sem("max0_stored"), 16)
                for to, of, loaded in weights[b] if b < 3 else ():
                    sp.dma_start(to, of).then_inc(sem(loaded), 16)
            sp.wait_ge(sem("y1_filled"), B)
            sp.dma_start(mem_v_sb, mem_v).then_inc(sem("memv_loaded"), 16)
            for b in range(B):
                sp.wait_ge(sem("t1_read_v"), b + 1)
                sp.dma_start(qa[b % 2][DK1:DK1 + 1], nmt1[:, :]).then_inc(sem("max1_stored"), 16)
            for t in range(NT):
                sp.wait_ge(sem("f3_read_v"), t + 1)
                sp.dma_start(out_tiles[:, t, :], xs[1][:, t, :]).then_inc(sem("out_stored"), 16)
            sp.wait_ge(sem("out_stored"), 16 * NT)

        @block.tensor
        def _(pe):
            def matmul(o, w, m, start=True, stop=True):
                return nc.tensor.matmul(o, w, m, start=start, stop=stop, skip_group_check=True)

            def k0(o, b):
                if b == 0:
                    pe.wait_ge(sem("ctx_loaded"), 16)
                    pe.wait_ge(sem("early_loaded"), 16)
                return matmul(bank(o, slice(0, S)), pk("wk0"), ctx_sb[:, b * S:(b + 1) * S])

            def v0_(o, half):
                for t in range(4):
                    at = half * 512 + t * P
                    mm = matmul(bank(o, slice(t * P, (t + 1) * P)), ctx_sb[:, at:at + P], pk("wv0"))
                return mm

            def transposes(layer, o, b):
                pe.wait_ge(sem("xn_ready"), layer * B + b + 1)
                for t in range(TB):
                    mm = nc.tensor.transpose(bank(o, slice(t * P, (t + 1) * P)), xn[:, b * TB + t, :], ident)
                return mm

            def q0(o, b):
                pe.wait_ge(sem("xt0_read_a"), b + 1)
                return matmul(bank(o, slice(0, S)), pk("wq0"), xt[:, b * S:(b + 1) * S])

            def a0(o, b, u):
                if u == 0:
                    pe.wait_ge(sem(f"stack_loaded{b % 2}"), 5 * 16 * (b // 2 + 1))
                hp, qt = u // 2, u % 2
                for j in range(2):
                    h = 2 * hp + j
                    mm = matmul(bank(o, slice(j * S, (j + 1) * S)),
                                q_stack[b % 2][0:ST0, h, qt * P:(qt + 1) * P], k_stack[b % 2][0:ST0, h, :])
                return mm

            def t0(o, b):
                pe.wait_ge(sem("nm_part_ready"), b + 1)
                pe.wait_ge(sem("ident_ready"), 1)
                for qt in range(TB):
                    mm = nc.tensor.transpose(bank(o, slice(0, P), slice(0, 2 * H)).bitcast(BF16)[:, qt * P:(qt + 1) * P],
                                             nm_part[:, qt, :], ident_bf[:, :])
                return mm

            def s0(o, b, hp):
                if hp == 0:
                    pe.wait_ge(sem("max0_stored"), 2 * 16 * (b + 1))
                for j in range(2):
                    h = 2 * hp + j
                    for kt in range(TB):
                        mm = matmul(bank(o + j, slice(kt * S, (kt + 1) * S)),
                                    k_stack[b % 2][:, h, kt * P:(kt + 1) * P], q_stack[b % 2][:, h, :])
                return mm

            def o0(o, b, g):
                if b == 0 and g == 0:
                    pe.wait_ge(sem("v0_read_v"), 2)
                pe.wait_ge(sem("s0_read_a"), 8 * b + 2 * g + 2)
                for kt in range(TB):
                    for j in range(4):
                        pair = 8 * b + 2 * g + j // 2
                        mm = matmul(bank(o, slice(0, S), slice(32 * j, 32 * j + 32)),
                                    v0[:, b * TB + kt, 4 * g + j, :], p0[:, pair % 4, j % 2, kt, :],
                                    start=(kt == 0), stop=(kt == TB - 1))
                return mm

            def d0(o, b):
                if b == 0:
                    pe.wait_ge(sem("late_loaded"), 16)
                pe.wait_ge(sem("o0_read_a"), 4 * b + 4)
                for g in range(4):
                    mm = matmul(bank(o, slice(0, S), slice(0, H)), pk("den_pick")[:, g * H:(g + 1) * H],
                                u0[b % 2][:, g * S:(g + 1) * S], start=(g == 0), stop=(g == 3))
                return mm

            def e0(o, b, half):
                pe.wait_ge(sem("d0_read_v"), b + 1)
                for j in range(2):
                    g = 2 * half + j
                    mm = matmul(bank(o, slice(j * S, (j + 1) * S)), pk("den_spread", H)[:, g * P:(g + 1) * P],
                                rden0)
                return mm

            def w0(o, b):
                pe.wait_ge(sem("e0_read_v"), 2 * b + 2)
                for t in range(TB):
                    for g in range(4):
                        mm = matmul(bank(o, slice(t * P, (t + 1) * P)),
                                    un0[:, g * S + t * P:g * S + (t + 1) * P], pk("wo0")[:, g * D:(g + 1) * D],
                                    start=(g == 0), stop=(g == 3))
                return mm

            def v1_(o, t, half):
                pe.wait_ge(sem("w1_loaded"), 5 * 16)
                return matmul(bank(o), ctx_sb[:, t * P:(t + 1) * P], wv1_sb[:, half * 512:(half + 1) * 512])

            def k1(o, b, c):
                return matmul(bank(o, slice(0, S)), wk1_sb[:, c * P:(c + 1) * P], ctx_sb[:, b * S:(b + 1) * S])

            def g1(o, b):
                pe.wait_ge(sem("xt1_read_a"), b + 1)
                return matmul(bank(o, slice(0, S)), pk("gw1"), xt[:, b * S:(b + 1) * S])

            def gc(o):
                pe.wait_ge(sem("g1_read_a"), B)
                return matmul(bank(o, slice(0, B)), pk("gw2"), hsum[:, :])

            def mb(o):
                pe.wait_ge(sem("gc_read_v"), 1)
                for c in range(FC):
                    mm = matmul(bank(o, slice(c * B, (c + 1) * B)), pk("tb1")[:, c * P:(c + 1) * P], gcol[:, :])
                return mm

            def merge(i, o, k):
                if i == 0 and k == 0:
                    pe.wait_ge(sem("tw_loaded"), 2 * 16)
                    pe.wait_ge(sem("gdiag_ready"), 1)
                for n in range(8):
                    at = (k * 8 + n) * P if i == 0 else (n * FC + k) * P
                    mm = matmul(bank(o, slice(n * B * J, (n + 1) * B * J)), tw_sb[i][:, at:at + P],
                                gdiag[:, :, :].rearrange("p b j -> p (b j)"))
                return mm

            def u1(o, b, c2):
                if b == 0 and c2 == 0:
                    pe.wait_ge(sem("m1_read_v"), 4)
                for j in range(2):
                    c = 2 * c2 + j
                    mm = matmul(bank(o, slice(j * S, (j + 1) * S)), mw1[:, b, c * P:(c + 1) * P],
                                xt[:, b * S:(b + 1) * S])
                return mm

            def y1(o, b):
                if b == 0:
                    pe.wait_ge(sem("m2_read_v"), 4)
                pe.wait_ge(sem("ffy_ready"), b + 1)
                for t in range(TB):
                    for c in range(FC):
                        matmul(bank(o, slice(t * P, (t + 1) * P)), ff_y[b][:, c * S + t * P:c * S + (t + 1) * P],
                               mw2[:, c, b, :], start=(c == 0), stop=False)
                    mm = matmul(bank(o, slice(t * P, (t + 1) * P)), gwide[:, b, :], pk("tb2"), start=False)
                return mm

            def q1(o, b, c):
                pe.wait_ge(sem("xt2_read_a"), b + 1)
                return matmul(bank(o, slice(0, S)), wq1_sb[:, c * P:(c + 1) * P], xt[:, b * S:(b + 1) * S])

            def tops(ap):
                return ap.bitcast(BF16)[:, 1::2]

            def a1(o, b, h, qt):
                qn, kn = index["q1", (b, h // 2)][0], index["k1", (b, h // 2)][0]
                for who in ("a" if h % 2 == 0 else "v"):
                    pe.wait_ge(sem("q1_read_" + who), qn)
                    pe.wait_ge(sem("k1_read_" + who), kn)
                w = tops(qa[b % 2][0:DK1, h, qt * P:(qt + 1) * P])
                matmul(bank(o, slice(0, S)), w, tops(kb[b % 2][0:DK1, h, :]))
                return matmul(bank(o, slice(S, S + MEM)), w, tops(mem_k_sb[0:DK1, h, :]))

            def t1(o, b):
                pe.wait_ge(sem("a1_read_v"), H * TB * (b + 1))
                for qt in range(TB):
                    mm = nc.tensor.transpose(bank(o, slice(qt * P, (qt + 1) * P), slice(0, H)),
                                             neg_max[:, b % 2, qt, :], ident)
                return mm

            def s1(o, b, h):
                if h == 0:
                    pe.wait_ge(sem("max1_stored"), 16 * (b + 1))
                    pe.wait_ge(sem("kb_ones"), 2)
                for kt in range(KT1):
                    w = kb[b % 2][:, h, kt * P:(kt + 1) * P] if kt < TB else mem_k_sb[:, h, :]
                    mm = matmul(bank(o + kt // 2, slice((kt % 2) * S, (kt % 2 + 1) * S)), w,
                                qa[b % 2][:, h, :])
                return mm

            def o1(o, b, hp):
                pe.wait_ge(sem("s1_read_a"), H * b + 2 * hp + 2)
                if b == 0 and hp == 0:
                    pe.wait_ge(sem("memv_loaded"), 16)
                    pe.wait_ge(sem("ones64_ready"), 1)
                for kt in range(KT1):
                    for j in range(2):
                        h = 2 * hp + j
                        w = v1[:, b * TB + kt] if kt < TB else mem_v_sb
                        matmul(bank(o, slice(0, S), slice(j * DK1, (j + 1) * DK1)), w[:, h * DK1:(h + 1) * DK1],
                               p1[:, (H * b + h) % 4, kt, :], start=(kt == 0), stop=(kt == KT1 - 1))
                pe.wait_ge(sem("key_sum_ready"), H // 2 * b + hp + 1)
                for j in range(2):
                    mm = matmul(bank(o, slice(S, 2 * S), slice(j * DK1, (j + 1) * DK1)), ones64[:, :],
                                key_sum[:, hp % 2, j, :])
                return mm

            def w1(o, b):
                pe.wait_ge(sem("o1_read_v"), (H // 2) * (b + 1))
                for t in range(TB):
                    for c in range(H // 2):
                        mm = matmul(bank(o, slice(t * P, (t + 1) * P)), ct1[b % 2][:, c, t * P:(t + 1) * P],
                                    wo1_sb[:, c * D:(c + 1) * D], start=(c == 0), stop=(c == H // 2 - 1))
                return mm

            def rt(o, b):
                pe.wait_ge(sem("xt3_read_a"), b + 1)
                for t in range(TB):
                    at = (b * TB + t) * P
                    mm = matmul(bank(o, slice(t * E, (t + 1) * E)), xt[:, at:at + P], pk("wr"))
                return mm

            def gu(o, t):
                return matmul(bank(o), xt[:, t * P:(t + 1) * P], pk("wgu"))

            def ht(o, t):
                pe.wait_ge(sem("hid_ready"), t + 1)
                for c in range(2):
                    mm = nc.tensor.transpose(bank(o, slice(c * P, (c + 1) * P)), hid[t % 2][:, c * P:(c + 1) * P],
                                             ident)
                return mm

            def f3(o, t):
                pe.wait_ge(sem("ht_read_a"), t + 1)
                pe.wait_ge(sem("conv_ready"), t // TB + 1)
                for c in range(2):
                    matmul(bank(o, slice(0, D)), hidt[t % 2][:, c * P:(c + 1) * P], pk("wd")[:, c * D:(c + 1) * D],
                           start=(c == 0), stop=False)
                return matmul(bank(o, slice(0, D)), conv[:, t * P:(t + 1) * P], ident, start=False)

            emit = {
                "k0": k0, "v0": v0_, "q0": q0, "a0": a0, "t0": t0, "s0": s0, "o0": o0, "d0": d0, "e0": e0, "w0": w0,
                "v1": v1_, "k1": k1, "g1": g1, "gc": gc, "mb": mb, "u1": u1, "y1": y1, "q1": q1, "a1": a1, "t1": t1,
                "s1": s1, "o1": o1, "w1": w1, "rt": rt, "gu": gu, "ht": ht, "f3": f3,
                "m1": lambda o, k: merge(0, o, k), "m2": lambda o, k: merge(1, o, k),
                "xt0": lambda o, h: transposes(0, o, h), "xt1": lambda o, h: transposes(1, o, h),
                "xt2": lambda o, h: transposes(2, o, h), "xt3": lambda o, h: transposes(3, o, h),
            }
            for (kind, key, banks, _), earlier in zip(units, before):
                if not banks:
                    continue
                for was in earlier:
                    if was:
                        for who in was[2]:
                            pe.wait_ge(sem(f"{was[0]}_read_{who}"), was[1])
                emit[kind](banks[0], *key).then_inc(sem(kind + "_filled"), 1)

        @block.scalar
        def _(act):
            def done(ins, kind):
                return ins.then_inc(sem(kind + "_read_a"), 1)

            for kind, key, banks, readers in units:
                if "a" not in readers:
                    continue
                o = ready(act, kind, *key) if banks else None
                if kind in ("k0", "q0"):
                    i, b = (1 if kind == "k0" else 0), key[0]
                    done(nc.scalar.activation(qk_f[i][:, b * S:(b + 1) * S], bank(o, slice(0, S)), ACT.Identity,
                                              bias=pk("bk0" if i else "bq0")), kind)
                elif kind in ("xt0", "xt1", "xt2", "xt3"):
                    layer, b = int(kind[2]), key[0]
                    if layer == 1:
                        act.wait_ge(sem("q0_filled"), b + 1)
                    if layer == 2:
                        act.wait_ge(sem("u1_filled"), 2 * (b + 1))
                    if layer == 3:
                        act.wait_ge(sem("q1_filled"), index["q1", (b, H // 2 - 1)][0])
                    done(nc.scalar.activation(xt[:, b * S:(b + 1) * S], bank(o, slice(0, S)), ACT.Copy), kind)
                elif kind == "stacks":
                    b = key[0]
                    act.wait_ge(sem("s0_filled"), index["s0", (b - 2, H // 2 - 1)][0])
                    act.wait_ge(sem("k_stored"), (b + 1) * 3 * 16)
                    act.wait_ge(sem("q_stored"), (b + 1) * 3 * 16)
                    load_k_stack(act, b)
                    load_q_stack(act, b)
                elif kind == "s0":
                    b, hp = key
                    pair = 8 * b + hp
                    if pair >= 4:
                        act.wait_ge(sem("o0_filled"), (pair - 4) // 2 + 1)
                    ins = nc.scalar.activation(p0[:, pair % 4].rearrange("p j k s -> p (j k s)"),
                                               psum[:, o:o + 2, :].rearrange("p a n -> p (a n)"), ACT.Exp,
                                               scale=float(DK0) ** -0.5)
                    ins.then_inc(sem("s0_read_a"), 1)
                elif kind == "o0":
                    b, g = key
                    if b >= 2 and g == 0:
                        act.wait_ge(sem("e0_read_v"), 2 * (b - 2) + 2)
                        act.wait_ge(sem("d0_filled"), b - 1)
                    nc.scalar.activation(u0[b % 2][:, g * S:(g + 1) * S], bank(o, slice(0, S)),
                                         ACT.Copy).then_inc(sem("o0_read_a"), 1)
                elif kind == "g1":
                    b = key[0]
                    if b:
                        act.wait_ge(sem("g1_read_a"), b)
                    done(nc.scalar.activation(gate_relu, bank(o, slice(0, S)), ACT.Relu, bias=pk("gb1"),
                                              accum_out=hsum[:, b:b + 1]), kind)
                elif kind in ("k1", "q1"):
                    b, c = key
                    if kind == "k1" and b == 0 and c == 0:
                        act.wait_ge(sem("s0_filled"), 8 * B)
                    if kind == "q1" and c == 0 and b < 2:
                        act.wait_ge(sem("m2_filled"), 4)
                        if b:
                            act.wait_ge(sem("y1_filled"), B)
                    if b >= 2:
                        act.wait_ge(sem("s1_filled"), index["s1", (b - 2, 2 * c)][0])
                    to = (kb if kind == "k1" else qa)[b % 2]
                    done(nc.scalar.activation(to[0:DK1, 2 * c, :], bank(o, slice(0, S), slice(0, DK1)), ACT.Identity,
                                              bias=pk("bk1" if kind == "k1" else "bq1")[0:DK1, c:c + 1]), kind)
                elif kind == "u1":
                    b, c2 = key
                    if b == 0 and c2 == 0:
                        act.wait_ge(sem("mb_read_v"), 1)
                        act.wait_ge(sem("w0_filled"), B)
                        act.wait_ge(sem("m1_filled"), 4)
                    for j in range(2):
                        c = 2 * c2 + j
                        of = bank(o, slice(j * S, (j + 1) * S))
                        nc.scalar.activation(ff_u[b][:, c * S:(c + 1) * S], of, ACT.Identity, bias=mb1[:, c, b:b + 1])
                        ins = nc.scalar.activation(ff_y[b][:, c * S:(c + 1) * S], of, ACT.Square,
                                                   bias=mb1_root[:, c, b:b + 1], scale=CUBIC ** 0.5)
                    ins.then_inc(sem("u1_read_a"), 1)
                elif kind == "tanh":
                    b = key[0]
                    act.wait_ge(sem("cubic_ready"), b + 1)
                    nc.scalar.activation(ff_y[b], ff_y[b], ACT.Tanh,
                                         scale=0.7978845608028654).then_inc(sem("tanh_ready"), 1)
                elif kind == "s1":
                    b, h = key
                    n = H * b + h
                    if n >= 4:
                        act.wait_ge(sem("o1_filled"), (n - 4) // 2 + 1)
                    elif n == 0:
                        act.wait_ge(sem("y1_filled"), B)
                    nc.scalar.activation(p1[:, n % 4].rearrange("p k s -> p (k s)"),
                                         psum[:, o:o + 2, :].rearrange("p a n -> p (a n)")[:, 0:KT1 * S], ACT.Exp,
                                         scale=float(DK1) ** -0.5).then_inc(sem("s1_read_a"), 1)
                elif kind == "rt":
                    b = key[0]
                    if b == 0:
                        act.wait_ge(sem("s1_filled"), (B - 1) * H)
                    nc.scalar.activation(router[:, 0, b * TB:(b + 1) * TB].rearrange("p t e -> p (t e)"),
                                         bank(o, slice(0, TB * E)), ACT.Tanh, scale=0.5).then_inc(sem("rt_read_a"), 1)
                elif kind == "gu":
                    t = key[0]
                    if t >= 2:
                        act.wait_ge(sem("gu_read_v"), t - 1)
                    nc.scalar.activation(gu_t[t % 2], bank(o, slice(0, 256)), ACT.Tanh,
                                         scale=0.5).then_inc(sem("gu_read_a"), 1)
                elif kind == "ht":
                    t = key[0]
                    if t >= 2:
                        act.wait_ge(sem("f3_filled"), t - 1)
                    nc.scalar.activation(hidt[t % 2], bank(o, slice(0, 256)), ACT.Copy).then_inc(sem("ht_read_a"), 1)

        @block.gpsimd
        def _(pool):
            steps = [0]

            def then(ins):
                steps[0] += 1
                ins.then_inc(sem("pool_step"), 1)
                pool.wait_ge(sem("pool_step"), steps[0])

            then(nc.gpsimd.memset(minus_half[:, :], -0.5))

            def inverse_root(layer, b):
                if layer * B + b:
                    pool.wait_ge(sem("rstd_ready"), layer * B + b)
                t = slice(b * TB, (b + 1) * TB)
                pool.wait_ge(sem("mv_ready"), layer * B + b + 1)
                then(nc.gpsimd.tensor_scalar(veps[:, t], mv[:, t, 1], EPS, None, ALU.add))
                nc.gpsimd.tensor_tensor(rstd[:, t], veps[:, t], minus_half[:, t], ALU.pow).then_inc(sem("rstd_ready"), 1)

            for i in range(2):
                words = r_k[:, (2 + i) * half_k:(3 + i) * half_k]
                then(nc.gpsimd.memset(words, 0.0))
                nc.gpsimd.memset(r_k[32:DK1, (2 + i) * half_k:(3 + i) * half_k], BF16_ONES).then_inc(sem("k_stack_cleared"), 1)
                pool.wait_ge(sem("k_stack_cleared"), i + 1)
                if i == 0:
                    inverse_root(0, 0)
            for b in range(1, B):
                inverse_root(0, b)
            pool.wait_ge(sem("rstd_ready"), B)
            pool.wait_ge(sem("k_stored"), B * 3 * 16)
            pool.wait_ge(sem("q_stored"), B * 3 * 16)
            then(nc.gpsimd.memset(mem_k_sb[DK1:P], 0.0))
            then(nc.gpsimd.memset(mem_k_sb[DK1:DK1 + 1], 1.0))
            pool.wait_ge(sem("rows_loaded"), 16)

            def add_bias(layer, b, key):
                for t in range(b * TB, (b + 1) * TB):
                    ins = nc.gpsimd.tensor_tensor(xb[layer][:, t, :], xs[layer][:, t, :], row(key), ALU.add)
                ins.then_inc(sem("bias_added"), 1)

            for b in range(B):
                pool.wait_ge(sem("xn_ready"), b + 1)
                add_bias(0, b, "bo0")
            for b in range(B):
                inverse_root(1, b)
                pool.wait_ge(sem("xn_ready"), B + b + 1)
                add_bias(1, b, "b2")
            pool.wait_ge(sem("s0_filled"), B * H // 2)
            pool.wait_ge(sem("bias_added"), 2 * B)
            for i in range(2):
                nc.gpsimd.memset(kb[i][DK1:DK1 + 1], 1.0).then_inc(sem("kb_ones"), 1)
                pool.wait_ge(sem("kb_ones"), i + 1)

            for b in range(B):
                inverse_root(2, b)
                pool.wait_ge(sem("xn_ready"), 2 * B + b + 1)
                add_bias(2, b, "bo1")

            def finish_layer(b):
                inverse_root(3, b)
                pool.wait_ge(sem("xn_ready"), 3 * B + b + 1)
                add_bias(3, b, "convb")

            pool.wait_ge(sem("y1_filled"), B)
            for b in range(B):
                for hp in range(H // 2):
                    pair = H // 2 * b + hp
                    pool.wait_ge(sem("s1_read_a"), 2 * pair + 2)
                    if pair >= 2:
                        pool.wait_ge(sem("o1_filled"), pair - 1)
                    n = 2 * (pair % 2)
                    to = key_sum[:, pair % 2]
                    then(nc.gpsimd.tensor_tensor(to, p1[:, n:n + 2, 0, :], p1[:, n:n + 2, 1, :], ALU.add))
                    nc.gpsimd.tensor_tensor(to, to, p1[:, n:n + 2, 2, :], ALU.add).then_inc(sem("key_sum_ready"), 1)
                    if b and hp == 2:
                        finish_layer(b - 1)
            finish_layer(B - 1)

        @block.vector
        def _(dve):
            steps = [0]

            def then(ins):
                steps[0] += 1
                ins.then_inc(sem("vector_step"), 1)
                dve.wait_ge(sem("vector_step"), steps[0])

            def signal(ins, kind):
                return ins.then_inc(sem(kind + "_read_v"), 1)

            def moments(layer, b):
                src = xs[layer]
                for t in range(b * TB, (b + 1) * TB):
                    ins = nc.vector.bn_stats(stats[:, t, :], src[:, t, :])
                then(ins)
                for t in range(b * TB, (b + 1) * TB):
                    ins = nc.vector.bn_aggr(mv[:, t, :], stats[:, t, :])
                ins.then_inc(sem("mv_ready"), 1)

            def normalise(layer, b):
                dve.wait_ge(sem("rstd_ready"), layer * B + b + 1)
                if layer:
                    dve.wait_ge(sem(f"xt{layer - 1}_filled"), b + 1)
                for t in range(b * TB, (b + 1) * TB):
                    ins = nc.vector.tensor_scalar(xn[:, t, :], xs[layer][:, t, :], mv[:, t, 0:1], rstd[:, t:t + 1],
                                                  ALU.subtract, ALU.mult)
                ins.then_inc(sem("xn_ready"), 1)

            def split(i, chunk):
                dve.wait_ge(sem("k0_read_a" if i else "q0_read_a"), B if chunk else 1)
                t = slice(S, T) if chunk else slice(0, S)
                of, (high, mid, low) = qk_f[i][:, t], (part[i][n][:, t] for n in range(3))

                def part_done(ins, n):
                    ins.then_inc(sem("part_ready"), 1)
                    dve.wait_ge(sem("part_ready"), 6 * chunk + 3 * (1 - i) + n + 1)

                part_done(nc.vector.tensor_copy(high, of), 0)
                then(nc.vector.tensor_tensor(rest[:, t], of, high, ALU.subtract))
                part_done(nc.vector.tensor_copy(mid, rest[:, t]), 1)
                part_done(nc.vector.tensor_tensor(low, rest[:, t], mid, ALU.subtract), 2)

            nc.vector.memset(r_k[:, 0:2 * half_k], 0.0).then_inc(sem("q_stack_cleared"), 1)
            dve.wait_ge(sem("x_loaded"), 16)
            for b in range(B):
                moments(0, b)
            nc.vector.memset(ones64[:, :], 1.0).then_inc(sem("ones64_ready"), 1)
            then(nc.vector.memset(v0[:, :, :, :].rearrange("p t h e -> p (t h e)"), 1.0))
            dve.wait_ge(sem("early_loaded"), 16)
            nc.vector.tensor_copy(ident_bf[:, :], ident).then_inc(sem("ident_ready"), 1)

            def cubic(b):
                dve.wait_ge(sem("u1_read_a"), 2 * b + 2)
                nc.vector.scalar_tensor_tensor(ff_y[b], ff_y[b], 1.0, ff_u[b], ALU.add, ALU.mult).then_inc(
                    sem("cubic_ready"), 1)

            def gate(b):
                dve.wait_ge(sem("tanh_ready"), b + 1)
                nc.vector.scalar_tensor_tensor(ff_y[b], ff_y[b], 1.0, ff_u[b], ALU.add, ALU.mult).then_inc(
                    sem("ffy_ready"), 1)

            def routing(b):
                tiles = slice(b * TB, (b + 1) * TB)
                s, biased, chosen, cw = (router[:, i, tiles] for i in range(4))
                dve.wait_ge(sem("rt_read_a"), b + 1)
                then(nc.vector.tensor_scalar(s, s, 0.5, 0.5, ALU.mult, ALU.add))
                then(nc.vector.tensor_tensor(biased, s, row("rb").unsqueeze(1).to_broadcast([P, TB, E]), ALU.add))
                other = biased.unsqueeze(2).to_broadcast([P, TB, E, E])
                mine = biased.unsqueeze(3).to_broadcast([P, TB, E, E])
                nc.vector.tensor_tensor(cmp_gt, other, mine, ALU.is_gt)
                then(nc.vector.tensor_tensor(cmp_eq, other, mine, ALU.is_equal))
                then(nc.vector.tensor_tensor(cmp_eq.rearrange("p t i j -> p t (i j)"),
                                             cmp_eq.rearrange("p t i j -> p t (i j)"),
                                             pk("before").unsqueeze(1).to_broadcast([P, TB, E * E]), ALU.mult))
                then(nc.vector.tensor_tensor(cmp_gt.rearrange("p t i j -> p (t i j)"),
                                             cmp_gt.rearrange("p t i j -> p (t i j)"),
                                             cmp_eq.rearrange("p t i j -> p (t i j)"), ALU.add))
                then(nc.vector.tensor_reduce(rank[:, tiles], cmp_gt, AX.X, ALU.add))
                then(nc.vector.tensor_scalar(chosen, rank[:, tiles], 1.5, None, ALU.is_lt))
                then(nc.vector.tensor_tensor(cw, s, chosen, ALU.mult))
                total, inverse = cw_sum[:, 0, tiles], cw_sum[:, 1, tiles]
                then(nc.vector.tensor_reduce(total, cw, AX.X, ALU.add))
                then(nc.vector.tensor_scalar(total, total, 1e-9, None, ALU.add))
                then(nc.vector.reciprocal(inverse, total))
                then(nc.vector.tensor_tensor(cw, cw, inverse.unsqueeze(2).to_broadcast([P, TB, E]), ALU.mult))
                nc.vector.tensor_tensor(stay[:, tiles], cw[:, :, EM], cw[:, :, EM + 2], ALU.add)
                then(nc.vector.tensor_scalar(cw[:, :, 0:EM], cw[:, :, 0:EM], 0.5, None, ALU.mult))

            def convolve(b):
                dve.wait_ge(sem("xt3_read_a"), b + 1)
                of, to = xt[:, b * S:(b + 1) * S], conv[:, b * S:(b + 1) * S]
                then(nc.vector.tensor_scalar(to, of, pk("convw")[:, KC - 1:KC], None, ALU.mult))
                for k in range(KC - 1):
                    back = KC - 1 - k
                    ins = nc.vector.scalar_tensor_tensor(to[:, back:], of[:, 0:S - back], pk("convw")[:, k:k + 1],
                                                         to[:, back:], ALU.mult, ALU.add)
                    if k < KC - 2:
                        then(ins)
                ins.then_inc(sem("conv_ready"), 1)
                dve.wait_ge(sem("bias_added"), 3 * B + b + 1)
                for t in range(b * TB, (b + 1) * TB):
                    ins = nc.vector.scalar_tensor_tensor(xs[2][:, t, :], xn[:, t, :], stay[:, t:t + 1],
                                                         xs[3][:, t, :], ALU.mult, ALU.add)
                then(ins)
                for t in range(b * TB, (b + 1) * TB):
                    ins = nc.vector.tensor_scalar(xs[0][:, t, :], xn[:, t, :], 0.0, router[:, 3, t, EM + 3:EM + 4],
                                                  ALU.max, ALU.mult)
                then(ins)
                then(nc.vector.tensor_tensor(xs[2][:, b * TB:(b + 1) * TB, :], xs[2][:, b * TB:(b + 1) * TB, :],
                                             xs[0][:, b * TB:(b + 1) * TB, :], ALU.add))

            for kind, key, banks, readers in units:
                if "v" not in readers:
                    continue
                o = ready(dve, kind, *key) if banks else None
                if kind == "norm":
                    normalise(*key)
                elif kind == "split":
                    split(*key)
                elif kind == "cubic":
                    cubic(*key)
                elif kind == "gate":
                    gate(*key)
                elif kind == "route":
                    routing(*key)
                elif kind == "conv":
                    convolve(*key)
                elif kind == "v0":
                    half = key[0]
                    dve.wait_ge(sem("rows_loaded"), 16)
                    for t in range(4):
                        ins = nc.vector.tensor_tensor(
                            v0[:, half * 4 + t, :, 0:DK0],
                            bank(o, slice(t * P, (t + 1) * P)).rearrange("p (h d) -> p h d", h=H),
                            row("bv0").rearrange("p (h d) -> p h d", h=H), ALU.add)
                    ins.then_inc(sem("v0_read_v"), 1)
                elif kind == "a0":
                    b, u = key
                    hp, qt = u // 2, u % 2
                    signal(nc.vector.tensor_reduce(neg_max[:, b % 2, qt, 2 * hp:2 * hp + 2],
                                                   bank(o).rearrange("p (j s) -> p j s", j=2), AX.X, ALU.max,
                                                   negate=True), kind)
                elif kind == "parts0":
                    b = key[0]
                    nm = neg_max[:, b % 2]
                    dve.wait_ge(sem("a0_read_v"), H * (b + 1))
                    if b:
                        dve.wait_ge(sem("t0_filled"), b)
                    then(nc.vector.tensor_copy(nm_part[:, :, 0:H], nm))
                    then(nc.vector.tensor_tensor(nm_rest[:, :, :], nm, nm_part[:, :, 0:H], ALU.subtract))
                    nc.vector.tensor_copy(nm_part[:, :, H:2 * H], nm_rest[:, :, :]).then_inc(sem("nm_part_ready"), 1)
                elif kind == "t0":
                    b = key[0]
                    if b:
                        dve.wait_ge(sem("max0_stored"), 2 * 16 * b)
                    signal(nc.vector.tensor_copy(nmt0[:, :], bank(o, slice(0, P), slice(0, 2 * H)).bitcast(BF16)),
                           kind)
                elif kind == "d0":
                    b = key[0]
                    if b:
                        dve.wait_ge(sem("e0_filled"), 2 * b)
                    signal(nc.vector.reciprocal(rden0, bank(o, slice(0, S), slice(0, H))), kind)
                elif kind == "e0":
                    b, half = key
                    if b and half == 0:
                        dve.wait_ge(sem("w0_filled"), b)
                    cols = slice(half * 512, (half + 1) * 512)
                    dve.wait_ge(sem("o0_read_a"), 4 * b + 4)
                    signal(nc.vector.tensor_tensor(un0[:, cols], u0[b % 2][:, cols], bank(o), ALU.mult), kind)
                elif kind in ("w0", "w1"):
                    b, layer = key[0], 0 if kind == "w0" else 2
                    dve.wait_ge(sem("bias_added"), layer * B + b + 1)
                    signal(nc.vector.tensor_tensor(
                        xs[layer + 1][:, b * TB:(b + 1) * TB, :].rearrange("p t d -> p (t d)"), bank(o, slice(0, S)),
                        xb[layer][:, b * TB:(b + 1) * TB, :].rearrange("p t d -> p (t d)"), ALU.add), kind)
                    dve.wait_ge(sem(kind + "_read_v"), b + 1)
                    moments(layer + 1, b)
                elif kind == "v1":
                    t, half = key
                    cols = slice(half * 512, (half + 1) * 512)
                    if t < 4:
                        dve.wait_ge(sem("o0_filled"), 4 * B)
                    signal(nc.vector.tensor_tensor(v1[:, t, cols], bank(o), row("bv1")[:, cols], ALU.add), kind)
                elif kind in ("k1", "q1"):
                    b, c = key
                    if kind == "k1" and b == 0 and c == 0:
                        dve.wait_ge(sem("s0_filled"), 8 * B)
                    if kind == "q1" and c == 0 and b < 2:
                        dve.wait_ge(sem("m2_filled"), 4)
                        if b:
                            dve.wait_ge(sem("y1_filled"), B)
                    if b >= 2:
                        dve.wait_ge(sem("s1_filled"), index["s1", (b - 2, 2 * c + 1)][0])
                    to = (kb if kind == "k1" else qa)[b % 2]
                    signal(nc.vector.tensor_scalar(to[0:DK1, 2 * c + 1, :], bank(o, slice(0, S), slice(DK1, P)),
                                                   pk("bk1" if kind == "k1" else "bq1")[DK1:P, c:c + 1], None,
                                                   ALU.add), kind)
                elif kind == "gc":
                    signal(nc.vector.tensor_scalar(gcol[:, :], bank(o, slice(0, B)), 1.0 / S, pk("gb2"), ALU.mult,
                                                   ALU.add), kind)
                    dve.wait_ge(sem("gc_read_v"), 1)
                    for b in range(B):
                        ins = nc.vector.tensor_scalar(gdiag[:, b, :], pk("delta"), gcol[:, b:b + 1], None, ALU.mult)
                    ins.then_inc(sem("gdiag_ready"), 1)
                    for b in range(B):
                        ins = nc.vector.tensor_scalar(gwide[:, b, :], ident, 0.0, gcol[:, b:b + 1], ALU.mult, ALU.add)
                    then(ins)
                    ins = nc.vector.tensor_scalar(gwide[:, :, :].rearrange("p b n -> p (b n)"),
                                                  gwide[:, :, :].rearrange("p b n -> p (b n)"), 2.0, None, ALU.mult)
                    then(ins)
                elif kind == "mb":
                    signal(nc.vector.tensor_tensor(mb1[:, :, :], bank(o, slice(0, FC * B)).rearrange(
                        "p (c b) -> p c b", c=FC), pk("b1").unsqueeze(2).to_broadcast([P, FC, B]), ALU.add), "mb_sum")
                    dve.wait_ge(sem("mb_sum_read_v"), 1)
                    signal(nc.vector.tensor_scalar(mb1_root[:, :, :], mb1[:, :, :], CUBIC ** 0.5, None, ALU.mult), kind)
                elif kind == "m1":
                    k = key[0]
                    if k == 0:
                        dve.wait_ge(sem("o0_filled"), 4 * B)
                    signal(nc.vector.tensor_tensor(
                        mw1[:, :, k * P:(k + 1) * P].rearrange("p b (c j) -> p c b j", j=J),
                        bank(o).rearrange("p (c b j) -> p c b j", b=B, j=J),
                        pk("w1")[:, k * P:(k + 1) * P].rearrange("p (c j) -> p c j", j=J).unsqueeze(2).to_broadcast(
                            [P, 8, B, J]), ALU.add), kind)
                elif kind == "m2":
                    k = key[0]
                    signal(nc.vector.tensor_tensor(
                        mw2[:, k, :, :].rearrange("p b (j n) -> p n b j", n=8),
                        bank(o).rearrange("p (n b j) -> p n b j", b=B, j=J),
                        pk("w2")[:, k * D:(k + 1) * D].rearrange("p (j n) -> p n j", n=8).unsqueeze(2).to_broadcast(
                            [P, 8, B, J]), ALU.add), kind)
                elif kind == "y1":
                    b = key[0]
                    dve.wait_ge(sem("bias_added"), B + b + 1)
                    signal(nc.vector.scalar_tensor_tensor(
                        xs[2][:, b * TB:(b + 1) * TB, :].rearrange("p t d -> p (t d)"), bank(o, slice(0, S)), 0.5,
                        xb[1][:, b * TB:(b + 1) * TB, :].rearrange("p t d -> p (t d)"), ALU.mult, ALU.add), kind)
                    dve.wait_ge(sem("y1_read_v"), b + 1)
                    moments(2, b)
                elif kind == "a1":
                    b, h, qt = key
                    if b >= 2 and h == 0 and qt == 0:
                        dve.wait_ge(sem("t1_filled"), b - 1)
                    signal(nc.vector.tensor_reduce(neg_max[:, b % 2, qt, h:h + 1], bank(o, slice(0, S + MEM)), AX.X,
                                                   ALU.max, negate=True), kind)
                elif kind == "t1":
                    b = key[0]
                    if b:
                        dve.wait_ge(sem("max1_stored"), 16 * b)
                    signal(nc.vector.tensor_copy(nmt1[:, :], bank(o, slice(0, S), slice(0, H))), kind)
                elif kind == "head_out":
                    b, hp = key
                    o = ready(dve, "o1", b, hp)
                    if b == 0 and hp == 0:
                        dve.wait_ge(sem("y1_filled"), B)
                    if b >= 2 and hp == 0:
                        dve.wait_ge(sem("w1_filled"), b - 1)
                    rd = rden1[:, hp % 2, :]
                    then(nc.vector.reciprocal(rd, bank(o, slice(S, 2 * S))))
                    signal(nc.vector.tensor_tensor(ct1[b % 2][:, hp, :], bank(o, slice(0, S)), rd, ALU.mult), "o1")
                elif kind == "gu":
                    t = key[0]
                    gt, w = gu_t[t % 2], gu_w[t % 2]
                    dve.wait_ge(sem("gu_read_a"), t + 1)
                    then(nc.vector.scalar_tensor_tensor(w, gt, 1.0, bank(o, slice(0, 256)), ALU.add, ALU.mult))
                    if t >= 2:
                        dve.wait_ge(sem("ht_filled"), t - 1)
                    signal(nc.vector.tensor_tensor(w, w, bank(o, slice(256, 512)), ALU.mult), kind)
                    dve.wait_ge(sem("gu_read_v"), t + 1)
                    nc.vector.tensor_tensor(
                        hid[t % 2].rearrange("p (e i) -> p e i", e=EM), w.rearrange("p (e i) -> p e i", e=EM),
                        router[:, 3, t, 0:EM].unsqueeze(2).to_broadcast([P, EM, EI]), ALU.mult).then_inc(
                            sem("hid_ready"), 1)
                elif kind == "f3":
                    t = key[0]
                    y = xs[1][:, t, :]
                    signal(nc.vector.tensor_tensor(y, bank(o, slice(0, D)), xs[2][:, t, :], ALU.add), kind)


def _layout(inp):
    g = {k: np.ascontiguousarray(np.asarray(v)) for k, v in inp.items()}

    def cols(v, n=P):
        return np.ascontiguousarray(v.reshape(-1, n).T)

    f_order = np.arange(F).reshape(J, F // J).T.reshape(-1)
    pack = {}
    pack["wk0"], pack["wv0"], pack["wq0"] = (g[f"L0_xattn_W{c}"].T for c in "kvq")
    pack["ident"] = np.eye(P, dtype=np.float32)
    pack["bk0"], pack["bq0"] = cols(g["L0_xattn_bk"]), cols(g["L0_xattn_bq"])
    pack["gb1"] = cols(g["L0_ffn_gate_b1"])
    pack["gb2"] = np.repeat(g["L0_ffn_gate_b2"], J)[:, None]
    pack["b1"] = cols(g["L0_ffn_b1"][f_order])
    pack["bq1"], pack["bk1"] = cols(g["L1_xattn_wq_b"]), cols(g["L1_xattn_wk_b"])
    pack["convw"] = g["L1_ffn_conv_w"][:, 0, :].T
    wo = g["L0_xattn_Wo"].T.reshape(4, 4, DK0, D)
    spread = np.zeros((P, 4, D), np.float32)
    for j in range(4):
        spread[32 * j:32 * j + DK0] = wo[:, j].transpose(1, 0, 2)
    pack["wo0"] = spread.reshape(P, 4 * D)
    pick = np.zeros((P, 4, H), np.float32)
    put = np.zeros((P, 4, P), np.float32)
    for q in range(4):
        for j in range(4):
            pick[32 * j + DK0, q, 4 * q + j] = 1
            put[4 * q + j, q, 32 * j:32 * j + 32] = 1
    pack["den_pick"], pack["den_spread"] = pick.reshape(P, -1), put.reshape(P, -1)
    pack["gw1"] = g["L0_ffn_gate_w1"].T
    pack["gw2"] = np.repeat(g["L0_ffn_gate_w2"].T, J, axis=1)
    pack["delta"] = np.tile(np.eye(J, dtype=np.float32), (E, 1))
    pack["w1"] = g["L0_ffn_W1"].T[:, f_order]
    pack["w2"] = g["L0_ffn_W2"].T[f_order].reshape(FC, P, D).transpose(1, 0, 2).reshape(P, FC * D)
    tb1, tb2 = np.zeros((P, F), np.float32), np.zeros((P, D), np.float32)
    tb1[::J], tb2[::J] = g["L0_ffn_Tb1"][:, f_order], g["L0_ffn_Tb2"]
    pack["tb1"], pack["tb2"] = tb1, tb2
    wg, wu = (g[f"L1_ffn_W{c}"].transpose(1, 0, 2).reshape(D, EM * EI) for c in "gu")
    pack["wgu"] = np.concatenate([wg, wu], 1)
    pack["wd"] = g["L1_ffn_Wd"].reshape(2, P, D).transpose(1, 0, 2).reshape(P, 2 * D)
    pack["wr"] = g["L1_ffn_Wr"]
    pack["before"] = np.tile(np.tril(np.ones((E, E), np.float32), -1).reshape(1, -1), (P, 1))
    packed = {}
    for name in ("early", "late"):
        packed[name] = np.concatenate([pack[k] for k, v in PACK.items() if v[0] == name], 1)
    rows = {"bv0": g["L0_xattn_bv"], "bo0": g["L0_xattn_bo"], "b2": g["L0_ffn_b2"], "bo1": g["L1_xattn_wo_b"],
            "convb": g["L1_ffn_conv_b"], "rb": g["L1_ffn_router_bias"], "bv1": g["L1_xattn_wv_b"]}
    tw2 = g["L0_ffn_TW2"][:, :, f_order].reshape(P, 8 * F)
    return {
        "x": g["x"].reshape(T, D),
        "ctx_t": g["ctx_1024"].reshape(T, D).T,
        "early": packed["early"], "late": packed["late"],
        "rows": np.concatenate([rows[k] for k in ROWS])[None, :],
        "tw1": g["L0_ffn_TW1"].reshape(P, 32 * D),
        "tw2": tw2,
        "wq1": g["L1_xattn_wq_w"], "wk1": g["L1_xattn_wk_w"], "wv1": g["L1_xattn_wv_w"],
        "wo1": g["L1_xattn_wo_w"].reshape(H // 2, P, D).transpose(1, 0, 2).reshape(P, -1),
        "mem_k": g["L1_xattn_mk"][0].reshape(MEM, H, DK1).transpose(2, 1, 0),
        "mem_v": g["L1_xattn_mv"][0],
    }


def kernel(**inputs):
    import concourse.bacc as _bacc
    from concourse.bass_utils import run_bass_kernel_spmd as _run

    nc = _bacc.Bacc("TRN2", target_bir_lowering=False, num_devices=1)
    arrays, args = {}, []
    for name, a in _layout(inputs).items():
        a = np.ascontiguousarray(a)
        arrays[f"in_{name}"] = a
        args.append(nc.dram_tensor(f"in_{name}", a.shape, F32, kind="ExternalInput").ap())
    args.append(nc.dram_tensor("out_x", (T, D), F32, kind="ExternalOutput").ap())
    xattn_ffn_kernel(nc, *args)
    r = _run(nc, [arrays], core_ids=[0])
    return r.results[0]["out_x"].reshape(B, S, D)
```

```python
from contextlib import ExitStack

import numpy as np

import concourse.bass as bass
from concourse import mybir

F32 = mybir.dt.float32
BF16 = mybir.dt.bfloat16
ALU = mybir.AluOpType
ACT = mybir.ActivationFunctionType
AX = mybir.AxisListType

P = 128
B, S, D = 4, 256, 128
T = B * S
NT = T // P
TB = S // P
H = 16
DK0 = D // H
DK1 = 64
MEM = 128
KT1 = (S + MEM) // P
E, F = 8, 512
J = P // E
FC = F // P
EM, EI = 4, 64
KC = 4
EPS = 1e-5
BF16_ONES = float(np.array(0x3F803F80, np.uint32).view(np.float32))
CUBIC = 0.044715

QPART = ("h", "m", "h", "m", "h", "l")
KPART = ("m", "m", "h", "h", "l", "h")
Q_SLOT, K_SLOT = "hml", "lmh"
ST0 = len(QPART) * DK0
NM0 = P - 2

PACK = {}


def _pack(name, *widths):
    at = 0
    for key, w in widths:
        PACK[key] = (name, at, w)
        at += w
    return at


N_EARLY = _pack("early", ("wk0", D), ("wv0", D), ("wq0", D), ("ident", P), ("bk0", 1), ("bq0", 1),
                ("gb1", 1), ("gb2", 1), ("b1", FC), ("bq1", H // 2), ("bk1", H // 2), ("convw", KC))
N_LATE = _pack("late", ("wo0", D), ("pick", 2 * 32), ("gw1", D), ("gw2", P),
               ("delta", J), ("w1", F), ("w2", FC * D), ("tb1", F), ("tb2", D), ("wgu", 2 * EM * EI),
               ("wd", 2 * D), ("wr", E), ("before", E * E))
ROWS = {}
_at = 0
for _k, _w in (("bv0", D), ("bo0", D), ("b2", D), ("bo1", D), ("convb", D), ("rb", E), ("bv1", H * DK1)):
    ROWS[_k] = (_at, _w)
    _at += _w
N_ROWS = _at


def schedule():
    units = []
    ring = [0]
    everything, wide, narrow0, narrow1 = tuple(range(8)), (0, 1, 2, 3, 4, 5), (0, 1, 5, 7), (0, 1)

    def small(kind, key, readers, banks):
        units.append((kind, key, (banks[ring[0] % len(banks)],), readers))
        ring[0] += 1

    def step(kind, key, engines="v"):
        units.append((kind, key, (), engines))

    def place(todo, banks):
        for kind, key, readers in todo:
            if readers in ("", "A"):
                step(kind, key, "a" if readers else "v")
            else:
                small(kind, key, readers, banks)

    step("moments", (0, 0))
    step("norm", (0, 0))
    small("k0", (0,), "a", everything)
    step("split", (1,))
    small("xt0", (0,), "a", everything)
    small("q0", (0,), "a", everything)
    step("moments", (0, 1))
    step("split", (0,))
    for b in range(2, B):
        step("moments", (0, b))
    for b in range(1, B):
        step("norm", (0, b))
    for b in range(1, B):
        small("k0", (b,), "a", everything)
    for b in range(1, B):
        small("xt0", (b,), "a", everything)
        small("q0", (b,), "a", everything)
        if b == 1:
            step("mid", (1,), "a")
    step("mid", (0,), "a")

    for u in range(H):
        small("a0", (0, u), "v", everything)
    step("parts0", (0,))
    small("t0", (0,), "v", everything)
    for half in range(2):
        small("v0", (half,), "v", everything)
    maxima_beside = (1,) * 9 + (2, 1, 1, 2, 1, 0, 0)
    for b in range(B):
        at = 0
        for h, n in enumerate(maxima_beside):
            units.append(("s0", (b, h), (2 + h % 3,), "a"))
            if b + 1 < B:
                for u in range(at, at + n):
                    small("a0", (b + 1, u), "v", narrow0)
                at += n
            if h % 2 == 0:
                continue
            hp = h // 2
            if hp == 1 and b:
                small("w0", (b - 1,), "v", narrow0)
                if b == B - 1:
                    step("moments", (1, b - 1))
            if hp == 3 and b == B - 1:
                step("norm", (1, b - 1))
            for late, first in ((2, 3), (1, 4)):
                if (late == 2 and b >= 2) or (late == 1 and b == B - 1):
                    if hp == first:
                        small("xt1", (b - late,), "a", narrow0)
                    if hp == first + 2:
                        small("g1", (b - late,), "a", narrow0)
            if hp in (2, 4) and b == B - 1:
                small("v1", (NT - 1, hp // 2 - 1), "v", narrow0)
            if hp % 2 == 0 and hp:
                units.append(("o0", (b, hp // 2 - 1), (6,), "a"))
        if b + 1 < B:
            step("parts0", (b + 1,))
            small("v1", (NT // 2 + b, 0), "v", narrow0)
            small("t0", (b + 1,), "v", narrow0)
            if b:
                step("moments", (1, b - 1))
        units.append(("o0", (b, H // 4 - 1), (6,), "a"))
        if b + 1 < B:
            small("v1", (NT // 2 + b, 1), "v", narrow0)
            small("d0", (b,), "v", narrow0)
            if b:
                step("norm", (1, b - 1))

    small("v1", (0, 0), "v", wide)
    small("d0", (B - 1,), "v", wide)
    for c in range(3):
        small("k1", (0, c), "a", wide)
    small("w0", (B - 1,), "v", wide)
    step("moments", (1, B - 1))
    small("v1", (0, 1), "v", wide)
    small("v1", (1, 0), "v", wide)
    step("norm", (1, B - 1))
    small("xt1", (B - 1,), "a", wide)
    for c in range(3, 6):
        small("k1", (0, c), "a", wide)
    small("g1", (B - 1,), "a", wide)
    for c in range(6, H // 2):
        small("k1", (0, c), "a", wide)
    small("gc", (), "v", wide)
    small("v1", (1, 1), "v", wide)
    small("mb", (), "v", wide)

    for k in range(4):
        small("m1", (k,), "v", wide)

    def u1(b):
        for c in range(2):
            small("u1", (b, c), "a", wide)

    u1(0)
    small("m2", (0,), "v", wide)
    step("cubic", (0,))
    u1(1)
    step("tanh", (0,), "a")
    small("m2", (1,), "v", wide)
    small("m2", (2,), "v", wide)
    step("gate", (0,))
    step("cubic", (1,))
    small("m2", (3,), "v", wide)
    step("tanh", (1,), "a")
    small("v1", (2, 0), "v", wide)
    small("y1", (0,), "v", wide)
    step("gate", (1,))
    u1(2)
    small("v1", (2, 1), "v", wide)
    step("norm", (2, 0))
    small("y1", (1,), "v", wide)
    step("cubic", (2,))
    small("xt2", (0,), "a", wide)
    small("q1", (0, 0), "a", wide)
    step("norm", (2, 1))
    small("q1", (0, 1), "a", wide)
    step("tanh", (2,), "a")
    small("k1", (1, 0), "a", wide)
    beside = [
        [("gate", (2,), ""), ("u1", (3, 0), "a")],
        [("u1", (3, 1), "a"), ("y1", (2,), "v")],
        [("cubic", (3,), ""), ("norm", (2, 2), ""), ("k1", (1, 1), "a")],
        [("tanh", (3,), "A"), ("xt2", (1,), "a"), ("k1", (1, 2), "a")],
        [("gate", (3,), ""), ("k1", (1, 3), "a"), ("xt2", (2,), "a")],
        [("y1", (3,), "v"), ("k1", (1, 4), "a")],
        [("k1", (1, 5), "a"), ("norm", (2, 3), ""), ("k1", (1, 6), "a")],
        [("xt2", (3,), "a"), ("k1", (1, 7), "a")],
    ]
    for c in range(H // 2):
        for h in (2 * c, 2 * c + 1):
            for qt in range(TB):
                small("a1", (0, h, qt), "v", wide)
        place(beside[c], wide)
        if c + 2 < H // 2:
            small("q1", (0, c + 2), "a", wide)
    small("t1", (0,), "v", wide)
    small("q1", (1, 0), "av", wide)
    for half in range(2):
        small("v1", (3, half), "v", wide)

    portions = 3 * (H // 2)
    filled = portions - 2
    last_layer_from = (0, 8, 15)

    def ahead(b):
        todo = []
        for c in range(H // 2):
            q, k = ([(kind, (b, c + 1), "av")] if c + 1 < H // 2 and (kind == "q1" or b > 1) else []
                    for kind in ("q1", "k1"))
            maxima = [("a1", (b, h, qt), "v") for h in (2 * c, 2 * c + 1) for qt in range(TB)]
            todo += q + maxima[0:2] + k + maxima[2:4]
        at = [len(todo) * i // filled for i in range(filled + 1)]
        return [todo[at[i]:at[i + 1]] for i in range(filled)] + [[] for _ in range(portions - filled)]

    def last_layer(b):
        return [[("xt3", (b,), "a")],
                [("rt", (b,), "a"), ("conv", (b,), ""), ("gu", (2 * b,), "av")],
                [("route", (b,), ""), ("gu", (2 * b + 1,), "av")],
                [],
                [("weigh", (2 * b,), ""), ("weigh", (2 * b + 1,), "")],
                [],
                [("ht", (2 * b,), "a"), ("ht", (2 * b + 1,), "a"), ("pass", (b,), "")],
                [("f3", (2 * b,), "v")], [("f3", (2 * b + 1,), "v")]]

    for b in range(B):
        beside = ahead(b + 1) if b + 1 < B else [[] for _ in range(portions)]
        if b == B - 1:
            for i, first in enumerate(last_layer_from):
                for n, todo in enumerate(last_layer(i)):
                    beside[first + n] += todo
        for hp in range(H // 2):
            for h in (2 * hp, 2 * hp + 1):
                units.append(("s1", (b, h), (2 + 2 * (h % 2), 3 + 2 * (h % 2)), "a"))
                place(beside[3 * hp + h % 2], narrow1)
            if hp == H // 2 - 1 and b + 1 < B:
                small("t1", (b + 1,), "v", narrow1)
            if hp >= 2:
                step("head_out", (b, hp - 2))
            if hp:
                units.append(("o1", (b, hp - 1), (6 + (hp - 1) % 2,), ""))
            place(beside[3 * hp + 2], narrow1)
            if hp == 1 and b:
                small("w1", (b - 1,), "v", narrow1)
            if hp == 2 and b:
                step("norm", (3, b - 1))
        step("head_out", (b, H // 2 - 2))
        units.append(("o1", (b, H // 2 - 1), (6 + (H // 2 - 1) % 2,), ""))
        if b + 2 < B:
            small("q1", (b + 2, 0), "av", narrow1)
            small("k1", (b + 2, 0), "av", narrow1)
        step("head_out", (b, H // 2 - 1))
    small("w1", (B - 1,), "v", narrow1)
    step("norm", (3, B - 1))
    place([("xt3", (B - 1,), "a"), ("rt", (B - 1,), "a"), ("route", (B - 1,), "")], everything)
    for kind, readers in (("gu", "av"), ("weigh", ""), ("ht", "a"), ("pass", ""), ("f3", "v")):
        place([(kind, (B - 1,), readers)] if kind == "pass" else
              [(kind, (t,), readers) for t in range(NT - TB, NT)], everything)
    return units


def xattn_ffn_kernel(nc, x, ctx_t, early, late, rows, tw1, tw2, wq1, wk1, wv1, wo1, mem_k, mem_v, out):
    units = schedule()
    index, count, read_count, when_read = {}, {}, {}, {}
    last_of_bank, before = {}, []
    for kind, key, banks, readers in units:
        count[kind] = count.get(kind, 0) + 1
        index[kind, key] = (count[kind], banks)
        before.append([last_of_bank.get(k) for k in banks])
        for who in readers or "v":
            read_count[kind, who] = read_count.get((kind, who), 0) + 1
            when_read[kind, key, who] = read_count[kind, who]
        for k in banks:
            last_of_bank[k] = [(f"{kind}_read_{who}", read_count[kind, who]) for who in readers or "v"]

    with ExitStack() as ctx:
        def sb(name, shape, dt=F32):
            return ctx.enter_context(nc.sbuf_tensor(name, shape, dt))

        sems = {}

        def sem(name):
            if name not in sems:
                sems[name] = ctx.enter_context(nc.semaphore(name))
            return sems[name]

        psum = ctx.enter_context(nc.psum_tensor("psum", [P, 8, 512], F32))

        scores1 = psum[:, 2:6, :].rearrange("p (j b) n -> p j (b n)", j=2)[:, :, 0:KT1 * S]

        r_q = sb("r_q", [P, 2 * H * S])
        r_k = sb("r_k", [P, 2 * H * S])
        r_p = sb("r_p", [P, 4096])
        r_w = sb("r_w", [P, 6144])
        r_o = sb("r_o", [P, 4096])
        r_v = sb("r_v", [P, NT * H * DK1])

        tw_sb = [r_q[:, i * 4096:(i + 1) * 4096] for i in (1, 0)]
        qa = [r_q[:, i * H * S:(i + 1) * H * S].rearrange("p (h s) -> p h s", h=H) for i in range(2)]
        kb = [r_k[:, i * H * S:(i + 1) * H * S].rearrange("p (h s) -> p h s", h=H) for i in range(2)]
        half_k = H * S // 2
        stack = [r_k[:, i * half_k:(i + 1) * half_k].bitcast(BF16).rearrange("p (h s) -> p h s", h=H)
                 for i in range(4)]
        q_stack, k_stack = stack[:2], stack[2:]
        p0 = r_p[:, :].rearrange("p (n j k s) -> p n j k s", n=4, j=2, k=2)
        p1 = r_p[:, 0:4 * KT1 * S].rearrange("p (n k s) -> p n k s", n=4, k=KT1)
        mw1 = r_p[:, 0:B * F].rearrange("p (b f) -> p b f", b=B)
        mw2 = r_p[:, B * F:2 * B * F].rearrange("p (c b h) -> p c b h", c=FC, b=B)
        qk_f = [r_w[:, i * T:(i + 1) * T] for i in range(2)]
        rest = [r_w[:, 2 * T:3 * T], r_v[:, 4 * T:5 * T]]
        part = [[r_w[:, 3 * T + (3 * i + n) * T // 2:3 * T + (3 * i + n + 1) * T // 2].bitcast(BF16)
                 for n in range(3)] for i in range(2)]
        wq1_sb, wk1_sb, wv1_sb, wo1_sb = (r_w[:, i * 1024:(i + 1) * 1024] for i in range(4))
        mem_k_sb = r_w[:, 4096:4096 + H * MEM].rearrange("p (h m) -> p h m", h=H)
        u0 = [r_o[:, i * 1024:(i + 1) * 1024] for i in range(2)]
        heads0 = [r_o[:, 2048 + i * S:2048 + (i + 1) * S] for i in range(2)]
        ct1 = [r_o[:, i * 2048:(i + 1) * 2048].rearrange("p (c s) -> p c s", c=H // 2) for i in range(2)]
        ff_u = [r_o[:, b * 1024:(b + 1) * 1024] for b in range(B)]
        ff_y = [r_q[:, 4096 + b * 1024:4096 + (b + 1) * 1024] for b in range(B)]
        mem_v_sb = r_p[:, 4 * KT1 * S:4 * KT1 * S + H * DK1]
        v0 = r_v[:, 0:NT * H * 32].rearrange("p (t h e) -> p t h e", t=NT, h=H)
        v1 = r_v[:, :].rearrange("p (t n) -> p t n", t=NT)

        hid = [r_q[:, i * 256:(i + 1) * 256] for i in range(2)]
        hidt = [r_q[:, 512 + i * 256:512 + (i + 1) * 256] for i in range(2)]
        gu_t = [r_q[:, 1024 + i * 256:1024 + (i + 1) * 256] for i in range(2)]
        gu_w = [r_q[:, 1536 + i * 256:1536 + (i + 1) * 256] for i in range(2)]
        conv = r_q[:, 2048:2048 + T]
        router = r_q[:, 3072:3072 + 4 * NT * E].rearrange("p (n t e) -> p n t e", n=4, t=NT)
        cmp_gt, cmp_eq = (r_q[:, 3328 + i * TB * E * E:3328 + (i + 1) * TB * E * E].rearrange(
            "p (t i j) -> p t i j", t=TB, i=E) for i in range(2))

        ctx_sb = sb("ctx_sb", [P, T])
        early_sb = sb("early_sb", [P, N_EARLY])
        late_sb = sb("late_sb", [P, N_LATE])
        rows_sb = sb("rows_sb", [P, N_ROWS])

        def pk(key, p=P):
            name, at, w = PACK[key]
            return (early_sb if name == "early" else late_sb)[0:p, at:at + w]

        xs = [sb("x0_sb", [P, NT, D]), sb("x1_sb", [P, NT, D]), sb("x2_sb", [P, NT, D])]
        xs.append(xs[0])
        xb = xs
        xn = sb("xn", [P, NT, D])
        xt = sb("xt", [P, T])
        stats = sb("stats", [P, NT, 6])
        mv = sb("mv", [P, NT, 2])
        veps = sb("veps", [P, NT])
        rstd = sb("rstd", [P, NT])
        minus_half = sb("minus_half", [P, NT])
        neg_max = sb("neg_max", [P, 2, TB, H])
        nm_rest = sb("nm_rest", [P, TB, H])
        nm_part = sb("nm_part", [P, TB, 2 * H], BF16)
        ident_bf = sb("ident_bf", [P, P], BF16)
        nmt0 = sb("nmt0", [2 * H, S], BF16)
        nmt1 = sb("nmt1", [H, S])
        rden1 = sb("rden1", [P, 2, S])
        rden0 = rden1[:, 0, :]
        ones64 = sb("ones64", [P, DK1])
        hsum = sb("hsum", [P, B])
        gate_relu = rden1[:, 1, :]
        gcol = sb("gcol", [P, B])
        gdiag = sb("gdiag", [P, B, J])
        gwide = sb("gwide", [P, B, P])
        mb1 = sb("mb1", [P, FC, B])
        mb1_root = sb("mb1_root", [P, FC, B])
        key_sum = late_sb[:, PACK["w1"][1]:PACK["w1"][1] + 4 * S].rearrange("p (n j s) -> p n j s", n=2, j=2)
        rank = sb("rank", [P, NT, E])
        cw_sum = sb("cw_sum", [P, 2, NT])
        stay = sb("stay", [P, NT])

        def row(key):
            at, w = ROWS[key]
            return rows_sb[:, at:at + w]

        ident = pk("ident")
        scratch = nc.dram_tensor("parts_dram", [2, B, 3, DK0, H, S], BF16).ap()

        def ready(eng, kind, *key):
            n, banks = index[kind, key]
            eng.wait_ge(sem(kind + "_filled"), n)
            return banks[0]

        def bank(n, cols=slice(0, 512), parts_=slice(0, P)):
            return psum[parts_, n, cols]

        x_tiles = x.rearrange("(t p) d -> p t d", p=P)
        out_tiles = out.rearrange("(t p) d -> p t d", p=P)

        def load_k_stack(queue, b):
            to, of = k_stack[b % 2], scratch[1, b].rearrange("n d h s -> n d (h s)")
            loaded = sem(f"stack_loaded{b % 2}")
            for at, n in ((0, 1), (2, 2)):
                queue.dma_start(to[at * DK0:(at + 2) * DK0].rearrange("p h s -> p (h s)"),
                                of[n].unsqueeze(0).to_broadcast([2, DK0, H * S])).then_inc(loaded, 16)
            queue.dma_start(to[4 * DK0:ST0].rearrange("p h s -> p (h s)"), of[0::2]).then_inc(loaded, 16)

        def load_q_stack(queue, b):
            to, of = q_stack[b % 2], scratch[0, b].rearrange("n d h s -> n d (h s)")
            loaded = sem(f"stack_loaded{b % 2}")
            queue.dma_start(to[0:4 * DK0].rearrange("p h s -> p (h s)"),
                            of[0:2].rearrange("n d c -> (n d) c").unsqueeze(0).to_broadcast(
                                [2, 2 * DK0, H * S])).then_inc(loaded, 16)
            queue.dma_start(to[4 * DK0:ST0].rearrange("p h s -> p (h s)"), of[0::2]).then_inc(loaded, 16)

        block = ctx.enter_context(nc.Block())

        @block.sync
        def _(sp):
            sp.dma_start(xs[0][:, 0:TB, :], x_tiles[:, 0:TB, :]).then_inc(sem("x_first_loaded"), 16)
            sp.dma_start(early_sb[:, :], early).then_inc(sem("early_loaded"), 16)
            sp.dma_start(ctx_sb[:, 0:S], ctx_t[:, 0:S]).then_inc(sem("ctx_first_loaded"), 16)
            sp.dma_start(xs[0][:, TB:NT, :], x_tiles[:, TB:NT, :]).then_inc(sem("x_loaded"), 16)
            sp.dma_start(ctx_sb[:, S:T], ctx_t[:, S:T]).then_inc(sem("ctx_loaded"), 16)

            def store_parts(b, i):
                for n, name in enumerate("hml"):
                    if n == 0:
                        sp.wait_ge(sem("k0_read_a" if i else "q0_read_a"), b + 1)
                    elif b == 0:
                        sp.wait_ge(sem("part_ready"), 2 * (1 - i) + n)
                    elif b == 1:
                        sp.wait_ge(sem("mid_ready" if n == 1 else "low_ready"), 2 - i)
                    sp.dma_start(scratch[i, b, (Q_SLOT, K_SLOT)[i].index(name)].rearrange("d h s -> h d s"),
                                 part[i][n][:, b * S:(b + 1) * S]).then_inc(sem("qk"[i] + "_stored"), 16)

            def store_maxima(b):
                sp.wait_ge(sem("t0_read_v"), b + 1)
                sp.dma_start(q_stack[b % 2][NM0:P], nmt0[:, :]).then_inc(sem("max0_stored"), 16)

            store_parts(0, 1)
            store_parts(0, 0)
            sp.wait_ge(sem("k_stack_cleared"), 1)
            sp.wait_ge(sem("k_stored"), 3 * 16)
            load_k_stack(sp, 0)
            sp.wait_ge(sem("q_stack_cleared"), 1)
            sp.wait_ge(sem("q_stored"), 3 * 16)
            load_q_stack(sp, 0)
            sp.dma_start(rows_sb[:, :], rows.broadcast_to([P, N_ROWS])).then_inc(sem("rows_loaded"), 16)
            sp.dma_start(late_sb[:, :], late).then_inc(sem("late_loaded"), 16)
            store_parts(1, 1)
            store_parts(1, 0)
            sp.wait_ge(sem("k_stack_cleared"), 2)
            sp.wait_ge(sem("k_stored"), 2 * 3 * 16)
            load_k_stack(sp, 1)
            sp.wait_ge(sem("q_stored"), 2 * 3 * 16)
            load_q_stack(sp, 1)
            store_maxima(0)
            for b in range(2, B):
                store_parts(b, 1)
                store_parts(b, 0)
            sp.wait_ge(sem("k_stored"), B * 3 * 16)
            sp.wait_ge(sem("q_stored"), B * 3 * 16)
            half = tw_sb[0].shape[1] // 2
            tw_halves = [((tw_sb[i][:, j * half:(j + 1) * half], w[:, j * half:(j + 1) * half]), "tw_loaded")
                         for i, w in enumerate((tw1, tw2)) for j in range(2)]
            weights = ((((wv1_sb, wv1), "wv1_loaded"), tw_halves[0]),
                       (((wk1_sb, wk1), "wk1_loaded"), tw_halves[1]),
                       (tw_halves[2], ((wq1_sb, wq1), "wq1_loaded")),
                       (tw_halves[3], ((wo1_sb, wo1), "wo1_loaded"), ((mem_k_sb[0:DK1], mem_k), "mem_k_loaded")))
            for b in range(B):
                if b:
                    store_maxima(b)
                if 0 < b < 3:
                    sp.wait_ge(sem(f"stack_loaded{(b + 1) % 2}"), 5 * 16 * ((b + 1) // 2 + 1))
                for (to, of), loaded in weights[b]:
                    sp.dma_start(to, of).then_inc(sem(loaded), 16)
                if b + 2 < B:
                    sp.wait_ge(sem("s0_filled"), index["s0", (b, H - 1)][0])
                    load_k_stack(sp, b + 2)
                    load_q_stack(sp, b + 2)
            sp.wait_ge(sem("y1_filled"), B)
            sp.dma_start(mem_v_sb, mem_v).then_inc(sem("memv_loaded"), 16)
            for b in range(B):
                sp.wait_ge(sem("t1_read_v"), b + 1)
                sp.dma_start(qa[b % 2][DK1:DK1 + 1], nmt1[:, :]).then_inc(sem("max1_stored"), 16)
            for t in range(NT):
                sp.wait_ge(sem("f3_read_v"), t + 1)
                sp.dma_start(out_tiles[:, t, :], xs[1][:, t, :]).then_inc(sem("out_stored"), 16)
            sp.wait_ge(sem("out_stored"), 16 * NT)

        @block.tensor
        def _(pe):
            def matmul(o, w, m, start=True, stop=True):
                return nc.tensor.matmul(o, w, m, start=start, stop=stop, skip_group_check=True)

            def k0(o, b):
                if b == 0:
                    pe.wait_ge(sem("ctx_first_loaded"), 16)
                    pe.wait_ge(sem("early_loaded"), 16)
                elif b == 1:
                    pe.wait_ge(sem("ctx_loaded"), 16)
                return matmul(bank(o, slice(0, S)), pk("wk0"), ctx_sb[:, b * S:(b + 1) * S])

            def v0_(o, half):
                for t in range(4):
                    at = half * 512 + t * P
                    mm = matmul(bank(o, slice(t * P, (t + 1) * P)), ctx_sb[:, at:at + P], pk("wv0"))
                return mm

            def transposes(layer, o, b):
                pe.wait_ge(sem("xn_ready"), layer * B + b + 1)
                for t in range(TB):
                    mm = nc.tensor.transpose(bank(o, slice(t * P, (t + 1) * P)), xn[:, b * TB + t, :], ident)
                return mm

            def q0(o, b):
                pe.wait_ge(sem("xt0_read_a"), b + 1)
                return matmul(bank(o, slice(0, S)), pk("wq0"), xt[:, b * S:(b + 1) * S])

            def a0(o, b, u):
                if u == 0:
                    pe.wait_ge(sem(f"stack_loaded{b % 2}"), 5 * 16 * (b // 2 + 1))
                hp, qt = u // 2, u % 2
                for j in range(2):
                    h = 2 * hp + j
                    mm = matmul(bank(o, slice(j * S, (j + 1) * S)),
                                q_stack[b % 2][0:NM0, h, qt * P:(qt + 1) * P], k_stack[b % 2][0:NM0, h, :])
                return mm

            def t0(o, b):
                pe.wait_ge(sem("nm_part_ready"), b + 1)
                pe.wait_ge(sem("ident_ready"), 1)
                for qt in range(TB):
                    mm = nc.tensor.transpose(bank(o, slice(0, P), slice(0, 2 * H)).bitcast(BF16)[:, qt * P:(qt + 1) * P],
                                             nm_part[:, qt, :], ident_bf[:, :])
                return mm

            def s0(o, b, h):
                if h == 0:
                    pe.wait_ge(sem("max0_stored"), 16 * (b + 1))
                for kt in range(TB):
                    mm = matmul(bank(o, slice(kt * S, (kt + 1) * S)), k_stack[b % 2][:, h, kt * P:(kt + 1) * P],
                                q_stack[b % 2][:, h, :])
                return mm

            def o0(o, b, g):
                if b == 0 and g == 0:
                    pe.wait_ge(sem("v0_read_v"), 2)
                pe.wait_ge(sem("s0_read_a"), H * b + 4 * g + 4)
                for kt in range(TB):
                    for j in range(4):
                        pair = 8 * b + 2 * g + j // 2
                        mm = matmul(bank(o, slice(0, S), slice(32 * j, 32 * j + 32)),
                                    v0[:, b * TB + kt, 4 * g + j, :], p0[:, pair % 4, j % 2, kt, :],
                                    start=(kt == 0), stop=(kt == TB - 1))
                return mm

            def d0(o, b):
                if b == 0:
                    pe.wait_ge(sem("late_loaded"), 16)
                pe.wait_ge(sem("o0_read_a"), 4 * b + 4)
                for i in range(2):
                    for g in range(4):
                        mm = matmul(bank(o, slice(i * S, (i + 1) * S), slice(32 * g, 32 * g + 32)),
                                    pk("pick")[:, i * 32:(i + 1) * 32], u0[b % 2][:, g * S:(g + 1) * S])
                return mm

            def w0(o, b):
                pe.wait_ge(sem("d0_read_v"), b + 1)
                for t in range(TB):
                    mm = matmul(bank(o, slice(t * P, (t + 1) * P)), heads0[b % 2][:, t * P:(t + 1) * P], pk("wo0"))
                return mm

            def v1_(o, t, half):
                pe.wait_ge(sem("wv1_loaded"), 16)
                return matmul(bank(o), ctx_sb[:, t * P:(t + 1) * P], wv1_sb[:, half * 512:(half + 1) * 512])

            def k1(o, b, c):
                pe.wait_ge(sem("wk1_loaded"), 16)
                return matmul(bank(o, slice(0, S)), wk1_sb[:, c * P:(c + 1) * P], ctx_sb[:, b * S:(b + 1) * S])

            def g1(o, b):
                pe.wait_ge(sem("xt1_read_a"), b + 1)
                return matmul(bank(o, slice(0, S)), pk("gw1"), xt[:, b * S:(b + 1) * S])

            def gc(o):
                pe.wait_ge(sem("g1_read_a"), B)
                return matmul(bank(o, slice(0, B)), pk("gw2"), hsum[:, :])

            def mb(o):
                pe.wait_ge(sem("gc_read_v"), 1)
                for c in range(FC):
                    mm = matmul(bank(o, slice(c * B, (c + 1) * B)), pk("tb1")[:, c * P:(c + 1) * P], gcol[:, :])
                return mm

            def merge(i, o, k):
                if i == 0 and k == 0:
                    pe.wait_ge(sem("tw_loaded"), 4 * 16)
                    pe.wait_ge(sem("gdiag_ready"), 1)
                for n in range(8):
                    at = (k * 8 + n) * P if i == 0 else (n * FC + k) * P
                    mm = matmul(bank(o, slice(n * B * J, (n + 1) * B * J)), tw_sb[i][:, at:at + P],
                                gdiag[:, :, :].rearrange("p b j -> p (b j)"))
                return mm

            def u1(o, b, c2):
                if b == 0 and c2 == 0:
                    pe.wait_ge(sem("m1_read_v"), 4)
                for j in range(2):
                    c = 2 * c2 + j
                    mm = matmul(bank(o, slice(j * S, (j + 1) * S)), mw1[:, b, c * P:(c + 1) * P],
                                xt[:, b * S:(b + 1) * S])
                return mm

            def y1(o, b):
                if b == 0:
                    pe.wait_ge(sem("m2_read_v"), 4)
                pe.wait_ge(sem("ffy_ready"), b + 1)
                for t in range(TB):
                    for c in range(FC):
                        matmul(bank(o, slice(t * P, (t + 1) * P)), ff_y[b][:, c * S + t * P:c * S + (t + 1) * P],
                               mw2[:, c, b, :], start=(c == 0), stop=False)
                    mm = matmul(bank(o, slice(t * P, (t + 1) * P)), gwide[:, b, :], pk("tb2"), start=False)
                return mm

            def q1(o, b, c):
                pe.wait_ge(sem("wq1_loaded"), 16)
                pe.wait_ge(sem("xt2_read_a"), b + 1)
                return matmul(bank(o, slice(0, S)), wq1_sb[:, c * P:(c + 1) * P], xt[:, b * S:(b + 1) * S])

            def tops(ap):
                return ap.bitcast(BF16)[:, 1::2]

            def a1(o, b, h, qt):
                for kind in ("q1", "k1"):
                    who = "v" if h % 2 and (kind, (b, h // 2), "v") in when_read else "a"
                    pe.wait_ge(sem(f"{kind}_read_{who}"), when_read[kind, (b, h // 2), who])
                pe.wait_ge(sem("mem_k_loaded"), 16)
                w = tops(qa[b % 2][0:DK1, h, qt * P:(qt + 1) * P])
                matmul(bank(o, slice(0, S)), w, tops(kb[b % 2][0:DK1, h, :]))
                return matmul(bank(o, slice(S, S + MEM)), w, tops(mem_k_sb[0:DK1, h, :]))

            def t1(o, b):
                pe.wait_ge(sem("a1_read_v"), H * TB * (b + 1))
                for qt in range(TB):
                    mm = nc.tensor.transpose(bank(o, slice(qt * P, (qt + 1) * P), slice(0, H)),
                                             neg_max[:, b % 2, qt, :], ident)
                return mm

            def s1(o, b, h):
                if h == 0:
                    pe.wait_ge(sem("max1_stored"), 16 * (b + 1))
                    pe.wait_ge(sem("kb_ones"), 2)
                for kt in range(KT1):
                    w = kb[b % 2][:, h, kt * P:(kt + 1) * P] if kt < TB else mem_k_sb[:, h, :]
                    mm = matmul(scores1[:, h % 2, kt * S:(kt + 1) * S], w, qa[b % 2][:, h, :])
                return mm

            def o1(o, b, hp):
                pe.wait_ge(sem("s1_read_a"), H * b + 2 * hp + 2)
                if b == 0 and hp == 0:
                    pe.wait_ge(sem("memv_loaded"), 16)
                    pe.wait_ge(sem("ones64_ready"), 1)
                for kt in range(KT1):
                    for j in range(2):
                        h = 2 * hp + j
                        w = v1[:, b * TB + kt] if kt < TB else mem_v_sb
                        matmul(bank(o, slice(0, S), slice(j * DK1, (j + 1) * DK1)), w[:, h * DK1:(h + 1) * DK1],
                               p1[:, (H * b + h) % 4, kt, :], start=(kt == 0), stop=(kt == KT1 - 1))
                pe.wait_ge(sem("key_sum_ready"), H // 2 * b + hp + 1)
                for j in range(2):
                    mm = matmul(bank(o, slice(S, 2 * S), slice(j * DK1, (j + 1) * DK1)), ones64[:, :],
                                key_sum[:, hp % 2, j, :])
                return mm

            def w1(o, b):
                pe.wait_ge(sem("wo1_loaded"), 16)
                for c in range(H // 2):
                    pe.wait_ge(sem("o1_read_v"), (H // 2) * b + c + 1)
                    for t in range(TB):
                        mm = matmul(bank(o, slice(t * P, (t + 1) * P)), ct1[b % 2][:, c, t * P:(t + 1) * P],
                                    wo1_sb[:, c * D:(c + 1) * D], start=(c == 0 and t == 0),
                                    stop=(c == H // 2 - 1))
                return mm

            def rt(o, b):
                pe.wait_ge(sem("xt3_read_a"), b + 1)
                for t in range(TB):
                    at = (b * TB + t) * P
                    mm = matmul(bank(o, slice(t * E, (t + 1) * E)), xt[:, at:at + P], pk("wr"))
                return mm

            def gu(o, t):
                return matmul(bank(o), xt[:, t * P:(t + 1) * P], pk("wgu"))

            def ht(o, t):
                pe.wait_ge(sem("hid_ready"), t + 1)
                for c in range(2):
                    mm = nc.tensor.transpose(bank(o, slice(c * P, (c + 1) * P)), hid[t % 2][:, c * P:(c + 1) * P],
                                             ident)
                return mm

            def f3(o, t):
                if t < NT - TB:
                    pe.wait_ge(sem("conv_ready"), t // TB + 1)
                else:
                    pe.wait_ge(sem("last_conv_ready"), 1)
                matmul(bank(o, slice(0, D)), conv[:, t * P:(t + 1) * P], ident, stop=False)
                pe.wait_ge(sem("ht_read_a"), t + 1)
                for c in range(2):
                    mm = matmul(bank(o, slice(0, D)), hidt[t % 2][:, c * P:(c + 1) * P],
                                pk("wd")[:, c * D:(c + 1) * D], start=False, stop=(c == 1))
                return mm

            emit = {
                "k0": k0, "v0": v0_, "q0": q0, "a0": a0, "t0": t0, "s0": s0, "o0": o0, "d0": d0, "w0": w0,
                "v1": v1_, "k1": k1, "g1": g1, "gc": gc, "mb": mb, "u1": u1, "y1": y1, "q1": q1, "a1": a1, "t1": t1,
                "s1": s1, "o1": o1, "w1": w1, "rt": rt, "gu": gu, "ht": ht, "f3": f3,
                "m1": lambda o, k: merge(0, o, k), "m2": lambda o, k: merge(1, o, k),
                "xt0": lambda o, h: transposes(0, o, h), "xt1": lambda o, h: transposes(1, o, h),
                "xt2": lambda o, h: transposes(2, o, h), "xt3": lambda o, h: transposes(3, o, h),
            }
            for (kind, key, banks, _), earlier in zip(units, before):
                if not banks:
                    continue
                for reads in earlier:
                    for name, n in reads or ():
                        pe.wait_ge(sem(name), n)
                emit[kind](banks[0], *key).then_inc(sem(kind + "_filled"), 1)

        @block.scalar
        def _(act):
            def done(ins, kind):
                return ins.then_inc(sem(kind + "_read_a"), 1)

            for kind, key, banks, readers in units:
                if "a" not in readers:
                    continue
                o = ready(act, kind, *key) if banks else None
                if kind in ("k0", "q0"):
                    i, b = (1 if kind == "k0" else 0), key[0]
                    for to in (qk_f[i], part[i][0]):
                        ins = nc.scalar.activation(to[:, b * S:(b + 1) * S], bank(o, slice(0, S)), ACT.Identity,
                                                   bias=pk("bk0" if i else "bq0"))
                    done(ins, kind)
                elif kind == "mid":
                    i = key[0]
                    act.wait_ge(sem("rest_ready"), 2 - i)
                    nc.scalar.activation(part[i][1][:, S:T], rest[i][:, S:T], ACT.Copy).then_inc(sem("mid_ready"), 1)
                elif kind in ("xt0", "xt1", "xt2", "xt3"):
                    layer, b = int(kind[2]), key[0]
                    if layer == 1:
                        act.wait_ge(sem("q0_filled"), b + 1)
                    if layer == 2:
                        act.wait_ge(sem("u1_filled"), 2 * (b + 1))
                    if layer == 3:
                        act.wait_ge(sem("q1_filled"), index["q1", (b, H // 2 - 1)][0])
                    done(nc.scalar.activation(xt[:, b * S:(b + 1) * S], bank(o, slice(0, S)), ACT.Copy), kind)
                elif kind == "s0":
                    b, h = key
                    n = H * b + h
                    if n >= 8:
                        act.wait_ge(sem("o0_filled"), (n - 8) // 4 + 1)
                    nc.scalar.activation(p0[:, n // 2 % 4, n % 2].rearrange("p k s -> p (k s)"), bank(o), ACT.Exp,
                                         scale=float(DK0) ** -0.5).then_inc(sem("s0_read_a"), 1)
                elif kind == "o0":
                    b, g = key
                    if b >= 2 and g == 0:
                        act.wait_ge(sem("d0_filled"), b - 1)
                    nc.scalar.activation(u0[b % 2][:, g * S:(g + 1) * S], bank(o, slice(0, S)),
                                         ACT.Copy).then_inc(sem("o0_read_a"), 1)
                elif kind == "g1":
                    b = key[0]
                    if b:
                        act.wait_ge(sem("g1_read_a"), b)
                    done(nc.scalar.activation(gate_relu, bank(o, slice(0, S)), ACT.Relu, bias=pk("gb1"),
                                              accum_out=hsum[:, b:b + 1]), kind)
                elif kind in ("k1", "q1"):
                    b, c = key
                    if kind == "k1" and b == 0 and c == 0:
                        act.wait_ge(sem("s0_filled"), B * H)
                    if kind == "q1" and c == 0 and b < 2:
                        act.wait_ge(sem("m2_filled"), 4)
                        if b:
                            act.wait_ge(sem("y1_filled"), B)
                    if b >= 2:
                        act.wait_ge(sem("s1_filled"), index["s1", (b - 2, 2 * c)][0])
                    to = (kb if kind == "k1" else qa)[b % 2]
                    bias = pk("bk1" if kind == "k1" else "bq1")
                    for j in range(2 if readers == "a" else 1):
                        rows_ = slice(j * DK1, (j + 1) * DK1)
                        ins = nc.scalar.activation(to[0:DK1, 2 * c + j, :], bank(o, slice(0, S), rows_), ACT.Identity,
                                                   bias=bias[rows_, c:c + 1])
                    done(ins, kind)
                elif kind == "u1":
                    b, c2 = key
                    if b == 0 and c2 == 0:
                        act.wait_ge(sem("mb_read_v"), 1)
                        act.wait_ge(sem("w0_filled"), B)
                        act.wait_ge(sem("m1_filled"), 4)
                    for j in range(2):
                        c = 2 * c2 + j
                        of = bank(o, slice(j * S, (j + 1) * S))
                        nc.scalar.activation(ff_u[b][:, c * S:(c + 1) * S], of, ACT.Identity, bias=mb1[:, c, b:b + 1])
                        ins = nc.scalar.activation(ff_y[b][:, c * S:(c + 1) * S], of, ACT.Square,
                                                   bias=mb1_root[:, c, b:b + 1], scale=CUBIC ** 0.5)
                    ins.then_inc(sem("u1_read_a"), 1)
                elif kind == "tanh":
                    b = key[0]
                    act.wait_ge(sem("cubic_ready"), b + 1)
                    nc.scalar.activation(ff_y[b], ff_y[b], ACT.Tanh,
                                         scale=0.7978845608028654).then_inc(sem("tanh_ready"), 1)
                elif kind == "s1":
                    b, h = key
                    n = H * b + h
                    if n >= 4:
                        act.wait_ge(sem("o1_filled"), (n - 4) // 2 + 1)
                    elif n == 0:
                        act.wait_ge(sem("y1_filled"), B)
                    nc.scalar.activation(p1[:, n % 4].rearrange("p k s -> p (k s)"),
                                         scores1[:, h % 2, :], ACT.Exp,
                                         scale=float(DK1) ** -0.5).then_inc(sem("s1_read_a"), 1)
                elif kind == "rt":
                    b = key[0]
                    if b == 0:
                        act.wait_ge(sem("s1_filled"), (B - 1) * H)
                    nc.scalar.activation(router[:, 0, b * TB:(b + 1) * TB].rearrange("p t e -> p (t e)"),
                                         bank(o, slice(0, TB * E)), ACT.Tanh, scale=0.5).then_inc(sem("rt_read_a"), 1)
                elif kind == "gu":
                    t = key[0]
                    if t >= 2:
                        act.wait_ge(sem("gu_read_v"), t - 1)
                    nc.scalar.activation(gu_t[t % 2], bank(o, slice(0, 256)), ACT.Tanh,
                                         scale=0.5).then_inc(sem("gu_read_a"), 1)
                elif kind == "ht":
                    t = key[0]
                    if t >= 2:
                        act.wait_ge(sem("f3_filled"), t - 1)
                    nc.scalar.activation(hidt[t % 2], bank(o, slice(0, 256)), ACT.Copy).then_inc(sem("ht_read_a"), 1)

        @block.gpsimd
        def _(pool):
            steps = [0]

            def then(ins):
                steps[0] += 1
                ins.then_inc(sem("pool_step"), 1)
                pool.wait_ge(sem("pool_step"), steps[0])

            then(nc.gpsimd.memset(minus_half[:, :], -0.5))

            def inverse_root(layer, b):
                if layer * B + b:
                    pool.wait_ge(sem("rstd_ready"), layer * B + b)
                t = slice(b * TB, (b + 1) * TB)
                pool.wait_ge(sem("mv_ready"), layer * B + b + 1)
                then(nc.gpsimd.tensor_scalar(veps[:, t], mv[:, t, 1], EPS, None, ALU.add))
                nc.gpsimd.tensor_tensor(rstd[:, t], veps[:, t], minus_half[:, t], ALU.pow).then_inc(sem("rstd_ready"), 1)

            def clear_keys(i):
                words = r_k[:, (2 + i) * half_k:(3 + i) * half_k]
                then(nc.gpsimd.memset(words, 0.0))
                nc.gpsimd.memset(r_k[96:P, (2 + i) * half_k:(3 + i) * half_k], BF16_ONES).then_inc(
                    sem("k_stack_cleared"), 1)
                pool.wait_ge(sem("k_stack_cleared"), i + 1)

            def less_first(i):
                pool.wait_ge(sem("k0_read_a" if i else "q0_read_a"), B)
                nc.gpsimd.tensor_tensor(rest[i][:, S:T], qk_f[i][:, S:T], part[i][0][:, S:T], ALU.subtract).then_inc(
                    sem("rest_ready"), 1)
                pool.wait_ge(sem("rest_ready"), 2 - i)

            def less_second(i):
                pool.wait_ge(sem("mid_ready"), 2 - i)
                nc.gpsimd.tensor_tensor(part[i][2][:, S:T], rest[i][:, S:T], part[i][1][:, S:T],
                                        ALU.subtract).then_inc(sem("low_ready"), 1)
                pool.wait_ge(sem("low_ready"), 2 - i)

            clear_keys(0)
            for b in range(B):
                inverse_root(0, b)
            pool.wait_ge(sem("rstd_ready"), B)
            less_first(1)
            clear_keys(1)
            less_second(1)
            less_first(0)
            nc.gpsimd.memset(ones64[:, :], 1.0).then_inc(sem("ones64_ready"), 1)
            pool.wait_ge(sem("ones64_ready"), 1)
            less_second(0)
            nc.gpsimd.memset(v0[:, :, :, :].rearrange("p t h e -> p (t h e)"), 1.0).then_inc(sem("v0_ones"), 1)
            pool.wait_ge(sem("v0_ones"), 1)
            pool.wait_ge(sem("k_stored"), B * 3 * 16)
            pool.wait_ge(sem("q_stored"), B * 3 * 16)
            then(nc.gpsimd.memset(mem_k_sb[DK1:P], 0.0))
            then(nc.gpsimd.memset(mem_k_sb[DK1:DK1 + 1], 1.0))
            pool.wait_ge(sem("rows_loaded"), 16)

            def add_bias(layer, b, key):
                for t in range(b * TB, (b + 1) * TB):
                    ins = nc.gpsimd.tensor_tensor(xb[layer][:, t, :], xs[layer][:, t, :], row(key), ALU.add)
                ins.then_inc(sem("bias_added"), 1)

            for b in range(B):
                pool.wait_ge(sem("xn_ready"), b + 1)
                add_bias(0, b, "bo0")
            for b in range(B):
                inverse_root(1, b)
                pool.wait_ge(sem("xn_ready"), B + b + 1)
                add_bias(1, b, "b2")
            pool.wait_ge(sem("s0_filled"), B * H)
            pool.wait_ge(sem("bias_added"), 2 * B)
            for i in range(2):
                then(nc.gpsimd.memset(r_k[96:P, (2 * i) * half_k:(2 * i + 2) * half_k], 0.0))
                nc.gpsimd.memset(kb[i][DK1:DK1 + 1], 1.0).then_inc(sem("kb_ones"), 1)
                pool.wait_ge(sem("kb_ones"), i + 1)

            for b in range(B):
                inverse_root(2, b)
                pool.wait_ge(sem("xn_ready"), 2 * B + b + 1)
                add_bias(2, b, "bo1")

            def finish_layer(b):
                inverse_root(3, b)
                pool.wait_ge(sem("xn_ready"), 3 * B + b + 1)
                add_bias(3, b, "convb")
                pool.wait_ge(sem("bias_added"), 3 * B + b + 1)

            pool.wait_ge(sem("y1_filled"), B)
            for b in range(B):
                for hp in range(H // 2):
                    pair = H // 2 * b + hp
                    pool.wait_ge(sem("s1_read_a"), 2 * pair + 2)
                    if pair >= 2:
                        pool.wait_ge(sem("o1_filled"), pair - 1)
                    n = 2 * (pair % 2)
                    to = key_sum[:, pair % 2]
                    then(nc.gpsimd.tensor_tensor(to, p1[:, n:n + 2, 0, :], p1[:, n:n + 2, 1, :], ALU.add))
                    nc.gpsimd.tensor_tensor(to, to, p1[:, n:n + 2, 2, :], ALU.add).then_inc(sem("key_sum_ready"), 1)
                    if b and hp == 2:
                        finish_layer(b - 1)
            finish_layer(B - 1)

            pool.wait_ge(sem("xt3_read_a"), B)
            of, to, term = xt[:, T - S:T], conv[:, T - S:T], key_sum[:, 0, 0, :]
            then(nc.gpsimd.tensor_scalar(to, of, pk("convw")[:, KC - 1:KC], None, ALU.mult))
            for k in range(KC - 1):
                back = KC - 1 - k
                then(nc.gpsimd.tensor_scalar(term, of, pk("convw")[:, k:k + 1], None, ALU.mult))
                ins = nc.gpsimd.tensor_tensor(to[:, back:], to[:, back:], term[:, 0:S - back], ALU.add)
                if k < KC - 2:
                    then(ins)
            ins.then_inc(sem("last_conv_ready"), 1)

        @block.vector
        def _(dve):
            steps = [0]

            def then(ins):
                steps[0] += 1
                ins.then_inc(sem("vector_step"), 1)
                dve.wait_ge(sem("vector_step"), steps[0])

            def signal(ins, kind):
                return ins.then_inc(sem(kind + "_read_v"), 1)

            def moments(layer, b):
                src = xs[layer]
                for t in range(b * TB, (b + 1) * TB):
                    ins = nc.vector.bn_stats(stats[:, t, :], src[:, t, :])
                then(ins)
                for t in range(b * TB, (b + 1) * TB):
                    ins = nc.vector.bn_aggr(mv[:, t, :], stats[:, t, :])
                ins.then_inc(sem("mv_ready"), 1)

            def normalise(layer, b):
                dve.wait_ge(sem("rstd_ready"), layer * B + b + 1)
                if layer:
                    dve.wait_ge(sem(f"xt{layer - 1}_filled"), b + 1)
                for t in range(b * TB, (b + 1) * TB):
                    ins = nc.vector.tensor_scalar(xn[:, t, :], xs[layer][:, t, :], mv[:, t, 0:1], rstd[:, t:t + 1],
                                                  ALU.subtract, ALU.mult)
                ins.then_inc(sem("xn_ready"), 1)

            def split(i):
                dve.wait_ge(sem("k0_read_a" if i else "q0_read_a"), 1)
                of, (high, mid, low) = qk_f[i][:, 0:S], (part[i][n][:, 0:S] for n in range(3))
                then(nc.vector.tensor_tensor(rest[i][:, 0:S], of, high, ALU.subtract))
                nc.vector.tensor_copy(mid, rest[i][:, 0:S]).then_inc(sem("part_ready"), 1)
                dve.wait_ge(sem("part_ready"), 2 * (1 - i) + 1)
                nc.vector.tensor_tensor(low, rest[i][:, 0:S], mid, ALU.subtract).then_inc(sem("part_ready"), 1)

            nc.vector.memset(r_k[:, 0:2 * half_k], 0.0).then_inc(sem("q_stack_cleared"), 1)
            dve.wait_ge(sem("early_loaded"), 16)
            nc.vector.tensor_copy(ident_bf[:, :], ident).then_inc(sem("ident_ready"), 1)

            def cubic(b):
                dve.wait_ge(sem("u1_read_a"), 2 * b + 2)
                nc.vector.scalar_tensor_tensor(ff_y[b], ff_y[b], 1.0, ff_u[b], ALU.add, ALU.mult).then_inc(
                    sem("cubic_ready"), 1)

            def gate(b):
                dve.wait_ge(sem("tanh_ready"), b + 1)
                nc.vector.scalar_tensor_tensor(ff_y[b], ff_y[b], 1.0, ff_u[b], ALU.add, ALU.mult).then_inc(
                    sem("ffy_ready"), 1)

            def routing(b):
                tiles = slice(b * TB, (b + 1) * TB)
                s, biased, chosen, cw = (router[:, i, tiles] for i in range(4))
                dve.wait_ge(sem("rt_read_a"), b + 1)
                then(nc.vector.tensor_scalar(s, s, 0.5, 0.5, ALU.mult, ALU.add))
                then(nc.vector.tensor_tensor(biased, s, row("rb").unsqueeze(1).to_broadcast([P, TB, E]), ALU.add))
                other = biased.unsqueeze(2).to_broadcast([P, TB, E, E])
                mine = biased.unsqueeze(3).to_broadcast([P, TB, E, E])
                nc.vector.tensor_tensor(cmp_gt, other, mine, ALU.is_gt)
                then(nc.vector.tensor_tensor(cmp_eq, other, mine, ALU.is_equal))
                then(nc.vector.tensor_tensor(cmp_eq.rearrange("p t i j -> p t (i j)"),
                                             cmp_eq.rearrange("p t i j -> p t (i j)"),
                                             pk("before").unsqueeze(1).to_broadcast([P, TB, E * E]), ALU.mult))
                then(nc.vector.tensor_tensor(cmp_gt.rearrange("p t i j -> p (t i j)"),
                                             cmp_gt.rearrange("p t i j -> p (t i j)"),
                                             cmp_eq.rearrange("p t i j -> p (t i j)"), ALU.add))
                then(nc.vector.tensor_reduce(rank[:, tiles], cmp_gt, AX.X, ALU.add))
                then(nc.vector.tensor_scalar(chosen, rank[:, tiles], 1.5, None, ALU.is_lt))
                then(nc.vector.tensor_tensor(cw, s, chosen, ALU.mult))
                total, inverse = cw_sum[:, 0, tiles], cw_sum[:, 1, tiles]
                then(nc.vector.tensor_reduce(total, cw, AX.X, ALU.add))
                then(nc.vector.tensor_scalar(total, total, 1e-9, None, ALU.add))
                then(nc.vector.reciprocal(inverse, total))
                then(nc.vector.tensor_tensor(cw, cw, inverse.unsqueeze(2).to_broadcast([P, TB, E]), ALU.mult))
                nc.vector.tensor_tensor(stay[:, tiles], cw[:, :, EM], cw[:, :, EM + 2], ALU.add)
                nc.vector.tensor_scalar(cw[:, :, 0:EM], cw[:, :, 0:EM], 0.5, None, ALU.mult).then_inc(
                    sem("route_ready"), 1)

            def convolve(b):
                dve.wait_ge(sem("xt3_read_a"), b + 1)
                if b == 0:
                    dve.wait_ge(sem("s1_filled"), (B - 1) * H)
                of, to = xt[:, b * S:(b + 1) * S], conv[:, b * S:(b + 1) * S]
                then(nc.vector.tensor_scalar(to, of, pk("convw")[:, KC - 1:KC], None, ALU.mult))
                for k in range(KC - 1):
                    back = KC - 1 - k
                    ins = nc.vector.scalar_tensor_tensor(to[:, back:], of[:, 0:S - back], pk("convw")[:, k:k + 1],
                                                         to[:, back:], ALU.mult, ALU.add)
                    if k < KC - 2:
                        then(ins)
                ins.then_inc(sem("conv_ready"), 1)

            def pass_through(b):
                dve.wait_ge(sem("route_ready"), b + 1)
                dve.wait_ge(sem("bias_added"), 3 * B + b + 1)
                both = slice(b * TB, (b + 1) * TB)
                for t in range(b * TB, (b + 1) * TB):
                    nc.vector.scalar_tensor_tensor(xs[2][:, t, :], xn[:, t, :], stay[:, t:t + 1], xs[3][:, t, :],
                                                   ALU.mult, ALU.add)
                for t in range(b * TB, (b + 1) * TB):
                    ins = nc.vector.tensor_scalar(xn[:, t, :], xn[:, t, :], 0.0, router[:, 3, t, EM + 3:EM + 4],
                                                  ALU.max, ALU.mult)
                then(ins)
                nc.vector.tensor_tensor(xs[2][:, both, :], xs[2][:, both, :], xn[:, both, :], ALU.add).then_inc(
                    sem("pass_ready"), 1)

            for kind, key, banks, readers in units:
                if "v" not in readers:
                    continue
                o = ready(dve, kind, *key) if banks else None
                if kind == "moments":
                    layer, b = key
                    if layer:
                        dve.wait_ge(sem("w0_read_v"), b + 1)
                    else:
                        dve.wait_ge(sem("x_loaded" if b else "x_first_loaded"), 16)
                    moments(layer, b)
                elif kind == "norm":
                    normalise(*key)
                elif kind == "split":
                    split(*key)
                elif kind == "cubic":
                    cubic(*key)
                elif kind == "gate":
                    gate(*key)
                elif kind == "route":
                    routing(*key)
                elif kind == "conv":
                    convolve(*key)
                elif kind == "pass":
                    pass_through(*key)
                elif kind == "v0":
                    half = key[0]
                    dve.wait_ge(sem("rows_loaded"), 16)
                    dve.wait_ge(sem("v0_ones"), 1)
                    for t in range(4):
                        ins = nc.vector.tensor_tensor(
                            v0[:, half * 4 + t, :, 0:DK0],
                            bank(o, slice(t * P, (t + 1) * P)).rearrange("p (h d) -> p h d", h=H),
                            row("bv0").rearrange("p (h d) -> p h d", h=H), ALU.add)
                    ins.then_inc(sem("v0_read_v"), 1)
                elif kind == "a0":
                    b, u = key
                    hp, qt = u // 2, u % 2
                    signal(nc.vector.tensor_reduce(neg_max[:, b % 2, qt, 2 * hp:2 * hp + 2],
                                                   bank(o).rearrange("p (j s) -> p j s", j=2), AX.X, ALU.max,
                                                   negate=True), kind)
                elif kind == "parts0":
                    b = key[0]
                    nm = neg_max[:, b % 2]
                    dve.wait_ge(sem("a0_read_v"), H * (b + 1))
                    if b:
                        dve.wait_ge(sem("t0_filled"), b)
                    then(nc.vector.tensor_copy(nm_part[:, :, 0:H], nm))
                    then(nc.vector.tensor_tensor(nm_rest[:, :, :], nm, nm_part[:, :, 0:H], ALU.subtract))
                    nc.vector.tensor_copy(nm_part[:, :, H:2 * H], nm_rest[:, :, :]).then_inc(sem("nm_part_ready"), 1)
                elif kind == "t0":
                    b = key[0]
                    if b:
                        dve.wait_ge(sem("max0_stored"), 16 * b)
                    signal(nc.vector.tensor_copy(nmt0[:, :], bank(o, slice(0, P), slice(0, 2 * H)).bitcast(BF16)),
                           kind)
                elif kind == "d0":
                    b = key[0]
                    if b:
                        dve.wait_ge(sem("d0_read_v"), b)
                        if b >= 2:
                            dve.wait_ge(sem("w0_filled"), b - 1)
                    then(nc.vector.reciprocal(rden0, bank(o, slice(S, 2 * S))))
                    signal(nc.vector.tensor_tensor(heads0[b % 2], bank(o, slice(0, S)), rden0, ALU.mult), kind)
                elif kind in ("w0", "w1"):
                    b, layer = key[0], 0 if kind == "w0" else 2
                    dve.wait_ge(sem("bias_added"), layer * B + b + 1)
                    signal(nc.vector.tensor_tensor(
                        xs[layer + 1][:, b * TB:(b + 1) * TB, :].rearrange("p t d -> p (t d)"), bank(o, slice(0, S)),
                        xb[layer][:, b * TB:(b + 1) * TB, :].rearrange("p t d -> p (t d)"), ALU.add), kind)
                    if layer:
                        dve.wait_ge(sem(kind + "_read_v"), b + 1)
                        moments(layer + 1, b)
                elif kind == "v1":
                    t, half = key
                    cols = slice(half * 512, (half + 1) * 512)
                    if t < B:
                        dve.wait_ge(sem("o0_filled"), 4 * (t + 1))
                    signal(nc.vector.tensor_tensor(v1[:, t, cols], bank(o), row("bv1")[:, cols], ALU.add), kind)
                elif kind in ("k1", "q1"):
                    b, c = key
                    if kind == "k1" and b == 0 and c == 0:
                        dve.wait_ge(sem("s0_filled"), B * H)
                    if kind == "q1" and c == 0 and b < 2:
                        dve.wait_ge(sem("m2_filled"), 4)
                        if b:
                            dve.wait_ge(sem("y1_filled"), B)
                    if b >= 2:
                        dve.wait_ge(sem("s1_filled"), index["s1", (b - 2, 2 * c + 1)][0])
                    to = (kb if kind == "k1" else qa)[b % 2]
                    signal(nc.vector.tensor_scalar(to[0:DK1, 2 * c + 1, :], bank(o, slice(0, S), slice(DK1, P)),
                                                   pk("bk1" if kind == "k1" else "bq1")[DK1:P, c:c + 1], None,
                                                   ALU.add), kind)
                elif kind == "gc":
                    signal(nc.vector.tensor_scalar(gcol[:, :], bank(o, slice(0, B)), 1.0 / S, pk("gb2"), ALU.mult,
                                                   ALU.add), kind)
                    dve.wait_ge(sem("gc_read_v"), 1)
                    for b in range(B):
                        ins = nc.vector.tensor_scalar(gdiag[:, b, :], pk("delta"), gcol[:, b:b + 1], None, ALU.mult)
                    ins.then_inc(sem("gdiag_ready"), 1)
                    for b in range(B):
                        ins = nc.vector.tensor_scalar(gwide[:, b, :], ident, 0.0, gcol[:, b:b + 1], ALU.mult, ALU.add)
                    then(ins)
                    ins = nc.vector.tensor_scalar(gwide[:, :, :].rearrange("p b n -> p (b n)"),
                                                  gwide[:, :, :].rearrange("p b n -> p (b n)"), 2.0, None, ALU.mult)
                    then(ins)
                elif kind == "mb":
                    signal(nc.vector.tensor_tensor(mb1[:, :, :], bank(o, slice(0, FC * B)).rearrange(
                        "p (c b) -> p c b", c=FC), pk("b1").unsqueeze(2).to_broadcast([P, FC, B]), ALU.add), "mb_sum")
                    dve.wait_ge(sem("mb_sum_read_v"), 1)
                    signal(nc.vector.tensor_scalar(mb1_root[:, :, :], mb1[:, :, :], CUBIC ** 0.5, None, ALU.mult), kind)
                elif kind == "m1":
                    k = key[0]
                    if k == 0:
                        dve.wait_ge(sem("o0_filled"), 4 * B)
                    signal(nc.vector.tensor_tensor(
                        mw1[:, :, k * P:(k + 1) * P].rearrange("p b (c j) -> p c b j", j=J),
                        bank(o).rearrange("p (c b j) -> p c b j", b=B, j=J),
                        pk("w1")[:, k * P:(k + 1) * P].rearrange("p (c j) -> p c j", j=J).unsqueeze(2).to_broadcast(
                            [P, 8, B, J]), ALU.add), kind)
                elif kind == "m2":
                    k = key[0]
                    signal(nc.vector.tensor_tensor(
                        mw2[:, k, :, :].rearrange("p b (j n) -> p n b j", n=8),
                        bank(o).rearrange("p (n b j) -> p n b j", b=B, j=J),
                        pk("w2")[:, k * D:(k + 1) * D].rearrange("p (j n) -> p n j", n=8).unsqueeze(2).to_broadcast(
                            [P, 8, B, J]), ALU.add), kind)
                elif kind == "y1":
                    b = key[0]
                    dve.wait_ge(sem("bias_added"), B + b + 1)
                    signal(nc.vector.scalar_tensor_tensor(
                        xs[2][:, b * TB:(b + 1) * TB, :].rearrange("p t d -> p (t d)"), bank(o, slice(0, S)), 0.5,
                        xb[1][:, b * TB:(b + 1) * TB, :].rearrange("p t d -> p (t d)"), ALU.mult, ALU.add), kind)
                    dve.wait_ge(sem("y1_read_v"), b + 1)
                    moments(2, b)
                elif kind == "a1":
                    b, h, qt = key
                    if b >= 2 and h == 0 and qt == 0:
                        dve.wait_ge(sem("t1_filled"), b - 1)
                    signal(nc.vector.tensor_reduce(neg_max[:, b % 2, qt, h:h + 1], bank(o, slice(0, S + MEM)), AX.X,
                                                   ALU.max, negate=True), kind)
                elif kind == "t1":
                    b = key[0]
                    if b:
                        dve.wait_ge(sem("max1_stored"), 16 * b)
                    signal(nc.vector.tensor_copy(nmt1[:, :], bank(o, slice(0, S), slice(0, H))), kind)
                elif kind == "head_out":
                    b, hp = key
                    o = ready(dve, "o1", b, hp)
                    if b == 0 and hp == 0:
                        dve.wait_ge(sem("y1_filled"), B)
                    if b >= 2 and hp == 0:
                        dve.wait_ge(sem("w1_filled"), b - 1)
                    rd = rden1[:, hp % 2, :]
                    then(nc.vector.reciprocal(rd, bank(o, slice(S, 2 * S))))
                    signal(nc.vector.tensor_tensor(ct1[b % 2][:, hp, :], bank(o, slice(0, S)), rd, ALU.mult), "o1")
                elif kind == "gu":
                    t = key[0]
                    gt, w = gu_t[t % 2], gu_w[t % 2]
                    dve.wait_ge(sem("gu_read_a"), t + 1)
                    then(nc.vector.scalar_tensor_tensor(w, gt, 1.0, bank(o, slice(0, 256)), ALU.add, ALU.mult))
                    if t >= 2:
                        dve.wait_ge(sem("hid_ready"), t - 1)
                    signal(nc.vector.tensor_tensor(w, w, bank(o, slice(256, 512)), ALU.mult), kind)
                elif kind == "weigh":
                    t = key[0]
                    dve.wait_ge(sem("route_ready"), t // TB + 1)
                    dve.wait_ge(sem("gu_read_v"), t + 1)
                    if t >= 2:
                        dve.wait_ge(sem("ht_filled"), t - 1)
                    w = gu_w[t % 2]
                    nc.vector.tensor_tensor(
                        hid[t % 2].rearrange("p (e i) -> p e i", e=EM), w.rearrange("p (e i) -> p e i", e=EM),
                        router[:, 3, t, 0:EM].unsqueeze(2).to_broadcast([P, EM, EI]), ALU.mult).then_inc(
                            sem("hid_ready"), 1)
                elif kind == "f3":
                    t = key[0]
                    dve.wait_ge(sem("pass_ready"), t // TB + 1)
                    y = xs[1][:, t, :]
                    signal(nc.vector.tensor_tensor(y, bank(o, slice(0, D)), xs[2][:, t, :], ALU.add), kind)


def _layout(inp):
    g = {k: np.ascontiguousarray(np.asarray(v)) for k, v in inp.items()}

    def cols(v, n=P):
        return np.ascontiguousarray(v.reshape(-1, n).T)

    f_order = np.arange(F).reshape(J, F // J).T.reshape(-1)
    pack = {}
    pack["wk0"], pack["wv0"], pack["wq0"] = (g[f"L0_xattn_W{c}"].T for c in "kvq")
    pack["ident"] = np.eye(P, dtype=np.float32)
    pack["bk0"], pack["bq0"] = cols(g["L0_xattn_bk"]), cols(g["L0_xattn_bq"])
    pack["gb1"] = cols(g["L0_ffn_gate_b1"])
    pack["gb2"] = np.repeat(g["L0_ffn_gate_b2"], J)[:, None]
    pack["b1"] = cols(g["L0_ffn_b1"][f_order])
    pack["bq1"], pack["bk1"] = cols(g["L1_xattn_wq_b"]), cols(g["L1_xattn_wk_b"])
    pack["convw"] = g["L1_ffn_conv_w"][:, 0, :].T
    pack["wo0"] = g["L0_xattn_Wo"].T
    pick = np.zeros((P, 2, 32), np.float32)
    for j in range(4):
        for d in range(DK0):
            pick[32 * j + d, 0, DK0 * j + d] = 1
            pick[32 * j + DK0, 1, DK0 * j + d] = 1
    pack["pick"] = pick.reshape(P, -1)
    pack["gw1"] = g["L0_ffn_gate_w1"].T
    pack["gw2"] = np.repeat(g["L0_ffn_gate_w2"].T, J, axis=1)
    pack["delta"] = np.tile(np.eye(J, dtype=np.float32), (E, 1))
    pack["w1"] = g["L0_ffn_W1"].T[:, f_order]
    pack["w2"] = g["L0_ffn_W2"].T[f_order].reshape(FC, P, D).transpose(1, 0, 2).reshape(P, FC * D)
    tb1, tb2 = np.zeros((P, F), np.float32), np.zeros((P, D), np.float32)
    tb1[::J], tb2[::J] = g["L0_ffn_Tb1"][:, f_order], g["L0_ffn_Tb2"]
    pack["tb1"], pack["tb2"] = tb1, tb2
    wg, wu = (g[f"L1_ffn_W{c}"].transpose(1, 0, 2).reshape(D, EM * EI) for c in "gu")
    pack["wgu"] = np.concatenate([wg, wu], 1)
    pack["wd"] = g["L1_ffn_Wd"].reshape(2, P, D).transpose(1, 0, 2).reshape(P, 2 * D)
    pack["wr"] = g["L1_ffn_Wr"]
    pack["before"] = np.tile(np.tril(np.ones((E, E), np.float32), -1).reshape(1, -1), (P, 1))
    packed = {}
    for name in ("early", "late"):
        packed[name] = np.concatenate([pack[k] for k, v in PACK.items() if v[0] == name], 1)
    rows = {"bv0": g["L0_xattn_bv"], "bo0": g["L0_xattn_bo"], "b2": g["L0_ffn_b2"], "bo1": g["L1_xattn_wo_b"],
            "convb": g["L1_ffn_conv_b"], "rb": g["L1_ffn_router_bias"], "bv1": g["L1_xattn_wv_b"]}
    tw2 = g["L0_ffn_TW2"][:, :, f_order].reshape(P, 8 * F)
    return {
        "x": g["x"].reshape(T, D),
        "ctx_t": g["ctx_1024"].reshape(T, D).T,
        "early": packed["early"], "late": packed["late"],
        "rows": np.concatenate([rows[k] for k in ROWS])[None, :],
        "tw1": g["L0_ffn_TW1"].reshape(P, 32 * D),
        "tw2": tw2,
        "wq1": g["L1_xattn_wq_w"], "wk1": g["L1_xattn_wk_w"], "wv1": g["L1_xattn_wv_w"],
        "wo1": g["L1_xattn_wo_w"].reshape(H // 2, P, D).transpose(1, 0, 2).reshape(P, -1),
        "mem_k": g["L1_xattn_mk"][0].reshape(MEM, H, DK1).transpose(2, 1, 0),
        "mem_v": g["L1_xattn_mv"][0],
    }


def kernel(**inputs):
    import concourse.bacc as _bacc
    from concourse.bass_utils import run_bass_kernel_spmd as _run

    nc = _bacc.Bacc("TRN2", target_bir_lowering=False, num_devices=1)
    arrays, args = {}, []
    for name, a in _layout(inputs).items():
        a = np.ascontiguousarray(a)
        arrays[f"in_{name}"] = a
        args.append(nc.dram_tensor(f"in_{name}", a.shape, F32, kind="ExternalInput").ap())
    args.append(nc.dram_tensor("out_x", (T, D), F32, kind="ExternalOutput").ap())
    xattn_ffn_kernel(nc, *args)
    r = _run(nc, [arrays], core_ids=[0])
    return r.results[0]["out_x"].reshape(B, S, D)
```
